# Optimizing a Trainium2 kernel written in Bass

```python
import numpy as np
import jax
import jax.numpy as jnp

def _softmax(x, axis=-1):
    return jax.nn.softmax(x, axis=axis)

def _gelu(x):
    return jax.nn.gelu(x, approximate=True)

def _silu(x):
    return jax.nn.silu(x)

def _sigmoid(x):
    return jax.nn.sigmoid(x)

def _layernorm(x, axis=-1, eps=1e-05):
    m = jnp.mean(x, axis=axis, keepdims=True)
    v = jnp.var(x, axis=axis, keepdims=True)
    return (x - m) / jnp.sqrt(v + eps)

def _scatter_add(tgt, idx, src, axis=0):
    return tgt.at[idx].add(src)

def _segment_sum(src, seg, n):
    return jax.ops.segment_sum(src, seg, n)
kernel_name = 'mk_seq_preln_d1_jaxref_r8_133a71'

def setup_inputs(seed: int=0):
    np.random.seed(seed)
    _w = jnp.asarray

    def _L0_attn_setup():
        import jax, jax.numpy as jnp
        import numpy as np
        from jax import lax
        D_MODEL = 128
        D_STATE = 16
        D_CONV = 4
        EXPAND = 2
        D_INNER = D_MODEL * EXPAND
        DT_RANK = 64
        BATCH = 2
        SEQ = 512
        DT_MIN, DT_MAX = (0.001, 0.1)
        key = jax.random.key(seed)
        ks = jax.random.split(key, 12)
        xavier = lambda k, shape: jax.random.normal(k, shape, jnp.float32) * np.float32(np.sqrt(2.0 / (shape[0] + shape[1])))
        x = jax.random.normal(ks[0], (BATCH, SEQ, D_MODEL), jnp.float32)
        in_proj_w = xavier(ks[1], (2 * D_INNER, D_MODEL))
        in_proj_b = jnp.zeros((2 * D_INNER,), jnp.float32)
        conv_w = jax.random.normal(ks[2], (D_INNER, D_CONV), jnp.float32) * 0.02
        conv_b = jnp.zeros((D_INNER,), jnp.float32)
        A_log = jnp.log(jnp.tile(jnp.arange(1, D_STATE + 1, dtype=jnp.float32)[:, None], (1, D_INNER)))
        D = jnp.ones((D_INNER,), jnp.float32)
        x_proj_w = xavier(ks[3], (DT_RANK + 2 * D_STATE, D_INNER))
        dt_proj_w = jax.random.normal(ks[4], (D_INNER, DT_RANK), jnp.float32) * np.float32(DT_RANK ** (-0.5))
        dt = jnp.exp(jax.random.uniform(ks[5], (D_INNER,), jnp.float32) * np.float32(np.log(DT_MAX) - np.log(DT_MIN)) + np.float32(np.log(DT_MIN)))
        dt_proj_b = dt + jnp.log(-jnp.expm1(-dt))
        out_proj_w = xavier(ks[6], (D_MODEL, D_INNER))
        out_proj_b = jnp.zeros((D_MODEL,), jnp.float32)
        return {'x': x, 'in_proj_w': in_proj_w, 'in_proj_b': in_proj_b, 'conv_w': conv_w, 'conv_b': conv_b, 'A_log': A_log, 'D': D, 'x_proj_w': x_proj_w, 'dt_proj_w': dt_proj_w, 'dt_proj_b': dt_proj_b, 'out_proj_w': out_proj_w, 'out_proj_b': out_proj_b}
    _L0_attn_in = _L0_attn_setup()

    def _L0_ffn_setup():
        import jax, jax.numpy as jnp
        import numpy as np
        B, S, D, F, E = (4, 256, 128, 512, 8)
        key = jax.random.key(seed)
        ks = jax.random.split(key, 7)
        s1 = 1.0 / np.sqrt(D)
        s2 = 1.0 / np.sqrt(F)
        x = jax.random.normal(ks[0], (B, S, D), dtype=jnp.float32)
        W1 = jax.random.uniform(ks[1], (E, D, F), jnp.float32, -s1, s1)
        b1 = jax.random.uniform(ks[2], (E, F), jnp.float32, -s1, s1)
        W2 = jax.random.uniform(ks[3], (E, F, D), jnp.float32, -s2, s2)
        b2 = jax.random.uniform(ks[4], (E, D), jnp.float32, -s2, s2)
        Wr = jax.random.uniform(ks[5], (D, E), jnp.float32, -s1, s1)
        br = jax.random.uniform(ks[6], (E,), jnp.float32, -s1, s1)
        return {'x': x, 'W1': W1, 'b1': b1, 'W2': W2, 'b2': b2, 'Wr': Wr, 'br': br}
    _L0_ffn_in = _L0_ffn_setup()
    _d = {'L0_attn_x': _L0_attn_in['x'], 'L0_attn_in_proj_w': _L0_attn_in['in_proj_w'], 'L0_attn_in_proj_b': _L0_attn_in['in_proj_b'], 'L0_attn_conv_w': _L0_attn_in['conv_w'], 'L0_attn_conv_b': _L0_attn_in['conv_b'], 'L0_attn_A_log': _L0_attn_in['A_log'], 'L0_attn_D': _L0_attn_in['D'], 'L0_attn_x_proj_w': _L0_attn_in['x_proj_w'], 'L0_attn_dt_proj_w': _L0_attn_in['dt_proj_w'], 'L0_attn_dt_proj_b': _L0_attn_in['dt_proj_b'], 'L0_attn_out_proj_w': _L0_attn_in['out_proj_w'], 'L0_attn_out_proj_b': _L0_attn_in['out_proj_b'], 'L0_ffn_W1': _L0_ffn_in['W1'], 'L0_ffn_b1': _L0_ffn_in['b1'], 'L0_ffn_W2': _L0_ffn_in['W2'], 'L0_ffn_b2': _L0_ffn_in['b2'], 'L0_ffn_Wr': _L0_ffn_in['Wr'], 'L0_ffn_br': _L0_ffn_in['br']}
    _x0 = _d['L0_attn_x']
    _d['L0_attn_x'] = jax.random.normal(jax.random.fold_in(jax.random.key(seed), 1), (8, 512, 128), dtype=_x0.dtype)
    del _x0
    return _d

def reference(L0_attn_x, L0_attn_in_proj_w, L0_attn_in_proj_b, L0_attn_conv_w, L0_attn_conv_b, L0_attn_A_log, L0_attn_D, L0_attn_x_proj_w, L0_attn_dt_proj_w, L0_attn_dt_proj_b, L0_attn_out_proj_w, L0_attn_out_proj_b, L0_ffn_W1, L0_ffn_b1, L0_ffn_W2, L0_ffn_b2, L0_ffn_Wr, L0_ffn_br):

    def _L0_attn_ref(x, in_proj_w, in_proj_b, conv_w, conv_b, A_log, D, x_proj_w, dt_proj_w, dt_proj_b, out_proj_w, out_proj_b):
        import jax, jax.numpy as jnp
        import numpy as np
        from jax import lax
        D_MODEL = 128
        D_STATE = 16
        D_CONV = 4
        EXPAND = 2
        D_INNER = D_MODEL * EXPAND
        DT_RANK = 64
        BATCH = 2
        SEQ = 512
        DT_MIN, DT_MAX = (0.001, 0.1)
        b, L, _ = x.shape
        xz = x @ in_proj_w.T + in_proj_b
        x_in, z = jnp.split(xz, 2, axis=-1)
        x_pad = jnp.pad(x_in, ((0, 0), (D_CONV - 1, 0), (0, 0)))
        x_conv = conv_b
        x_conv = sum((x_pad[:, k:k + L, :] * conv_w[None, None, :, k] for k in range(D_CONV))) + conv_b
        x_conv = jax.nn.silu(x_conv)
        x_dbl = x_conv @ x_proj_w.T
        dt_low = x_dbl[..., :DT_RANK]
        Bm = x_dbl[..., DT_RANK:DT_RANK + D_STATE]
        Cm = x_dbl[..., DT_RANK + D_STATE:]
        dt = jax.nn.softplus(dt_low @ dt_proj_w.T + dt_proj_b)
        A = -jnp.exp(A_log).T
        safe_A = jnp.where(jnp.abs(A) < 1e-06, jnp.ones_like(A), A)

        def step(h, inp):
            xt, dtt, Bt, Ct = inp
            A_bar = jnp.exp(dtt[..., None] * A)
            B_bar = (A_bar - 1.0) / safe_A * Bt[:, None, :]
            h = A_bar * h + B_bar * xt[..., None]
            y = jnp.einsum('bds,bs->bd', h, Ct) + D * xt
            return (h, y)
        xs = (jnp.swapaxes(x_conv, 0, 1), jnp.swapaxes(dt, 0, 1), jnp.swapaxes(Bm, 0, 1), jnp.swapaxes(Cm, 0, 1))
        h0 = jnp.zeros((b, D_INNER, D_STATE), x.dtype)
        _, ys = lax.scan(step, h0, xs)
        y = jnp.swapaxes(ys, 0, 1) * jax.nn.silu(z)
        return y @ out_proj_w.T + out_proj_b

    def _L0_ffn_ref(x, W1, b1, W2, b2, Wr, br):
        import jax, jax.numpy as jnp
        import numpy as np
        B, S, D, F, E = (4, 256, 128, 512, 8)
        b, s, d = x.shape
        e = Wr.shape[1]
        logits = x @ Wr + br
        idx = jnp.argmax(logits, axis=-1)
        probs = jax.nn.softmax(logits, axis=-1)
        gates = jnp.take_along_axis(probs, idx[..., None], axis=-1)[..., 0]
        xf = x.reshape(-1, d)
        idxf = idx.reshape(-1)
        gf = gates.reshape(-1)
        out = jnp.zeros_like(xf)
        for ei in range(e):
            h = jax.nn.gelu(xf @ W1[ei] + b1[ei], approximate=False)
            y = h @ W2[ei] + b2[ei]
            mask = (idxf == ei).astype(xf.dtype)
            out = out + y * (gf * mask)[:, None]
        return out.reshape(b, s, d)
    x = L0_attn_x
    x = x + _L0_attn_ref(_layernorm(x, axis=-1), L0_attn_in_proj_w, L0_attn_in_proj_b, L0_attn_conv_w, L0_attn_conv_b, L0_attn_A_log, L0_attn_D, L0_attn_x_proj_w, L0_attn_dt_proj_w, L0_attn_dt_proj_b, L0_attn_out_proj_w, L0_attn_out_proj_b)
    x = x + _L0_ffn_ref(_layernorm(x, axis=-1), L0_ffn_W1, L0_ffn_b1, L0_ffn_W2, L0_ffn_b2, L0_ffn_Wr, L0_ffn_br)
    return x

_drawn_inputs = setup_inputs


def setup_inputs(seed=0):
    import zlib

    import numpy as np

    out = dict(_drawn_inputs(seed))
    spreads = {'L0_attn_in_proj_b': (0.0, 0.8),
     'L0_attn_conv_b': (0.0, 0.328),
     'L0_attn_D': (1.0, 0.6),
     'L0_attn_out_proj_b': (0.0, 0.1)}
    factors = {'L0_attn_conv_w': 8.0,
     'L0_attn_A_log': 8.0,
     'L0_attn_x_proj_w': 8.0,
     'L0_attn_dt_proj_w': 8.0,
     'L0_attn_dt_proj_b': 8.0,
     'L0_ffn_b1': 8.0,
     'L0_ffn_b2': 8.0,
     'L0_ffn_br': 3.931}
    for name, (base, spread) in spreads.items():
        noise = np.random.default_rng([zlib.crc32(name.encode()), seed]).standard_normal(out[name].shape)
        drawn = base * np.exp(spread * noise) if base else spread * noise
        out[name] = jnp.asarray(drawn.astype(out[name].dtype))
    for name, factor in factors.items():
        out[name] = (out[name] * factor).astype(out[name].dtype)
    return out
```

```python
import numpy as np
import concourse.bass as bass
import concourse.mybir as mybir
from contextlib import ExitStack

P = 128
NB, L, DM = 8, 512, 128
TILES = L // P
H, S, R = 2, 16, 64
DI = H * P
TAPS = 4
E, FF = 8, 512
FK = FF // P
TOK = NB * L
REGION = TOK + P
FTILES = TOK // P + E
ROWS = E * REGION + (FTILES - TOK // P) * P
RW = 2 * DM + 2
NO_TOKEN = TOK
BW = P + 1
EW = FF + FK * DM + FK + DM
EPS = 1e-5

QUAD_A = (1.0093575430011281, -0.08225440736378242, -1.424741164592344, -2.3216937658543895)
QUAD_B = (1.106067408717108, 3.2574833956522826, 2.702115883781287, 0.43240884150072795)
LEAD = 0.0052325939439559314

PACK = [("ident", P), ("bidiag", BW), ("before", P), ("ones", P), ("expert_no", E), ("expert_no8", E),
        ("region_at", E), ("token", TILES), ("quad_a", 4), ("minus_half", TILES), ("eps", TILES), ("tile_at", TOK // P),
        ("tile_no", FTILES),
        ("w_in", 2 * DI), ("b_in", 2 * H), ("conv_w", H * TAPS), ("conv_b", H), ("a_log", H * S),
        ("d_skip", H), ("x_proj", H * (R + 2 * S)), ("dt_w", DI), ("dt_b", H), ("a_log_s", DI),
        ("out_w", H * DM), ("out_b", DM), ("w_r", E), ("b_r", E)]
AT, PACK_W = {}, 0
for _name, _width in PACK:
    AT[_name] = (PACK_W, PACK_W + _width)
    PACK_W += _width

POOL_STATES = (2, 6, 10, 14)
VEC_STATES = tuple(s for s in range(S) if s not in POOL_STATES)
NV, NP_ = len(VEC_STATES), len(POOL_STATES)


def vec_before(s):
    return sum(1 for q in VEC_STATES if q < s)


def pool_before(s):
    return sum(1 for q in POOL_STATES if q < s)


def early(n, m=1):
    return isinstance(n, int) and n < m


FU = 8


LOADS_AHEAD = 4


def after(k, c):
    return (k, c + 1) if c + 1 < FU else (k + 1, 0)


def ahead(k, c):
    return (k, c - 1) if c else (k - 1, FU - 1)


def starts(k, c, n):
    return isinstance(k, int) and FU * k + c < n


def ends(k, c):
    return isinstance(k, int) and FU * k + c == FTILES - 1


def program(nc, x_d, pack_d, experts_d, out_d, c_scratch, rows_d):
    F32, I32 = mybir.dt.float32, mybir.dt.int32
    ALU, ACT, AX = mybir.AluOpType, mybir.ActivationFunctionType, mybir.AxisListType
    ctx = ExitStack()
    with ctx:
        def sb(name, shape, dt=F32):
            return ctx.enter_context(nc.sbuf_tensor(name, shape, dt))

        def sem(name):
            return ctx.enter_context(nc.semaphore(name))

        pack = sb("pack", [P, PACK_W])

        def const(name):
            return pack[:, AT[name][0]:AT[name][1]]

        ident, bidiag, before, ones = const("ident"), const("bidiag"), const("before"), const("ones")
        w_in, b_in = const("w_in"), const("b_in")
        conv_w = const("conv_w").rearrange("p (h k) -> p h k", h=H)
        conv_b, d_skip, dt_b = const("conv_b"), const("d_skip"), const("dt_b")
        x_proj = const("x_proj").rearrange("p (h r) -> p h r", h=H)
        out_w = const("out_w").rearrange("p (h r) -> p h r", h=H)
        dt_w = pack[0:R, AT["dt_w"][0]:AT["dt_w"][1]]
        a_log_s = pack[0:S, AT["a_log_s"][0]:AT["a_log_s"][1]]

        half_bin = sb("half_bin", [P, 2 * H])
        neg_d = sb("neg_d", [P, H])
        neg_a = sb("neg_a", [P, H * S])
        inv_a = sb("inv_a", [P, H * S])
        tiny_a = sb("tiny_a", [P, H * S])
        tiny_s = sb("tiny_s", [S, DI])
        inv_a_s = sb("inv_a_s", [S, DI])
        diag = sb("diag", [P, H, S, P])

        
        x_in = [sb(f"x_in{i}", [P, TILES, DM]) for i in range(2)]
        stat1, mv1 = sb("stat1", [P, TILES, 6]), sb("mv1", [P, TILES, 2])
        var1, rstd1 = sb("var1", [P, TILES]), sb("rstd1", [P, TILES])
        xn, xnT = sb("xn", [P, TILES, DM]), sb("xnT", [P, L])
        xpad = sb("xpad", [P, H, TAPS - 1 + L])
        tanh_z = sb("tanh_z", [P, H, L])
        tanh_u = sb("tanh_u", [P, H, L])
        conv = sb("conv", [P, H, L])
        z_half = sb("z_half", [P, H, L])
        abs_p, y_exp, relu_p, poly = tanh_z, tanh_u, conv, z_half
        square = [sb(f"square{i}", [P, H, L]) for i in range(2)]
        gate_z = [sb(f"gate_z{i}", [P, H, L]) for i in range(2)]
        xc = sb("xc", [P, H, L])
        xcT = [sb(f"xcT{i}", [P, TILES, DI]) for i in range(2)]
        x_dbl = sb("x_dbl", [R + 2 * S, L])
        bc_T, bc_mul = sb("bc_T", [P, TILES, 2 * S]), sb("bc_mul", [P, TILES, S])
        bc_s = sb("bc_s", [S, L])
        skip = [sb(f"skip{i}", [P, H, L]) for i in range(2)]
        dt = [sb(f"dt{i}", [P, H, L]) for i in range(2)]

        big = sb("big", [P, S * TILES * BW + S * L])
        delta = big[:, 0:S * TILES * BW].rearrange("p (s j c) -> p s j c", s=S, j=TILES)
        c_all = big[:, S * TILES * BW:].rearrange("p (s t) -> p s t", s=S)
        w_all = big[:, 0:E * EW].rearrange("p (e c) -> p e c", e=E)
        a_bar = [sb(f"a_bar{i}", [P, L]) for i in range(4)]
        steps = sb("steps", [P, 4 * H * L])

        def step_slot(i):
            return steps[:, i * H * L:(i + 1) * H * L].rearrange("p (h t) -> p h t", h=H)

        k_st, prod = [step_slot(i) for i in range(2)], [step_slot(2 + i) for i in range(2)]

        y = sb("y", [P, H, L])
        x_res = sb("x_res", [P, TILES, DM])
        row = sb("row", [P, TILES, RW])
        stat2, mv2 = sb("stat2", [P, TILES, 6]), sb("mv2", [P, TILES, 2])
        var2, rstd2 = sb("var2", [P, TILES]), sb("rstd2", [P, TILES])
        xn2T = sb("xn2T", [P, L])
        logit, shifted, expd = (sb(n, [P, TILES, E]) for n in ("logit", "shifted", "expd"))
        top, chosen, zsum = (sb(n, [P, TILES]) for n in ("top", "chosen", "zsum"))
        is_top, cand, one_hot = (sb(n, [P, TILES, E]) for n in ("is_top", "cand", "one_hot"))
        slot_e, slot_m, slot = sb("slot_e", [P, TILES, E]), sb("slot_m", [P, TILES, E]), sb("slot", [P, TILES])
        slot_i = sb("slot_i", [P, TILES], I32)
        filled = sb("filled", [P, E])
        token = sb("token", [P, TILES])

        plan_w = [0]

        def plan(width, dt=F32):
            at = plan_w[0]
            plan_w[0] += width
            v = square[0][0:1, :, :].rearrange("p h t -> p (h t)")[:, at:at + width]
            return v if dt == F32 else v.bitcast(dt)

        count, n_tiles, end_tile, filled_i = plan(E), plan(E), plan(E), plan(E, I32)
        full = plan(E * (TOK // P)).rearrange("p (e j) -> p e j", e=E)
        passed = plan(FTILES * E).rearrange("p (i e) -> p i e", e=E)
        t_exp, t_off, t_row = plan(FTILES), plan(FTILES), plan(FTILES)
        t_exp_i, t_row_i = plan(FTILES, I32), plan(FTILES, I32)
        passed_n = square[1][0:1, 0, 0:FTILES * E].rearrange("p (i e) -> p i e", e=E)
        zero8 = sb("zero8", [1, E])
        pad = sb("pad", [P, RW])
        f_row = [v[:, :, :].rearrange("p j d -> p (j d)")[:, i * RW:(i + 1) * RW]
                 for v in (xcT[0], xcT[1], skip[0], skip[1]) for i in range(2)]
        f_xT = [xnT[:, i * P:(i + 1) * P] for i in range(2)]
        f_w = [steps[:, 0:EW], steps[:, 2 * H * L:2 * H * L + EW]]
        f_h = [tanh_z[:, 0, :], tanh_u[:, 0, :]]
        f_out = [v[:, c, :] for v in (xn, x_res) for c in range(TILES)]

        bank = [ctx.enter_context(nc.psum_tensor(f"bank{i}", [P, L], F32)) for i in range(4)]
        dv = [ctx.enter_context(nc.psum_tensor(f"dv{i}", [P, L], F32)) for i in range(2)]
        ysum = ctx.enter_context(nc.psum_tensor("ysum", [P, H, L], F32))

        wait_carrier = sem("wait_carrier")
        s_pack, s_pad_ready = sem("pack_loaded"), sem("pad_ready")
        x_loaded, res_loaded = sem("x_loaded"), sem("res_loaded")
        c_stored = sem("c_stored")
        c_loaded = [sem(f"c_loaded{g}") for g in range(4)]
        setup_a, setup = sem("setup_a"), sem("setup")
        stats1, mv1_ready, var1_ready, rstd1_ready = sem("stats1"), sem("mv1_ready"), sem("var1_ready"), sem("rstd1_ready")
        xn_ready, xn_turned, xnT_ready = sem("xn_ready"), sem("xn_turned"), sem("xnT_ready")
        in_done, in_read = sem("in_done"), sem("in_read")
        conv_step, tanhz_ready, tanhu_ready = sem("conv_step"), sem("tanhz_ready"), sem("tanhu_ready")
        gate_ready, xc_ready = sem("gate_ready"), sem("xc_ready")
        xdbl_done, xdbl_ready = sem("xdbl_done"), sem("xdbl_ready")
        xc_turned, xcT_ready = sem("xc_turned"), sem("xcT_ready")
        xdbl_turned, bcT_ready, bcmul_ready = sem("xdbl_turned"), sem("bcT_ready"), sem("bcmul_ready")
        bc_turned, bcs_ready, q_done, skip_ready = sem("bc_turned"), sem("bcs_ready"), sem("q_done"), sem("skip_ready")
        dt_done, dt_read, yexp_ready, square_ready, poly_step = (
            sem("dt_done"), sem("dt_read"), sem("yexp_ready"), sem("square_ready"), sem("poly_step"))
        delta_ready, dv_ready, abar_ready, scanned = sem("delta_ready"), sem("dv_ready"), sem("abar_ready"), sem("scanned")
        prod_vec, prod_pool, summed = sem("prod_vec"), sem("prod_pool"), sem("summed")
        y_ready, yg_ready, out_done, res_ready = sem("y_ready"), sem("yg_ready"), sem("out_done"), sem("res_ready")
        x1_ready, stats2, mv2_ready, var2_ready, rstd2_ready = (
            sem("x1_ready"), sem("stats2"), sem("mv2_ready"), sem("var2_ready"), sem("rstd2_ready"))
        xn2_ready, xn2_turned, xn2T_ready, logit_done = sem("xn2_ready"), sem("xn2_turned"), sem("xn2T_ready"), sem("logit_done")
        route, expd_ready, rank_done, placed, scattered = (
            sem("route"), sem("expd_ready"), sem("rank_done"), sem("placed"), sem("scattered"))

        pad_zero, padded, planned, w_loaded, rows_filled = sem("pad_zero"), sem("padded"), sem("planned"), sem("w_loaded"), sem("rows_filled")
        f_loaded = [sem(f"f_loaded{c}") for c in range(FU)]
        f_stored = [sem(f"f_stored{c}") for c in range(FU)]
        f_turned, f_xT_ready, w1_taken, w2_taken = sem("f_turned"), sem("f_xT_ready"), sem("w1_taken"), sem("w2_taken")
        hidden_done, gelu_done, mlp_done, combined = sem("hidden_done"), sem("gelu_done"), sem("mlp_done"), sem("combined")

        block = ctx.enter_context(nc.Block())


        @block.sync
        def _(sp):
            def load_x(n, p):
                if not early(n):
                    sp.wait_ge(x_loaded, 16 * n)
                    sp.sem_inc(wait_carrier)
                if not early(n, 2):
                    sp.wait_ge(xn_ready, n - 1)
                sp.dma_start(x_in[p][:, :, :], x_d[n].rearrange("(j q) d -> q j d", q=P)).then_inc(x_loaded, 16)

            def load_residual(t):
                if not early(t):
                    sp.wait_ge(scanned, 32 * t + 32)
                sp.dma_start(x_res[:, :, :], x_d[t].rearrange("(j q) d -> q j d", q=P)).then_inc(res_loaded, 16)

            def store_c(n, p):
                sp.wait_ge(xdbl_ready, n + 1)
                sp.dma_start(c_scratch[p], x_dbl[R + S:R + 2 * S, :]).then_inc(c_stored, 16)

            def load_c(n, p, g):
                sp.wait_ge(c_stored, 16 * (n + 1))
                if not early(n):
                    sp.sem_inc(wait_carrier)
                    sp.wait_ge(prod_vec, NV * (n - 1) + vec_before(4 * g + 4))
                    sp.sem_inc(wait_carrier)
                    sp.wait_ge(prod_pool, NP_ * (n - 1) + pool_before(4 * g + 4))
                src = bass.AP(c_scratch.tensor, (p * S + 4 * g) * L, [[0, P], [1, 4 * L]])
                sp.dma_start(c_all[:, 4 * g:4 * g + 4, :].rearrange("p s t -> p (s t)"), src).then_inc(c_loaded[g], 16)

            def body(b, p, first=False, last=False):
                if not last:
                    load_x(b + 1, 1 - p)
                load_c(b, p, 3)
                if not first:
                    load_residual(b - 1)
                if not last:
                    store_c(b + 1, 1 - p)
                    for g in range(3):
                        load_c(b + 1, 1 - p, g)

            sp.dma_start(pack[:, :], pack_d).then_inc(s_pack, 16)
            load_x(0, 0)
            store_c(0, 0)
            for g in range(3):
                load_c(0, 0, g)
            body(0, 0, first=True)
            with sp.Fori(0, (NB - 2) // 2) as i:
                body(2 * i + 1, 1)
                body(2 * i + 2, 0)
            body(NB - 1, 1, last=True)
            load_residual(NB - 1)
            sp.wait_ge(dv_ready, 32 * NB)
            sp.wait_ge(prod_vec, NV * NB)
            sp.wait_ge(prod_pool, NP_ * NB)
            for e in range(E):
                sp.dma_start(w_all[:, e, :], experts_d[e]).then_inc(w_loaded, 16)
            sp.wait_ge(w_loaded, 16 * E)

        @block.tensor
        def _(pe):
            def turn_xn(n):
                pe.wait_ge(xn_ready, n + 1)
                if not early(n):
                    pe.wait_ge(skip_ready, 2 * n - 1)
                for j in range(TILES):
                    last = nc.tensor.transpose(bank[0][:, j * P:(j + 1) * P], xn[:, j, :], ident)
                last.then_inc(xn_turned, 1)

            def in_proj(n, m):
                if m == 0:
                    pe.wait_ge(xnT_ready, n + 1)
                    if not early(n):
                        pe.wait_ge(bcs_ready, n)
                if m == 1 and not early(n):
                    pe.wait_ge(skip_ready, 2 * n)
                nc.tensor.matmul(bank[(m + 1) % 4][:, :], w_in[:, m * P:(m + 1) * P], xnT[:, :],
                                 start=True, stop=True).then_inc(in_done, 1)

            def x_projection(n, t):
                pe.wait_ge(xc_ready, n + 1)
                if t is not None:
                    pe.wait_ge(x1_ready, t + 1)
                for h in range(H):
                    last = nc.tensor.matmul(bank[1][0:R + 2 * S, :], x_proj[:, h, :], xc[:, h, :],
                                            start=(h == 0), stop=(h == H - 1))
                last.then_inc(xdbl_done, 1)

            def turn_xc(n, t, part):
                if part == 0:
                    pe.wait_ge(in_read, 4 * n + 4)
                elif t is not None:
                    pe.wait_ge(xn2T_ready, t + 1)
                to = bank[2 * part]
                for j in range(2):
                    for h in range(H):
                        at = j * DI + h * P
                        j0 = (2 * part + j) * P
                        last = nc.tensor.transpose(to[:, at:at + P], xc[:, h, j0:j0 + P], ident)
                last.then_inc(xc_turned, 1)

            def turn_xdbl(n):
                pe.wait_ge(xdbl_ready, n + 1)
                for j in range(TILES):
                    last = nc.tensor.transpose(bank[1][:, j * 96:(j + 1) * 96], x_dbl[:, j * P:(j + 1) * P],
                                               ident[0:96, 0:96])
                last.then_inc(xdbl_turned, 1)

            def dt_proj(n, h):
                pe.wait_ge(xcT_ready, 2 * n + h + 1)
                nc.tensor.matmul(bank[2 * h][:, :], dt_w[:, h * P:(h + 1) * P], x_dbl[0:R, :],
                                 start=True, stop=True).then_inc(dt_done, 1)

            def turn_bc(n):
                pe.wait_ge(bcmul_ready, n + 1)
                for j in range(TILES):
                    last = nc.tensor.transpose(bank[1][0:S, j * P:(j + 1) * P], bc_mul[:, j, :], ident)
                last.then_inc(bc_turned, 1)

            def q_matmul(n, h):
                pe.wait_ge(bcs_ready, n + 1)
                pe.wait_ge(dt_read, 2 * n + h + 1)
                nc.tensor.matmul(bank[2 * h][:, :], inv_a_s[:, h * P:(h + 1) * P], bc_s[:, :],
                                 start=True, stop=True).then_inc(q_done, 1)

            def out_proj(t, n):
                pe.wait_ge(yg_ready, t + 1)
                if n is not None:
                    pe.wait_ge(in_read, 4 * n + 1)
                else:
                    pe.wait_ge(bcs_ready, NB)
                    pe.wait_ge(x1_ready, t)
                for j in range(TILES):
                    for h in range(H):
                        last = nc.tensor.matmul(bank[1][:, j * P:(j + 1) * P], y[:, h, j * P:(j + 1) * P],
                                                out_w[:, h, :], start=(h == 0), stop=(h == H - 1))
                last.then_inc(out_done, 1)

            def turn_xn2(t, n):
                pe.wait_ge(xn2_ready, t + 1)
                if n is not None:
                    pe.wait_ge(in_read, 4 * n + 2)
                else:
                    pe.wait_ge(skip_ready, 2 * NB)
                    pe.wait_ge(xn2T_ready, t)
                for j in range(TILES):
                    last = nc.tensor.transpose(bank[2][:, j * P:(j + 1) * P], row[:, j, 0:DM], ident)
                last.then_inc(xn2_turned, 1)

            def router(t, n):
                pe.wait_ge(xn2T_ready, t + 1)
                if n is not None:
                    pe.wait_ge(in_read, 4 * n + 3)
                else:
                    pe.wait_ge(placed, 9 * t)
                for j in range(TILES):
                    last = nc.tensor.matmul(bank[3][:, j * E:(j + 1) * E], xn2T[:, j * P:(j + 1) * P],
                                            const("w_r"), start=True, stop=True)
                last.then_inc(logit_done, 1)

            def ranks(t):
                pe.wait_ge(route, 7 * t + 6)
                hot = one_hot[:, :, :].rearrange("p j e -> p (j e)")
                nc.tensor.matmul(bank[3][:, 64:64 + TILES * E], before, hot, start=True, stop=False,
                                 skip_group_check=True)
                for j in range(TILES - 1):
                    for to in range(j + 1, TILES):
                        at = 64 + to * E
                        nc.tensor.matmul(bank[3][:, at:at + E], ones, one_hot[:, j, :], start=False,
                                         stop=(to == j + 1), skip_group_check=True)
                for j in range(TILES):
                    last = nc.tensor.matmul(bank[3][:, 128:128 + E], ones, one_hot[:, j, :], start=(j == 0),
                                            stop=(j == TILES - 1))
                last.then_inc(rank_done, 1)

            def difference(n, p, s, h):
                k = 32 * n + 2 * s + h
                if s % 4 == 0 and h == 0:
                    pe.wait_ge(delta_ready, 4 * n + s // 4 + 1)
                if s == 0 and h == 0:
                    pe.wait_ge(xcT_ready, 2 * n + 2)
                if not (isinstance(n, int) and k < 2):
                    pe.wait_ge(scanned, k - 1)
                for j in range(TILES):
                    w = BW if j < TILES - 1 else P
                    last = nc.tensor.matmul(dv[h][:, j * P:j * P + w], xcT[p][:, j, h * P:(h + 1) * P],
                                            delta[:, s, j, 0:w], start=(j == 0), stop=(j == TILES - 1),
                                            skip_group_check=True)
                last.then_inc(dv_ready, 1)

            def sum_states(n, s):
                if s in POOL_STATES:
                    pe.wait_ge(prod_pool, NP_ * n + pool_before(s + 1))
                else:
                    pe.wait_ge(prod_vec, NV * n + vec_before(s + 1))
                if s == 0 and not early(n):
                    pe.wait_ge(y_ready, n)
                for h in range(H):
                    nc.tensor.matmul(ysum[:, h, :], diag[:, h, s, :], prod[s % 2][:, h, :],
                                     start=(s == 0), stop=(s == S - 1), skip_group_check=True).then_inc(summed, 1)

            def body(b, p, first=False, last=False):
                n = None if last else b + 1
                t = None if first else b - 1
                for s in range(S):
                    difference(b, p, s, 0)
                    difference(b, p, s, 1)
                    if s >= 2:
                        sum_states(b, s - 2)
                    elif not first:
                        sum_states(b - 1, S + s - 2)
                    if n is not None and s == 2:
                        turn_xn(n)
                    if n is not None and s == 3:
                        in_proj(n, 0)
                        in_proj(n, 1)
                    if n is not None and s == 4:
                        in_proj(n, 2)
                        in_proj(n, 3)
                    if t is not None and s == 5:
                        out_proj(t, n)
                    if n is not None and s == 7:
                        x_projection(n, t)
                    if t is not None and s == 8:
                        turn_xn2(t, n)
                    if n is not None and s == 8:
                        turn_xc(n, t, 0)
                    if t is not None and s == 9:
                        router(t, n)
                    if n is not None and s == 9:
                        turn_xdbl(n)
                        turn_xc(n, t, 1)
                    if n is not None and s == 10:
                        dt_proj(n, 0)
                        dt_proj(n, 1)
                    if n is not None and s == 11:
                        turn_bc(n)
                    if t is not None and s == 12:
                        ranks(t)
                    if n is not None and s == 13:
                        q_matmul(n, 0)
                        q_matmul(n, 1)

            pe.wait_ge(s_pack, 16)
            turn_xn(0)
            for m in range(4):
                in_proj(0, m)
            x_projection(0, None)
            turn_xc(0, None, 0)
            turn_xc(0, None, 1)
            turn_xdbl(0)
            dt_proj(0, 0)
            dt_proj(0, 1)
            turn_bc(0)
            pe.wait_ge(setup, 8)
            q_matmul(0, 0)
            q_matmul(0, 1)
            body(0, 0, first=True)
            with pe.Fori(0, (NB - 2) // 2) as i:
                body(2 * i + 1, 1)
                body(2 * i + 2, 0)
            body(NB - 1, 1, last=True)
            sum_states(NB - 1, S - 2)
            sum_states(NB - 1, S - 1)
            out_proj(NB - 1, None)
            turn_xn2(NB - 1, None)
            router(NB - 1, None)
            ranks(NB - 1)

            def turn_row(k, c):
                i = FU * k + c
                pe.wait_ge(f_loaded[c], 16 * (k + 1))
                if not starts(k, c, 2):
                    pe.wait_ge(f_xT_ready, i - 1)
                nc.tensor.transpose(bank[c % 2][:, 0:P], f_row[c][:, 0:DM], ident).then_inc(f_turned, 1)

            def hidden(k, c):
                i = FU * k + c
                pe.wait_ge(f_xT_ready, i + 1)
                pe.wait_ge(w1_taken, i + 1)
                if not starts(k, c, 2):
                    pe.wait_ge(gelu_done, i - 1)
                for f in range(FK):
                    last = nc.tensor.matmul(bank[2 + c % 2][:, f * P:(f + 1) * P], f_w[c % 2][:, f * P:(f + 1) * P],
                                            f_xT[c % 2][:, :], start=True, stop=True)
                last.then_inc(hidden_done, 1)

            def mlp_out(k, c):
                i = FU * k + c
                pe.wait_ge(gelu_done, i + 1)
                pe.wait_ge(w2_taken, i + 1)
                if not starts(k, c, 2):
                    pe.wait_ge(combined, i - 1)
                to = dv[c % 2][:, 0:DM]
                nc.tensor.matmul(to, ones[0:1, :], f_w[c % 2][0:1, EW - DM:EW], start=True, stop=False)
                for f in range(FK):
                    last = nc.tensor.matmul(to, f_h[c % 2][:, f * P:(f + 1) * P],
                                            f_w[c % 2][:, FF + f * DM:FF + (f + 1) * DM], start=False, stop=(f == FK - 1))
                last.then_inc(mlp_done, 1)

            def tiles(k):
                for c in range(FU):
                    if not ends(k, c):
                        turn_row(*after(k, c))
                    hidden(k, c)
                    if not starts(k, c, 1):
                        mlp_out(*ahead(k, c))

            turn_row(0, 0)
            tiles(0)
            with pe.Fori(1, FTILES // FU - 1) as k:
                tiles(k)
            tiles(FTILES // FU - 1)
            mlp_out(FTILES // FU - 1, FU - 1)

        @block.scalar
        def _(act):
            def copy_xnT(n):
                act.wait_ge(xn_turned, n + 1)
                if not early(n):
                    act.wait_ge(in_done, 4 * n)
                nc.scalar.activation(xnT[:, :], bank[0][:, :], ACT.Copy).then_inc(xnT_ready, 1)

            def read_in_proj(n, m):
                act.wait_ge(in_done, 4 * n + m + 1)
                if m == 0 and not early(n):
                    act.wait_ge(conv_step, 8 * n)
                if m == 2 and not early(n):
                    act.wait_ge(poly_step, 5 * n)
                frm = bank[(m + 1) % 4][:, :]
                if m < H:
                    nc.scalar.activation(xpad[:, m, TAPS - 1:], frm, ACT.Identity,
                                         bias=b_in[:, m:m + 1]).then_inc(in_read, 1)
                else:
                    nc.scalar.activation(z_half[:, m - H, :], frm, ACT.Identity, bias=half_bin[:, m:m + 1],
                                         scale=0.5).then_inc(in_read, 1)

            def tanh_of_z(n):
                act.wait_ge(in_read, 4 * n + 4)
                if not early(n):
                    act.wait_ge(yexp_ready, n)
                nc.scalar.activation(tanh_z[:, :, :], z_half[:, :, :], ACT.Tanh).then_inc(tanhz_ready, 1)

            def tanh_of_conv(n):
                act.wait_ge(conv_step, 8 * n + 8)
                nc.scalar.activation(tanh_u[:, :, :], conv[:, :, :], ACT.Tanh).then_inc(tanhu_ready, 1)

            def copy_xdbl(n):
                act.wait_ge(xdbl_done, n + 1)
                if not early(n):
                    act.wait_ge(dt_done, 2 * n)
                    act.wait_ge(c_stored, 16 * n)
                nc.scalar.activation(x_dbl[:, :], bank[1][0:R + 2 * S, :], ACT.Copy).then_inc(xdbl_ready, 1)

            def copy_xcT(n, p, part):
                act.wait_ge(xc_turned, 2 * n + part + 1)
                if part == 0 and not early(n, 2):
                    act.wait_ge(dv_ready, 32 * (n - 1))
                to = xcT[p][:, 2 * part:2 * part + 2, :].rearrange("p j d -> p (j d)")
                nc.scalar.activation(to, bank[2 * part][:, :], ACT.Copy).then_inc(xcT_ready, 1)

            def softplus_parts(n, h):
                act.wait_ge(dt_done, 2 * n + h + 1)
                if h == 0:
                    act.wait_ge(gate_ready, n + 1)
                    act.wait_ge(xc_ready, n + 1)
                nc.scalar.activation(abs_p[:, h, :], bank[2 * h][:, :], ACT.Abs, bias=dt_b[:, h:h + 1])
                nc.scalar.activation(relu_p[:, h, :], bank[2 * h][:, :], ACT.Relu,
                                     bias=dt_b[:, h:h + 1]).then_inc(dt_read, 1)

            def softplus_exp(n):
                act.wait_ge(dt_read, 2 * n + 2)
                nc.scalar.activation(y_exp[:, :, :], abs_p[:, :, :], ACT.Exp, scale=-1.0).then_inc(yexp_ready, 1)

            def softplus_square(n, i):
                if i == 0:
                    act.wait_ge(yexp_ready, n + 1)
                if not (isinstance(n, int) and n == 0 and i < 2):
                    act.wait_ge(poly_step, 5 * n + i - 1 if i >= 2 else 5 * n)
                qa = const("quad_a")[:, i:i + 1]
                nc.scalar.activation(square[i % 2][:, :, :], y_exp[:, :, :], ACT.Square,
                                     bias=qa).then_inc(square_ready, 1)

            def copy_bc(n):
                act.wait_ge(bc_turned, n + 1)
                if not early(n):
                    act.wait_ge(q_done, 2 * n)
                nc.scalar.activation(bc_s[:, :], bank[1][0:S, :], ACT.Copy).then_inc(bcs_ready, 1)

            def copy_xn2T(t):
                act.wait_ge(xn2_turned, t + 1)
                nc.scalar.activation(xn2T[:, :], bank[2][:, :], ACT.Copy).then_inc(xn2T_ready, 1)

            def exp_logits(t):
                act.wait_ge(route, 7 * t + 7)
                nc.scalar.activation(expd[:, :, :], shifted[:, :, :], ACT.Exp).then_inc(expd_ready, 1)

            def decay(n, p, s, h):
                k = 32 * n + 2 * s + h
                if s == 0 and h == 0:
                    act.wait_ge(poly_step, 5 * n + 5)
                if not (isinstance(n, int) and k < 4):
                    act.wait_ge(scanned, k - 3)
                at = h * S + s
                nc.scalar.activation(a_bar[(2 * s + h) % 4][:, :], dt[p][:, h, :], ACT.Exp,
                                     scale=neg_a[:, at:at + 1]).then_inc(abar_ready, 1)

            def body(b, p, first=False, last=False):
                n = None if last else b + 1
                t = None if first else b - 1
                for s in range(S):
                    decay(b, p, s, 0)
                    decay(b, p, s, 1)
                    if n is not None and s == 2:
                        copy_xnT(n)
                    if n is not None and s == 3:
                        read_in_proj(n, 0)
                        read_in_proj(n, 1)
                    if n is not None and s == 4:
                        read_in_proj(n, 2)
                        read_in_proj(n, 3)
                        tanh_of_z(n)
                    if n is not None and s == 6:
                        tanh_of_conv(n)
                    if n is not None and s == 7:
                        copy_xdbl(n)
                    if t is not None and s == 8:
                        copy_xn2T(t)
                    if n is not None and s == 8:
                        copy_xcT(n, 1 - p, 0)
                    if n is not None and s == 9:
                        copy_xcT(n, 1 - p, 1)
                    if n is not None and s == 10:
                        softplus_parts(n, 0)
                        softplus_parts(n, 1)
                    if n is not None and s == 11:
                        softplus_exp(n)
                        softplus_square(n, 0)
                        softplus_square(n, 1)
                        copy_bc(n)
                    if t is not None and s == 11:
                        exp_logits(t)
                    if n is not None and s == 12:
                        softplus_square(n, 2)
                    if n is not None and s == 13:
                        softplus_square(n, 3)

            act.wait_ge(s_pack, 16)
            nc.scalar.activation(neg_a[:, :], const("a_log"), ACT.Exp)
            nc.scalar.activation(inv_a_s[:, :], a_log_s, ACT.Exp).then_inc(setup_a, 1)
            copy_xnT(0)
            for m in range(2):
                read_in_proj(0, m)
            act.wait_ge(setup, 4)
            for m in range(2, 4):
                read_in_proj(0, m)
            tanh_of_z(0)
            tanh_of_conv(0)
            copy_xdbl(0)
            copy_xcT(0, 0, 0)
            copy_xcT(0, 0, 1)
            softplus_parts(0, 0)
            softplus_parts(0, 1)
            softplus_exp(0)
            softplus_square(0, 0)
            softplus_square(0, 1)
            copy_bc(0)
            softplus_square(0, 2)
            softplus_square(0, 3)
            act.wait_ge(setup, 8)
            body(0, 0, first=True)
            with act.Fori(0, (NB - 2) // 2) as i:
                body(2 * i + 1, 1)
                body(2 * i + 2, 0)
            body(NB - 1, 1, last=True)
            copy_xn2T(NB - 1)
            exp_logits(NB - 1)

            def load_rows(k, c):
                at = act.value_load(t_row_i[0:1, bass.ds(FU * k + c, 1)], min_val=0, max_val=ROWS - P)
                if not starts(k, c, FU):
                    act.wait_ge(f_stored[c], 16 * k)
                act.dma_start(f_row[c][:, :], rows_d[bass.ds(at, P), :]).then_inc(f_loaded[c], 16)

            def gelu(k, c):
                i = FU * k + c
                act.wait_ge(hidden_done, i + 1)
                act.wait_ge(w2_taken, i + 1)
                if not starts(k, c, 2):
                    act.wait_ge(mlp_done, i - 1)
                for f in range(FK):
                    at = FF + FK * DM + f
                    last = nc.scalar.activation(f_h[c % 2][:, f * P:(f + 1) * P], bank[2 + c % 2][:, f * P:(f + 1) * P],
                                                ACT.Gelu, bias=f_w[c % 2][:, at:at + 1])
                last.then_inc(gelu_done, 1)

            def tiles(k):
                for c in range(FU):
                    gelu(k, c)
                    if not (isinstance(k, int) and FU * k + c + LOADS_AHEAD >= FTILES):
                        load_rows(*((k, c + LOADS_AHEAD) if c + LOADS_AHEAD < FU else (k + 1, c + LOADS_AHEAD - FU)))

            act.wait_ge(rows_filled, 1)
            act.wait_ge(planned, 10)
            for c in range(LOADS_AHEAD):
                load_rows(0, c)
            tiles(0)
            with act.Fori(1, FTILES // FU - 1) as k:
                tiles(k)
            tiles(FTILES // FU - 1)

        @block.vector
        def _(dve):
            def statistics(n, p):
                dve.wait_ge(x_loaded, 16 * (n + 1))
                for j in range(TILES):
                    last = nc.vector.bn_stats(stat1[:, j, :], x_in[p][:, j, :])
                last.then_inc(stats1, 1)
                dve.wait_ge(stats1, n + 1)
                dve.sem_inc(wait_carrier)
                for j in range(TILES):
                    last = nc.vector.bn_aggr(mv1[:, j, :], stat1[:, j, :])
                last.then_inc(mv1_ready, 1)

            def normalise(n, p):
                dve.wait_ge(rstd1_ready, n + 1)
                if not early(n):
                    dve.wait_ge(xn_turned, n)
                for j in range(TILES):
                    last = nc.vector.tensor_scalar(xn[:, j, :], x_in[p][:, j, :], mv1[:, j, 0:1],
                                                   rstd1[:, j:j + 1], ALU.subtract, ALU.mult)
                last.then_inc(xn_ready, 1)

            def convolve(n, m):
                tap, h = m // H, m % H
                if m == 0:
                    dve.wait_ge(in_read, 4 * n + 2)
                if tap == 0:
                    nc.vector.tensor_scalar(conv[:, h, :], xpad[:, h, 0:L], conv_w[:, h, 0:1], conv_b[:, h:h + 1],
                                            ALU.mult, ALU.add).then_inc(conv_step, 1)
                else:
                    dve.wait_ge(conv_step, 8 * n + m - 1)
                    nc.vector.scalar_tensor_tensor(conv[:, h, :], xpad[:, h, tap:tap + L],
                                                   conv_w[:, h, tap:tap + 1], conv[:, h, :],
                                                   ALU.mult, ALU.add).then_inc(conv_step, 1)

            def silu_z(n, p):
                dve.wait_ge(tanhz_ready, n + 1)
                if not early(n, 2):
                    dve.wait_ge(yg_ready, n - 1)
                nc.vector.scalar_tensor_tensor(gate_z[p][:, :, :], tanh_z[:, :, :], 1.0, z_half[:, :, :],
                                               ALU.add, ALU.mult).then_inc(gate_ready, 1)

            def silu_conv(n):
                dve.wait_ge(tanhu_ready, n + 1)
                if not early(n):
                    dve.wait_ge(xc_turned, 2 * n)
                    dve.wait_ge(skip_ready, 2 * n)
                nc.vector.scalar_tensor_tensor(xc[:, :, :], tanh_u[:, :, :], 1.0, conv[:, :, :],
                                               ALU.add, ALU.mult).then_inc(xc_ready, 1)

            def copy_bcT(n):
                dve.wait_ge(xdbl_turned, n + 1)
                if not early(n):
                    dve.wait_ge(delta_ready, 4 * n)
                frm = bank[1][:, 0:TILES * 96].rearrange("p (j c) -> p j c", j=TILES)[:, :, R:]
                nc.vector.tensor_copy(bc_T[:, :, :], frm).then_inc(bcT_ready, 1)
                dve.wait_ge(bcT_ready, n + 1)
                if not early(n):
                    dve.wait_ge(bc_turned, n)
                nc.vector.tensor_tensor(bc_mul[:, :, :], bc_T[:, :, 0:S], bc_T[:, :, S:],
                                        ALU.mult).then_inc(bcmul_ready, 1)

            def skip_term(n, p, h):
                dve.wait_ge(q_done, 2 * n + h + 1)
                if not early(n, 2):
                    dve.wait_ge(y_ready, n - 1)
                nc.vector.scalar_tensor_tensor(skip[p][:, h, :], bank[2 * h][:, :], neg_d[:, h:h + 1],
                                               xc[:, h, :], ALU.add, ALU.mult).then_inc(skip_ready, 1)

            def softplus_poly(n, p, i):
                if i < 4:
                    dve.wait_ge(square_ready, 4 * n + i + 1)
                if i == 0:
                    nc.vector.scalar_tensor_tensor(poly[:, :, :], square[0][:, :, :], QUAD_B[0], y_exp[:, :, :],
                                                   ALU.add, ALU.mult).then_inc(poly_step, 1)
                elif i < 4:
                    dve.wait_ge(poly_step, 5 * n + i)
                    nc.vector.scalar_tensor_tensor(poly[:, :, :], square[i % 2][:, :, :], QUAD_B[i], poly[:, :, :],
                                                   ALU.add, ALU.mult).then_inc(poly_step, 1)
                else:
                    dve.wait_ge(poly_step, 5 * n + i)
                    if not early(n, 2):
                        dve.wait_ge(abar_ready, 32 * (n - 1))
                    nc.vector.scalar_tensor_tensor(dt[p][:, :, :], poly[:, :, :], LEAD, relu_p[:, :, :],
                                                   ALU.mult, ALU.add).then_inc(poly_step, 1)

            def scan(n, s, h):
                k = 32 * n + 2 * s + h
                dve.wait_ge(dv_ready, k + 1)
                dve.wait_ge(abar_ready, k + 1)
                if h == 0:
                    m, before_s = (n, s - 2) if s >= 2 else (n - 1, S + s - 2)
                    if not (isinstance(m, int) and m < 0):
                        if before_s in POOL_STATES:
                            dve.wait_ge(prod_pool, NP_ * m + pool_before(before_s + 1))
                        else:
                            dve.wait_ge(prod_vec, NV * m + vec_before(before_s + 1))
                nc.vector.tensor_tensor_scan(k_st[s % 2][:, h, :], dv[h][:, :], a_bar[(2 * s + h) % 4][:, :], 0.0,
                                             ALU.add, ALU.mult).then_inc(scanned, 1)

            def times_c(n, s):
                dve.wait_ge(scanned, 32 * n + 2 * s + 2)
                if s % 4 == 0:
                    dve.wait_ge(c_loaded[s // 4], 16 * (n + 1))
                if not (isinstance(n, int) and 32 * n + 2 * s < 4):
                    dve.wait_ge(summed, 32 * n + 2 * s - 2)
                nc.vector.tensor_tensor(prod[s % 2][:, :, :], k_st[s % 2][:, :, :],
                                        c_all[:, s:s + 1, :].to_broadcast([P, H, L]),
                                        ALU.mult).then_inc(prod_vec, 1)

            def finish_y(t, p):
                dve.wait_ge(summed, 32 * t + 32)
                nc.vector.tensor_tensor(y[:, :, :], ysum[:, :, :], skip[p][:, :, :],
                                        ALU.subtract).then_inc(y_ready, 1)

            def residual(t):
                dve.wait_ge(out_done, t + 1)
                dve.wait_ge(res_ready, t + 1)
                dve.wait_ge(scattered, 64 * t + 16)
                nc.vector.tensor_tensor(row[:, :, DM:2 * DM], bank[1][:, :].rearrange("p (j d) -> p j d", j=TILES),
                                        x_res[:, :, :], ALU.add).then_inc(x1_ready, 1)
                dve.wait_ge(x1_ready, t + 1)
                for j in range(TILES):
                    last = nc.vector.bn_stats(stat2[:, j, :], row[:, j, DM:2 * DM])
                last.then_inc(stats2, 1)
                dve.wait_ge(stats2, t + 1)
                dve.sem_inc(wait_carrier)
                for j in range(TILES):
                    last = nc.vector.bn_aggr(mv2[:, j, :], stat2[:, j, :])
                last.then_inc(mv2_ready, 1)

            def normalise2(t):
                dve.wait_ge(rstd2_ready, t + 1)
                for j in range(TILES):
                    last = nc.vector.tensor_scalar(row[:, j, 0:DM], row[:, j, DM:2 * DM], mv2[:, j, 0:1],
                                                   rstd2[:, j:j + 1], ALU.subtract, ALU.mult)
                last.then_inc(xn2_ready, 1)

            def choose(t):
                def spread(v):
                    return v.unsqueeze(1).to_broadcast([P, TILES, E])

                def along(v):
                    return v.unsqueeze(2).to_broadcast([P, TILES, E])

                dve.wait_ge(logit_done, t + 1)
                nc.vector.tensor_tensor(logit[:, :, :], bank[3][:, 0:TILES * E].rearrange("p (j e) -> p j e", j=TILES),
                                        spread(const("b_r")), ALU.add).then_inc(route, 1)
                dve.wait_ge(route, 7 * t + 1)
                nc.vector.tensor_reduce(top[:, :], logit[:, :, :], AX.X, ALU.max).then_inc(route, 1)
                dve.wait_ge(route, 7 * t + 2)
                nc.vector.tensor_tensor(is_top[:, :, :], logit[:, :, :], along(top[:, :]),
                                        ALU.is_equal).then_inc(route, 1)
                dve.wait_ge(route, 7 * t + 3)
                nc.vector.scalar_tensor_tensor(cand[:, :, :], is_top[:, :, :], -float(E), spread(const("expert_no8")),
                                               ALU.mult, ALU.add).then_inc(route, 1)
                dve.wait_ge(route, 7 * t + 4)
                nc.vector.tensor_reduce(chosen[:, :], cand[:, :, :], AX.X, ALU.min).then_inc(route, 1)
                dve.wait_ge(route, 7 * t + 5)
                nc.vector.tensor_tensor(one_hot[:, :, :], spread(const("expert_no")), along(chosen[:, :]),
                                        ALU.is_equal).then_inc(route, 1)
                nc.vector.tensor_tensor(shifted[:, :, :], logit[:, :, :], along(top[:, :]),
                                        ALU.subtract).then_inc(route, 1)

            def place(t):
                dve.wait_ge(rank_done, t + 1)
                nc.vector.tensor_tensor(slot_e[:, :, :],
                                        bank[3][:, 64:64 + TILES * E].rearrange("p (j e) -> p j e", j=TILES),
                                        filled[:, :].unsqueeze(1).to_broadcast([P, TILES, E]), ALU.add).then_inc(placed, 1)
                dve.wait_ge(placed, 9 * t + 1)
                nc.vector.tensor_tensor(filled[:, :], bank[3][:, 128:128 + E], filled[:, :], ALU.add).then_inc(placed, 1)
                nc.vector.tensor_tensor(slot_m[:, :, :], slot_e[:, :, :], one_hot[:, :, :], ALU.mult).then_inc(placed, 1)
                dve.wait_ge(placed, 9 * t + 3)
                nc.vector.tensor_reduce(slot[:, :], slot_m[:, :, :], AX.X, ALU.add).then_inc(placed, 1)
                dve.wait_ge(placed, 9 * t + 4)
                nc.vector.tensor_copy(slot_i[:, :], slot[:, :]).then_inc(placed, 1)
                dve.wait_ge(expd_ready, t + 1)
                nc.vector.tensor_reduce(zsum[:, :], expd[:, :, :], AX.X, ALU.add).then_inc(placed, 1)
                dve.wait_ge(placed, 9 * t + 6)
                nc.vector.reciprocal(row[:, :, 2 * DM], zsum[:, :]).then_inc(placed, 1)
                nc.vector.tensor_copy(row[:, :, :].bitcast(I32)[:, :, 2 * DM + 1], token[:, :]).then_inc(placed, 1)
                dve.wait_ge(placed, 9 * t + 8)
                nc.vector.tensor_scalar(token[:, :], token[:, :], float(L), None, ALU.add).then_inc(placed, 1)

            def body(b, p, first=False, last=False):
                n = None if last else b + 1
                t = None if first else b - 1
                for s in range(S):
                    scan(b, s, 0)
                    if s >= 1 and s - 1 in VEC_STATES:
                        times_c(b, s - 1)
                    if s == 0 and t is not None:
                        times_c(b - 1, S - 1)
                    scan(b, s, 1)
                    if n is not None and s == 1:
                        statistics(n, 1 - p)
                    if t is not None and s == 2:
                        finish_y(t, 1 - p)
                    if n is not None and s == 2:
                        normalise(n, 1 - p)
                    if n is not None and s in (4, 5):
                        for m in range(4 * (s - 4), 4 * (s - 3)):
                            convolve(n, m)
                    if n is not None and s == 6:
                        silu_z(n, 1 - p)
                        silu_conv(n)
                    if t is not None and s == 6:
                        residual(t)
                    if t is not None and s == 7:
                        normalise2(t)
                    if n is not None and s == 10:
                        copy_bcT(n)
                    if t is not None and s == 10:
                        choose(t)
                    if n is not None and s == 12:
                        softplus_poly(n, 1 - p, 0)
                        softplus_poly(n, 1 - p, 1)
                    if t is not None and s == 13:
                        place(t)
                    if n is not None and s == 13:
                        softplus_poly(n, 1 - p, 2)
                    if n is not None and s == 14:
                        skip_term(n, 1 - p, 0)
                        skip_term(n, 1 - p, 1)
                        softplus_poly(n, 1 - p, 3)
                    if n is not None and s == 15:
                        softplus_poly(n, 1 - p, 4)

            nc.vector.memset(xpad[:, :, 0:TAPS - 1], 0.0)
            nc.vector.memset(zero8[:, :], 0.0)
            dve.wait_ge(s_pack, 16)
            nc.vector.tensor_copy(filled[:, :], const("region_at"))
            nc.vector.tensor_copy(token[:, :], const("token")).then_inc(setup, 1)
            statistics(0, 0)
            normalise(0, 0)
            nc.vector.tensor_scalar(half_bin[:, :], b_in, 0.5, None, ALU.mult).then_inc(setup, 1)
            nc.vector.tensor_scalar(const("conv_w"), const("conv_w"), 0.5, None, ALU.mult).then_inc(setup, 1)
            nc.vector.tensor_scalar(conv_b, conv_b, 0.5, None, ALU.mult).then_inc(setup, 1)
            dve.wait_ge(setup, 4)
            for m in range(8):
                convolve(0, m)
            silu_z(0, 0)
            silu_conv(0)
            dve.wait_ge(setup_a, 1)
            nc.vector.tensor_scalar(tiny_a[:, :], neg_a[:, :], 1e-6, None, ALU.is_lt)
            nc.vector.tensor_scalar(tiny_s[:, :], inv_a_s[:, :], 1e-6, None, ALU.is_lt)
            nc.vector.tensor_scalar(neg_d[:, :], d_skip, -1.0, None, ALU.mult).then_inc(setup, 1)
            dve.wait_ge(setup, 5)
            nc.vector.scalar_tensor_tensor(inv_a[:, :], tiny_a[:, :], 1.0, neg_a[:, :], ALU.subtract, ALU.mult)
            nc.vector.scalar_tensor_tensor(inv_a_s[:, :], tiny_s[:, :], 1.0, inv_a_s[:, :],
                                           ALU.subtract, ALU.mult).then_inc(setup, 1)
            dve.wait_ge(setup, 6)
            nc.vector.tensor_tensor(inv_a[:, :], inv_a[:, :], tiny_a[:, :], ALU.add)
            nc.vector.tensor_scalar(neg_a[:, :], neg_a[:, :], -1.0, None, ALU.mult)
            nc.vector.tensor_tensor(inv_a_s[:, :], inv_a_s[:, :], tiny_s[:, :], ALU.add).then_inc(setup, 1)
            dve.wait_ge(setup, 7)
            nc.vector.reciprocal(inv_a[:, :], inv_a[:, :])
            nc.vector.reciprocal(inv_a_s[:, :], inv_a_s[:, :]).then_inc(setup, 1)
            copy_bcT(0)
            softplus_poly(0, 0, 0)
            softplus_poly(0, 0, 1)
            skip_term(0, 0, 0)
            skip_term(0, 0, 1)
            for i in range(2, 5):
                softplus_poly(0, 0, i)
            dve.wait_ge(setup, 8)
            for h in range(H):
                for s in range(S):
                    at = h * S + s
                    last = nc.vector.tensor_scalar(diag[:, h, s, :], ident, inv_a[:, at:at + 1], None, ALU.mult)
            last.then_inc(setup, 1)
            body(0, 0, first=True)
            with dve.Fori(0, (NB - 2) // 2) as i:
                body(2 * i + 1, 1)
                body(2 * i + 2, 0)
            body(NB - 1, 1, last=True)
            times_c(NB - 1, S - 1)
            finish_y(NB - 1, 1)
            residual(NB - 1)
            normalise2(NB - 1)
            choose(NB - 1)
            place(NB - 1)

            def link(count_now):
                dve.wait_ge(planned, count_now)

            dve.wait_ge(placed, 9 * NB)
            nc.vector.tensor_copy(filled_i[:, :], filled[0:1, :]).then_inc(planned, 1)
            nc.vector.tensor_tensor(count[:, :], filled[0:1, :], const("region_at")[0:1, :], ALU.subtract).then_inc(planned, 1)
            link(2)
            nc.vector.tensor_tensor(full[:, :, :], count[:, :].unsqueeze(2).to_broadcast([1, E, TOK // P]),
                                    const("tile_at")[0:1, :].unsqueeze(1).to_broadcast([1, E, TOK // P]),
                                    ALU.is_gt).then_inc(planned, 1)
            link(3)
            nc.vector.tensor_reduce(n_tiles[:, :], full[:, :, :], AX.X, ALU.add).then_inc(planned, 1)
            link(4)
            nc.vector.tensor_tensor_scan(end_tile[:, :], n_tiles[:, :], zero8[:, :], 0.0, ALU.add,
                                         ALU.add).then_inc(planned, 1)
            link(5)
            tile_no = const("tile_no")[0:1, :]
            nc.vector.tensor_tensor(passed[:, :, :], end_tile[:, :].unsqueeze(1).to_broadcast([1, FTILES, E]),
                                    tile_no.unsqueeze(2).to_broadcast([1, FTILES, E]), ALU.is_le).then_inc(planned, 1)
            link(6)
            nc.vector.tensor_reduce(t_exp[:, :], passed[:, :, :], AX.X, ALU.add)
            nc.vector.tensor_tensor(passed_n[:, :, :], passed[:, :, :],
                                    n_tiles[:, :].unsqueeze(1).to_broadcast([1, FTILES, E]), ALU.mult).then_inc(planned, 1)
            link(7)
            nc.vector.tensor_reduce(t_off[:, :], passed_n[:, :, :], AX.X, ALU.add)
            nc.vector.tensor_scalar(t_exp_i[:, :], t_exp[:, :], float(E - 1), None, ALU.min)
            nc.vector.tensor_scalar(t_row[:, :], t_exp[:, :], float(REGION), None, ALU.mult).then_inc(planned, 1)
            link(8)
            nc.vector.tensor_tensor(t_off[:, :], tile_no, t_off[:, :], ALU.subtract).then_inc(planned, 1)
            link(9)
            nc.vector.scalar_tensor_tensor(t_row_i[:, :], t_off[:, :], float(P), t_row[:, :], ALU.mult,
                                           ALU.add).then_inc(planned, 1)
            link(10)

            def take_weights(k, c):
                i = FU * k + c
                e = dve.value_load(t_exp_i[0:1, bass.ds(i, 1)], min_val=0, max_val=E - 1)
                if not starts(k, c, 2):
                    dve.wait_ge(hidden_done, i - 1)
                nc.vector.tensor_copy(f_w[c % 2][:, 0:FF], w_all[:, bass.ds(e, 1), 0:FF].squeeze(1)).then_inc(w1_taken, 1)
                if not starts(k, c, 2):
                    dve.wait_ge(mlp_done, i - 1)
                nc.vector.tensor_copy(f_w[c % 2][:, FF:], w_all[:, bass.ds(e, 1), FF:].squeeze(1)).then_inc(w2_taken, 1)

            def take_xT(k, c):
                i = FU * k + c
                dve.wait_ge(f_turned, i + 1)
                if not starts(k, c, 2):
                    dve.wait_ge(hidden_done, i - 1)
                nc.vector.tensor_copy(f_xT[c % 2][:, :], bank[c % 2][:, 0:P]).then_inc(f_xT_ready, 1)

            def combine(k, c):
                i = FU * k + c
                dve.wait_ge(mlp_done, i + 1)
                nc.vector.scalar_tensor_tensor(f_out[c], dv[c % 2][:, 0:P], f_row[c][:, 2 * DM:2 * DM + 1],
                                               f_row[c][:, DM:2 * DM], ALU.mult, ALU.add).then_inc(combined, 1)

            def tiles(k):
                for c in range(FU):
                    if not ends(k, c):
                        take_weights(*after(k, c))
                        take_xT(*after(k, c))
                    if not starts(k, c, 1):
                        combine(*ahead(k, c))

            dve.wait_ge(w_loaded, 16 * E)
            take_weights(0, 0)
            take_xT(0, 0)
            tiles(0)
            with dve.Fori(1, FTILES // FU - 1) as k:
                tiles(k)
            tiles(FTILES // FU - 1)
            combine(FTILES // FU - 1, FU - 1)

        @block.gpsimd
        def _(pool):
            def rstd(n):
                pool.wait_ge(mv1_ready, n + 1)
                nc.gpsimd.tensor_tensor(var1[:, :], mv1[:, :, 1], const("eps"), ALU.add).then_inc(var1_ready, 1)
                pool.wait_ge(var1_ready, n + 1)
                if not early(n):
                    pool.wait_ge(xn_ready, n)
                nc.gpsimd.tensor_tensor(rstd1[:, :], var1[:, :], const("minus_half"), ALU.pow).then_inc(rstd1_ready, 1)

            def rstd_2(t):
                pool.wait_ge(mv2_ready, t + 1)
                nc.gpsimd.tensor_tensor(var2[:, :], mv2[:, :, 1], const("eps"), ALU.add).then_inc(var2_ready, 1)
                pool.wait_ge(var2_ready, t + 1)
                nc.gpsimd.tensor_tensor(rstd2[:, :], var2[:, :], const("minus_half"), ALU.pow).then_inc(rstd2_ready, 1)

            def build_delta(n, g):
                pool.wait_ge(bcT_ready, n + 1)
                if not early(n):
                    pool.wait_ge(dv_ready, 32 * (n - 1) + 8 * g + 8)
                b_col = bc_T[:, :, 4 * g:4 * g + 4].rearrange("p j s -> p s j")
                nc.gpsimd.tensor_tensor(delta[:, 4 * g:4 * g + 4, :, :],
                                        bidiag.unsqueeze(1).unsqueeze(1).to_broadcast([P, 4, TILES, BW]),
                                        b_col.unsqueeze(3).to_broadcast([P, 4, TILES, BW]),
                                        ALU.mult).then_inc(delta_ready, 1)

            def times_c(n, s):
                pool.wait_ge(scanned, 32 * n + 2 * s + 2)
                pool.wait_ge(c_loaded[s // 4], 16 * (n + 1))
                if not (isinstance(n, int) and 32 * n + 2 * s < 4):
                    pool.wait_ge(summed, 32 * n + 2 * s - 2)
                nc.gpsimd.tensor_tensor(prod[s % 2][:, :, :], k_st[s % 2][:, :, :],
                                        c_all[:, s:s + 1, :].to_broadcast([P, H, L]), ALU.mult).then_inc(prod_pool, 1)

            def times_gate(t, p):
                pool.wait_ge(y_ready, t + 1)
                pool.wait_ge(gate_ready, t + 1)
                nc.gpsimd.tensor_tensor(y[:, :, :], y[:, :, :], gate_z[p][:, :, :], ALU.mult).then_inc(yg_ready, 1)
                pool.wait_ge(res_loaded, 16 * (t + 1))
                nc.gpsimd.tensor_tensor(x_res[:, :, :], x_res[:, :, :],
                                        const("out_b").unsqueeze(1).to_broadcast([P, TILES, DM]),
                                        ALU.add).then_inc(res_ready, 1)

            def scatter(t):
                pool.wait_ge(placed, 9 * t + 8)
                pool.wait_ge(xn2_ready, t + 1)
                pool.sem_inc(wait_carrier)
                for j in range(TILES):
                    nc.gpsimd.indirect_dma_start(rows_d, bass.IndirectOffsetOnAxis(ap=slot_i[:, j:j + 1], axis=0),
                                                 row[:, j, :], None, bounds_check=ROWS - 1,
                                                 oob_is_err=False).then_inc(scattered, 16)

            def body(b, p, first=False, last=False):
                n = None if last else b + 1
                t = None if first else b - 1
                for s in range(S):
                    if s >= 1 and s - 1 in POOL_STATES:
                        times_c(b, s - 1)
                    if n is not None and s == 1:
                        rstd(n)
                    if t is not None and s == 2:
                        times_gate(t, 1 - p)
                    if t is not None and s == 4:
                        build_delta(b, 3)
                    if t is not None and s == 6:
                        rstd_2(t)
                    if n is not None and s in (11, 13, 15):
                        build_delta(n, (s - 11) // 2)
                    if t is not None and s == 14:
                        scatter(t)

            nc.gpsimd.memset(pad[:, :], 0.0).then_inc(pad_zero, 1)
            pool.wait_ge(pad_zero, 1)
            nc.gpsimd.memset(pad[:, :].bitcast(I32)[:, 2 * DM + 1:], NO_TOKEN).then_inc(s_pad_ready, 1)
            pool.wait_ge(s_pad_ready, 1)
            pool.dma_start(rows_d[E * REGION:ROWS, :].rearrange("(c q) w -> q c w", q=P),
                           pad[:, :].unsqueeze(1).to_broadcast([P, (ROWS - E * REGION) // P, RW])).then_inc(scattered, 16)
            pool.wait_ge(s_pack, 16)
            rstd(0)
            for g in range(4):
                build_delta(0, g)
            body(0, 0, first=True)
            with pool.Fori(0, (NB - 2) // 2) as i:
                body(2 * i + 1, 1)
                body(2 * i + 2, 0)
            body(NB - 1, 1, last=True)
            times_gate(NB - 1, 1)
            rstd_2(NB - 1)
            scatter(NB - 1)

            pool.wait_ge(planned, 1)
            for e in range(E):
                at = pool.value_load(filled_i[0:1, e:e + 1], min_val=e * REGION, max_val=e * REGION + TOK)
                pool.dma_start(rows_d[bass.ds(at, P), :], pad[:, :]).then_inc(padded, 16)
            pool.wait_ge(scattered, 64 * NB + 16)
            pool.wait_ge(padded, 16 * E)
            pool.sem_inc(rows_filled)

            def store_rows(k, c):
                pool.wait_ge(combined, FU * k + c + 1)
                pool.sem_inc(wait_carrier)
                nc.gpsimd.indirect_dma_start(
                    out_d, bass.IndirectOffsetOnAxis(ap=f_row[c][:, :].bitcast(I32)[:, 2 * DM + 1:], axis=0),
                    f_out[c], None, bounds_check=TOK - 1, oob_is_err=False).then_inc(f_stored[c], 16)

            def tiles(k):
                for c in range(FU):
                    store_rows(k, c)

            tiles(0)
            with pool.Fori(1, FTILES // FU - 1) as k:
                tiles(k)
            tiles(FTILES // FU - 1)
            for c in range(FU):
                pool.wait_ge(f_stored[c], 16 * (FTILES // FU))


def packed(a):
    f = np.float32
    pack = np.zeros((P, PACK_W), f)

    def put(name, v):
        v = np.asarray(v, f)
        pack[:v.shape[0], AT[name][0]:AT[name][1]] = v

    def rows(v):
        return np.broadcast_to(np.asarray(v, f), (P, len(v)))

    def halves(v):
        return np.swapaxes(v.reshape((-1, P) + v.shape[1:]), 0, 1).reshape(P, -1)

    put("ident", np.eye(P))
    put("bidiag", np.eye(P, BW) - np.eye(P, BW, 1))
    put("before", np.triu(np.ones((P, P)), 1))
    put("ones", np.ones((P, P)))
    put("expert_no", rows(range(E)))
    put("expert_no8", rows(range(E, 2 * E)))
    put("region_at", rows([e * REGION for e in range(E)]))
    put("token", np.arange(TILES)[None, :] * P + np.arange(P)[:, None])
    put("quad_a", rows(QUAD_A))
    put("minus_half", np.full((P, TILES), -0.5))
    put("eps", np.full((P, TILES), EPS))
    put("tile_at", rows([P * j for j in range(TOK // P)]))
    put("tile_no", rows(range(FTILES)))
    put("w_in", a["L0_attn_in_proj_w"].T)
    put("b_in", halves(a["L0_attn_in_proj_b"]))
    put("conv_w", halves(a["L0_attn_conv_w"]))
    put("conv_b", halves(a["L0_attn_conv_b"]))
    put("a_log", halves(a["L0_attn_A_log"].T))
    put("d_skip", halves(a["L0_attn_D"]))
    put("x_proj", halves(a["L0_attn_x_proj_w"].T))
    put("dt_w", a["L0_attn_dt_proj_w"].T)
    put("dt_b", halves(a["L0_attn_dt_proj_b"]))
    put("a_log_s", a["L0_attn_A_log"])
    put("out_w", halves(a["L0_attn_out_proj_w"].T))
    put("out_b", rows(a["L0_attn_out_proj_b"]))
    put("w_r", a["L0_ffn_Wr"])
    put("b_r", rows(a["L0_ffn_br"]))
    return pack


def kernel(**inputs):
    import concourse.bacc as bacc
    from concourse.bass_utils import run_bass_kernel_spmd

    a = {k: np.asarray(v) for k, v in inputs.items()}
    experts = np.zeros((E, P, EW), np.float32)
    experts[:, :, 0:FF] = a["L0_ffn_W1"]
    experts[:, :, FF:FF + FK * DM] = a["L0_ffn_W2"].reshape(E, FK, P, DM).transpose(0, 2, 1, 3).reshape(E, P, FK * DM)
    experts[:, :, FF + FK * DM:FF + FK * DM + FK] = a["L0_ffn_b1"].reshape(E, FK, P).transpose(0, 2, 1)
    experts[:, 0, EW - DM:] = a["L0_ffn_b2"]
    arrays = {"x_d": np.ascontiguousarray(a["L0_attn_x"]), "pack_d": packed(a), "experts_d": experts}

    nc = bacc.Bacc("TRN2", target_bir_lowering=False, num_devices=1)
    f32 = mybir.dt.float32
    args = [nc.dram_tensor(n, v.shape, f32, kind="ExternalInput").ap() for n, v in arrays.items()]
    out = nc.dram_tensor("out", (TOK, DM), f32, kind="ExternalOutput").ap()
    c_scratch = nc.dram_tensor("c_scratch", (2, S, L), f32, kind="Internal").ap()
    rows_d = nc.dram_tensor("rows_d", (ROWS, RW), f32, kind="Internal").ap()
    program(nc, *args, out, c_scratch, rows_d)
    r = run_bass_kernel_spmd(nc, [arrays], core_ids=[0])
    return r.results[0]["out"].reshape(NB, L, DM)
```

```python
import numpy as np
import concourse.bass as bass
import concourse.mybir as mybir
from contextlib import ExitStack

P = 128
NB, L, DM = 8, 512, 128
TILES = L // P
H, S, R = 2, 16, 64
DI = H * P
TAPS = 4
E, FF = 8, 512
FK = FF // P
TOK = NB * L
REGION = TOK + P
FU = 8
FTILES = TOK // P + E
EARLY = 2 * FU
assert EARLY * P <= (NB - 1) * L - E * (P - 1)
ROWS = E * REGION + (FTILES - TOK // P) * P
RW = 2 * DM + 2
NO_TOKEN = TOK
RANKS = 64
BW = P + 1
EW = FF + FK * DM + FK + DM
EPS = 1e-5

QUAD_A = (1.0093575430011281, -0.08225440736378242, -1.424741164592344, -2.3216937658543895)
QUAD_B = (1.106067408717108, 3.2574833956522826, 2.702115883781287, 0.43240884150072795)
LEAD = 0.0052325939439559314

PACK = [("ident", P), ("bidiag", BW), ("before", P), ("ones", P), ("expert_no", E), ("expert_no8", E),
        ("region_at", E), ("token", TILES), ("quad_a", 4), ("minus_half", TILES), ("eps", TILES), ("tile_at", TOK // P),
        ("tile_no", FTILES),
        ("w_in", 2 * DI), ("b_in", 2 * H), ("conv_w", H * TAPS), ("conv_b", H), ("a_log", H * S),
        ("d_skip", H), ("x_proj", H * (R + 2 * S)), ("dt_w", DI), ("dt_b", H), ("a_log_s", DI),
        ("out_w", H * DM), ("out_b", DM), ("w_r", E), ("b_r", E)]
AT, PACK_W = {}, 0
for _name, _width in PACK:
    AT[_name] = (PACK_W, PACK_W + _width)
    PACK_W += _width

POOL_STATES = (2, 6, 10, 14)
VEC_STATES = tuple(s for s in range(S) if s not in POOL_STATES)
NV, NP_ = len(VEC_STATES), len(POOL_STATES)


def vec_before(s):
    return sum(1 for q in VEC_STATES if q < s)


def pool_before(s):
    return sum(1 for q in POOL_STATES if q < s)


def early(n, m=1):
    return isinstance(n, int) and n < m


PADS_AT = 6


def after(k, c, n=1):
    return (k, c + n) if c + n < FU else (k + 1, c + n - FU)


def ahead(k, c):
    return (k, c - 1) if c else (k - 1, FU - 1)


def starts(k, c, n):
    return isinstance(k, int) and FU * k + c < n


def ends(k, c, n=1):
    return isinstance(k, int) and FU * k + c >= FTILES - n


def program(nc, x_d, pack_d, experts_d, out_d, c_scratch, rows_d):
    F32, I32 = mybir.dt.float32, mybir.dt.int32
    ALU, ACT, AX = mybir.AluOpType, mybir.ActivationFunctionType, mybir.AxisListType
    ctx = ExitStack()
    with ctx:
        def sb(name, shape, dt=F32):
            return ctx.enter_context(nc.sbuf_tensor(name, shape, dt))

        def sem(name):
            return ctx.enter_context(nc.semaphore(name))

        pack = sb("pack", [P, PACK_W])

        def const(name):
            return pack[:, AT[name][0]:AT[name][1]]

        ident, bidiag, before, ones = const("ident"), const("bidiag"), const("before"), const("ones")
        w_in, b_in = const("w_in"), const("b_in")
        conv_w = const("conv_w").rearrange("p (h k) -> p h k", h=H)
        conv_b, d_skip, dt_b = const("conv_b"), const("d_skip"), const("dt_b")
        x_proj = const("x_proj").rearrange("p (h r) -> p h r", h=H)
        out_w = const("out_w").rearrange("p (h r) -> p h r", h=H)
        dt_w = pack[0:R, AT["dt_w"][0]:AT["dt_w"][1]]
        a_log_s = pack[0:S, AT["a_log_s"][0]:AT["a_log_s"][1]]

        half_bin = sb("half_bin", [P, 2 * H])
        conv_in = sb("conv_in", [P, H])
        neg_d = sb("neg_d", [P, H])
        neg_a = sb("neg_a", [P, H * S])
        inv_a = sb("inv_a", [P, H * S])
        tiny_a = sb("tiny_a", [P, H * S])
        tiny_s = sb("tiny_s", [S, DI])
        inv_a_s = sb("inv_a_s", [S, DI])
        diag = sb("diag", [P, H, S, P])

        
        x_in = [sb(f"x_in{i}", [P, TILES, DM]) for i in range(2)]
        stat1, mv1 = sb("stat1", [P, TILES, 6]), sb("mv1", [P, TILES, 2])
        var1, rstd1 = sb("var1", [P, TILES]), sb("rstd1", [P, TILES])
        xn, xnT = sb("xn", [P, TILES, DM]), sb("xnT", [P, L])
        xpad = sb("xpad", [P, H, TAPS - 1 + L])
        tanh_z = sb("tanh_z", [P, H, L])
        tanh_u = sb("tanh_u", [P, H, L])
        conv = sb("conv", [P, H, L])
        z_half = sb("z_half", [P, H, L])
        abs_p, y_exp, relu_p, poly = tanh_z, tanh_u, conv, z_half
        square = [sb(f"square{i}", [P, H, L]) for i in range(2)]
        gate_z = [sb(f"gate_z{i}", [P, H, L]) for i in range(2)]
        xc = sb("xc", [P, H, L])
        xcT = [sb(f"xcT{i}", [P, TILES, DI]) for i in range(2)]
        x_dbl = sb("x_dbl", [R + 2 * S, L])
        bc_T, bc_mul = sb("bc_T", [P, TILES, 2 * S]), sb("bc_mul", [P, TILES, S])
        bc_s = sb("bc_s", [S, L])
        skip = [sb(f"skip{i}", [P, H, L]) for i in range(2)]
        dt = [sb(f"dt{i}", [P, H, L]) for i in range(2)]

        big = sb("big", [P, S * TILES * BW + S * L])
        delta = big[:, 0:S * TILES * BW].rearrange("p (s j c) -> p s j c", s=S, j=TILES)
        c_all = big[:, S * TILES * BW:].rearrange("p (s t) -> p s t", s=S)
        w_all = big[:, 0:E * EW].rearrange("p (e c) -> p e c", e=E)
        a_bar = [sb(f"a_bar{i}", [P, L]) for i in range(4)]
        steps = sb("steps", [P, 4 * H * L])

        def step_slot(i):
            return steps[:, i * H * L:(i + 1) * H * L].rearrange("p (h t) -> p h t", h=H)

        k_st, prod = [step_slot(i) for i in range(2)], [step_slot(2 + i) for i in range(2)]

        y = sb("y", [P, H, L])
        x_res = sb("x_res", [P, TILES, DM])
        row = sb("row", [P, TILES, RW])
        stat2, mv2 = sb("stat2", [P, TILES, 6]), sb("mv2", [P, TILES, 2])
        var2, rstd2 = sb("var2", [P, TILES]), sb("rstd2", [P, TILES])
        xn2T = sb("xn2T", [P, L])
        logit, shifted, expd = (sb(n, [P, TILES, E]) for n in ("logit", "shifted", "expd"))
        top, chosen, zsum = (sb(n, [P, TILES]) for n in ("top", "chosen", "zsum"))
        is_top, cand = (sb(n, [P, TILES, E]) for n in ("is_top", "cand"))
        one_hot = sb("one_hot", [P, TILES + 1, E])
        slot_e, slot_m, slot = sb("slot_e", [P, TILES, E]), sb("slot_m", [P, TILES, E]), sb("slot", [P, TILES])
        slot_i = sb("slot_i", [P, TILES], I32)
        filled = sb("filled", [P, E])
        token = sb("token", [P, TILES])

        def flat(v):
            return v[:, :, :].rearrange("p h t -> p (h t)")

        plan_w = [0]

        def plan(width, dt=F32):
            at = plan_w[0]
            plan_w[0] += width
            v = flat(square[0])[0:1, at:at + width]
            return v if dt == F32 else v.bitcast(dt)

        STAGE = max(EARLY, FTILES - EARLY)
        count, n_tiles, end_tile, filled_i, jump = plan(E), plan(E), plan(E), plan(E, I32), plan(E)
        taken = plan(E + 1)
        full = plan(E * (TOK // P)).rearrange("p (e j) -> p e j", e=E)
        passed_all, passed_jump = (plan(STAGE * E).rearrange("p (i e) -> p i e", e=E) for _ in range(2))
        t_exp, t_off, t_row = plan(STAGE), plan(STAGE), plan(STAGE)
        t_exp_i, t_row_i = plan(FTILES, I32), plan(FTILES, I32)
        zero8 = sb("zero8", [1, E])
        pad = sb("pad", [P, RW])
        f_row = [flat(v)[:, i * RW:(i + 1) * RW] for v in (xcT[0], skip[0], gate_z[0]) for i in range(3)][:FU]
        f_xT = [xnT[:, i * P:(i + 1) * P] for i in range(4)]
        f_w1 = [conv[:, i, :] for i in range(2)]
        f_w2 = [flat(v)[:, 0:EW - FF] for v in (z_half, tanh_u, xc, square[1])]
        f_h = [tanh_z[:, i, :] for i in range(2)]
        f_out = [v[:, c, :] for v in x_in for c in range(TILES)]

        bank = [ctx.enter_context(nc.psum_tensor(f"bank{i}", [P, L], F32)) for i in range(4)]
        dv = [ctx.enter_context(nc.psum_tensor(f"dv{i}", [P, L], F32)) for i in range(2)]
        ysum = ctx.enter_context(nc.psum_tensor("ysum", [P, H, L], F32))

        wait_carrier = sem("wait_carrier")
        s_pack, s_pad_ready = sem("pack_loaded"), sem("pad_ready")
        x_loaded, res_loaded = sem("x_loaded"), sem("res_loaded")
        c_stored = sem("c_stored")
        c_loaded = [sem(f"c_loaded{g}") for g in range(4)]
        setup_a, setup = sem("setup_a"), sem("setup")
        stats1, mv1_ready, var1_ready, rstd1_ready = sem("stats1"), sem("mv1_ready"), sem("var1_ready"), sem("rstd1_ready")
        xn_ready, xn_turned, xnT_ready = sem("xn_ready"), sem("xn_turned"), sem("xnT_ready")
        in_done, in_read = sem("in_done"), sem("in_read")
        conv_step, tanhz_ready, tanhu_ready = sem("conv_step"), sem("tanhz_ready"), sem("tanhu_ready")
        gate_ready, xc_ready = sem("gate_ready"), sem("xc_ready")
        xdbl_done, xdbl_ready = sem("xdbl_done"), sem("xdbl_ready")
        xc_turned, xcT_ready = sem("xc_turned"), sem("xcT_ready")
        xdbl_turned, bcT_ready, bcmul_ready = sem("xdbl_turned"), sem("bcT_ready"), sem("bcmul_ready")
        bc_turned, bcs_ready, q_done, skip_ready = sem("bc_turned"), sem("bcs_ready"), sem("q_done"), sem("skip_ready")
        dt_done, dt_read, yexp_ready, square_ready, poly_step = (
            sem("dt_done"), sem("dt_read"), sem("yexp_ready"), sem("square_ready"), sem("poly_step"))
        delta_ready, dv_ready, abar_ready, scanned = sem("delta_ready"), sem("dv_ready"), sem("abar_ready"), sem("scanned")
        prod_vec, prod_pool, summed = sem("prod_vec"), sem("prod_pool"), sem("summed")
        y_ready, yg_ready, out_done, res_ready = sem("y_ready"), sem("yg_ready"), sem("out_done"), sem("res_ready")
        x1_ready, stats2, mv2_ready, var2_ready, rstd2_ready = (
            sem("x1_ready"), sem("stats2"), sem("mv2_ready"), sem("var2_ready"), sem("rstd2_ready"))
        xn2_ready, xn2_turned, xn2T_ready, logit_done = sem("xn2_ready"), sem("xn2_turned"), sem("xn2T_ready"), sem("logit_done")
        route, expd_ready, rank_done, placed, scattered = (
            sem("route"), sem("expd_ready"), sem("rank_done"), sem("placed"), sem("scattered"))

        pad_zero, padded, planned, w_loaded = sem("pad_zero"), sem("padded"), sem("planned"), sem("w_loaded")
        early_ends, ends_ready = sem("early_ends"), sem("ends_ready")
        f_loaded = [sem(f"f_loaded{c}") for c in range(FU)]
        f_stored = [sem(f"f_stored{c}") for c in range(FU)]
        f_turned, f_xT_ready, w1_taken, w2_taken = sem("f_turned"), sem("f_xT_ready"), sem("w1_taken"), sem("w2_taken")
        hidden_done, gelu_done, mlp_done, combined = sem("hidden_done"), sem("gelu_done"), sem("mlp_done"), sem("combined")

        block = ctx.enter_context(nc.Block())


        @block.sync
        def _(sp):
            def load_x(n, p):
                if not early(n):
                    sp.wait_ge(x_loaded, 16 * n)
                    sp.sem_inc(wait_carrier)
                if not early(n, 2):
                    sp.wait_ge(xn_ready, n - 1)
                sp.dma_start(x_in[p][:, :, :], x_d[n].rearrange("(j q) d -> q j d", q=P)).then_inc(x_loaded, 16)

            def load_residual(t):
                if not early(t):
                    sp.wait_ge(x1_ready, t)
                sp.dma_start(x_res[:, :, :], x_d[t].rearrange("(j q) d -> q j d", q=P)).then_inc(res_loaded, 16)

            def store_c(n, p):
                sp.wait_ge(xdbl_ready, n + 1)
                sp.dma_start(c_scratch[p], x_dbl[R + S:R + 2 * S, :]).then_inc(c_stored, 16)

            def load_c(n, p, g):
                sp.wait_ge(c_stored, 16 * (n + 1))
                if not early(n):
                    sp.sem_inc(wait_carrier)
                    sp.wait_ge(prod_vec, NV * (n - 1) + vec_before(4 * g + 4))
                    sp.sem_inc(wait_carrier)
                    sp.wait_ge(prod_pool, NP_ * (n - 1) + pool_before(4 * g + 4))
                src = bass.AP(c_scratch.tensor, (p * S + 4 * g) * L, [[0, P], [1, 4 * L]])
                sp.dma_start(c_all[:, 4 * g:4 * g + 4, :].rearrange("p s t -> p (s t)"), src).then_inc(c_loaded[g], 16)

            def body(b, p, first=False, last=False):
                if not last:
                    load_x(b + 1, 1 - p)
                load_c(b, p, 3)
                if not first:
                    load_residual(b - 1)
                if not last:
                    store_c(b + 1, 1 - p)
                    for g in range(3):
                        load_c(b + 1, 1 - p, g)

            sp.dma_start(pack[:, :], pack_d).then_inc(s_pack, 16)
            load_x(0, 0)
            store_c(0, 0)
            for g in range(3):
                load_c(0, 0, g)
            body(0, 0, first=True)
            with sp.Fori(0, (NB - 2) // 2) as i:
                body(2 * i + 1, 1)
                body(2 * i + 2, 0)
            body(NB - 1, 1, last=True)
            load_residual(NB - 1)

            def load_weights(e):
                states = min(S, -(-(e + 1) * EW // (TILES * BW)))
                sp.wait_ge(dv_ready, 32 * (NB - 1) + 2 * states)
                if (e + 1) * EW > S * TILES * BW:
                    c_states = -(-((e + 1) * EW - S * TILES * BW) // L)
                    sp.wait_ge(prod_vec, NV * (NB - 1) + vec_before(c_states))
                    sp.wait_ge(prod_pool, NP_ * (NB - 1) + pool_before(c_states))
                sp.dma_start(w_all[:, e, :], experts_d[e]).then_inc(w_loaded, 16)

            def load_rows(k, c):
                if not starts(k, c, FU):
                    sp.wait_ge(f_stored[c], 16 * k)
                    sp.sem_inc(wait_carrier)
                at = sp.value_load(t_row_i[0:1, bass.ds(FU * k + c, 1)], min_val=0, max_val=ROWS - P)
                sp.dma_start(f_row[c][:, :], rows_d[bass.ds(at, P), :]).then_inc(f_loaded[c], 16)

            for e in range(E):
                load_weights(e)
            sp.wait_ge(scattered, 64 * (NB - 1) + 16)
            sp.wait_ge(planned, 10)
            sp.sem_inc(wait_carrier)
            for c in range(FU):
                load_rows(0, c)
            for c in range(PADS_AT):
                load_rows(1, c)
            sp.wait_ge(ends_ready, 1)
            sp.sem_inc(wait_carrier)
            for e in range(E // 2):
                at = sp.value_load(filled_i[0:1, e:e + 1], min_val=e * REGION, max_val=e * REGION + TOK)
                sp.dma_start(rows_d[bass.ds(at, P), :], pad[:, :]).then_inc(padded, 16)
            for c in range(PADS_AT, FU):
                load_rows(1, c)
            sp.wait_ge(scattered, 64 * NB + 16)
            sp.wait_ge(padded, 16 * E)
            sp.wait_ge(planned, 20)
            sp.sem_inc(wait_carrier)
            with sp.Fori(EARLY // FU, FTILES // FU) as k:
                for c in range(FU):
                    load_rows(k, c)
            sp.wait_ge(w_loaded, 16 * E)

        @block.tensor
        def _(pe):
            def turn_xn(n):
                pe.wait_ge(xn_ready, n + 1)
                if not early(n):
                    pe.wait_ge(skip_ready, 2 * n - 1)
                for j in range(TILES):
                    last = nc.tensor.transpose(bank[0][:, j * P:(j + 1) * P], xn[:, j, :], ident)
                last.then_inc(xn_turned, 1)

            def in_proj(n, m):
                if m == 0:
                    pe.wait_ge(xnT_ready, n + 1)
                    if not early(n):
                        pe.wait_ge(bcs_ready, n)
                if m == 1 and not early(n):
                    pe.wait_ge(skip_ready, 2 * n)
                nc.tensor.matmul(bank[(m + 1) % 4][:, :], w_in[:, m * P:(m + 1) * P], xnT[:, :],
                                 start=True, stop=True).then_inc(in_done, 1)

            def x_projection(n):
                pe.wait_ge(xc_ready, n + 1)
                for h in range(H):
                    last = nc.tensor.matmul(bank[1][0:R + 2 * S, :], x_proj[:, h, :], xc[:, h, :],
                                            start=(h == 0), stop=(h == H - 1))
                last.then_inc(xdbl_done, 1)

            def turn_xc(n, part):
                pe.wait_ge(dt_read, 2 * n + part + 1)
                to = bank[2 * part]
                for j in range(2):
                    for h in range(H):
                        at = j * DI + h * P
                        j0 = (2 * part + j) * P
                        last = nc.tensor.transpose(to[:, at:at + P], xc[:, h, j0:j0 + P], ident)
                last.then_inc(xc_turned, 1)

            def turn_xdbl(n):
                pe.wait_ge(xdbl_ready, n + 1)
                for j in range(TILES):
                    last = nc.tensor.transpose(bank[1][:, j * 96:(j + 1) * 96], x_dbl[:, j * P:(j + 1) * P],
                                               ident[0:96, 0:96])
                last.then_inc(xdbl_turned, 1)

            def dt_proj(n, t, h):
                pe.wait_ge(xdbl_ready, n + 1)
                if h == 0 and t is not None:
                    pe.wait_ge(x1_ready, t + 1)
                elif h == 0:
                    pe.wait_ge(in_read, 4 * n + 4)
                nc.tensor.matmul(bank[2 * h][:, :], dt_w[:, h * P:(h + 1) * P], x_dbl[0:R, :],
                                 start=True, stop=True).then_inc(dt_done, 1)

            def turn_bc(n):
                pe.wait_ge(bcmul_ready, n + 1)
                for j in range(TILES):
                    last = nc.tensor.transpose(bank[1][0:S, j * P:(j + 1) * P], bc_mul[:, j, :], ident)
                last.then_inc(bc_turned, 1)

            def q_matmul(n, h):
                pe.wait_ge(bcs_ready, n + 1)
                pe.wait_ge(xcT_ready, 2 * n + h + 1)
                nc.tensor.matmul(bank[2 * h][:, :], inv_a_s[:, h * P:(h + 1) * P], bc_s[:, :],
                                 start=True, stop=True).then_inc(q_done, 1)

            def out_proj(t, n):
                pe.wait_ge(yg_ready, t + 1)
                if n is not None:
                    pe.wait_ge(in_read, 4 * n + 4)
                else:
                    pe.wait_ge(skip_ready, 2 * NB)
                    pe.wait_ge(x1_ready, t)
                for j in range(TILES):
                    for h in range(H):
                        last = nc.tensor.matmul(bank[0][:, j * P:(j + 1) * P], y[:, h, j * P:(j + 1) * P],
                                                out_w[:, h, :], start=(h == 0), stop=(h == H - 1))
                last.then_inc(out_done, 1)

            def turn_xn2(t, n):
                pe.wait_ge(xn2_ready, t + 1)
                if n is not None:
                    pe.wait_ge(in_read, 4 * n + 3)
                else:
                    pe.wait_ge(placed, 9 * t)
                for j in range(TILES):
                    last = nc.tensor.transpose(bank[3][:, j * P:(j + 1) * P], row[:, j, 0:DM], ident)
                last.then_inc(xn2_turned, 1)

            def router(t):
                pe.wait_ge(xn2T_ready, t + 1)
                for j in range(TILES):
                    last = nc.tensor.matmul(bank[3][:, j * E:(j + 1) * E], xn2T[:, j * P:(j + 1) * P],
                                            const("w_r"), start=True, stop=True)
                last.then_inc(logit_done, 1)

            def ranks(t):
                pe.wait_ge(route, 7 * t + 6)
                hot = one_hot[:, :, :].rearrange("p j e -> p (j e)")
                nc.tensor.matmul(bank[3][:, RANKS:RANKS + (TILES + 1) * E], before, hot, start=True, stop=False,
                                 skip_group_check=True)
                for j in range(1, TILES + 1):
                    last = nc.tensor.matmul(bank[3][:, RANKS + j * E:RANKS + (TILES + 1) * E], ones,
                                            hot[:, 0:(TILES + 1 - j) * E], start=False, stop=(j == TILES),
                                            skip_group_check=True)
                last.then_inc(rank_done, 1)

            def difference(n, p, s, h):
                k = 32 * n + 2 * s + h
                if s % 4 == 0 and h == 0:
                    pe.wait_ge(delta_ready, 4 * n + s // 4 + 1)
                if s == 0 and h == 0:
                    pe.wait_ge(xcT_ready, 2 * n + 2)
                if not (isinstance(n, int) and k < 2):
                    pe.wait_ge(scanned, k - 1)
                for j in range(TILES):
                    w = BW if j < TILES - 1 else P
                    last = nc.tensor.matmul(dv[h][:, j * P:j * P + w], xcT[p][:, j, h * P:(h + 1) * P],
                                            delta[:, s, j, 0:w], start=(j == 0), stop=(j == TILES - 1),
                                            skip_group_check=True)
                last.then_inc(dv_ready, 1)

            def sum_states(n, s):
                if s in POOL_STATES:
                    pe.wait_ge(prod_pool, NP_ * n + pool_before(s + 1))
                else:
                    pe.wait_ge(prod_vec, NV * n + vec_before(s + 1))
                if s == 0 and not early(n):
                    pe.wait_ge(y_ready, n)
                for h in range(H):
                    nc.tensor.matmul(ysum[:, h, :], diag[:, h, s, :], prod[s % 2][:, h, :],
                                     start=(s == 0), stop=(s == S - 1), skip_group_check=True).then_inc(summed, 1)

            def body(b, p, first=False, last=False):
                n = None if last else b + 1
                t = None if first else b - 1
                for s in range(S):
                    difference(b, p, s, 0)
                    difference(b, p, s, 1)
                    if s >= 2:
                        sum_states(b, s - 2)
                    elif not first:
                        sum_states(b - 1, S + s - 2)
                    if n is not None and s == 2:
                        turn_xn(n)
                    if n is not None and s == 3:
                        in_proj(n, 0)
                        in_proj(n, 1)
                    if n is not None and s == 4:
                        in_proj(n, 2)
                        in_proj(n, 3)
                    if t is not None and s == 5:
                        out_proj(t, n)
                    if n is not None and s == 7:
                        x_projection(n)
                    if n is not None and s == 8:
                        dt_proj(n, t, 0)
                        dt_proj(n, t, 1)
                        turn_xdbl(n)
                    if t is not None and s == 9:
                        turn_xn2(t, n)
                    if n is not None and s == 9:
                        turn_xc(n, 0)
                    if n is not None and s == 10:
                        turn_xc(n, 1)
                        turn_bc(n)
                    if t is not None and s == 10:
                        router(t)
                    if n is not None and s == 12:
                        q_matmul(n, 0)
                        q_matmul(n, 1)
                    if t is not None and s == (11 if last else 13):
                        ranks(t)

            pe.wait_ge(s_pack, 16)
            turn_xn(0)
            for m in range(4):
                in_proj(0, m)
            x_projection(0)
            dt_proj(0, None, 0)
            dt_proj(0, None, 1)
            turn_xdbl(0)
            turn_xc(0, 0)
            turn_xc(0, 1)
            turn_bc(0)
            pe.wait_ge(setup, 9)
            q_matmul(0, 0)
            q_matmul(0, 1)
            body(0, 0, first=True)
            with pe.Fori(0, (NB - 2) // 2) as i:
                body(2 * i + 1, 1)
                body(2 * i + 2, 0)
            body(NB - 1, 1, last=True)

            def turn_row(k, c):
                i = FU * k + c
                pe.wait_ge(f_loaded[c], 16 * (k + 1))
                if starts(k, c, 2):
                    pe.wait_ge(skip_ready, 2 * NB)
                else:
                    pe.wait_ge(f_xT_ready, i - 1)
                nc.tensor.transpose(bank[1 + c % 2][:, 0:P], f_row[c][:, 0:DM], ident).then_inc(f_turned, 1)

            def hidden(k, c):
                i = FU * k + c
                pe.wait_ge(f_xT_ready, i + 1)
                pe.wait_ge(w1_taken, i + 1)
                if not starts(k, c, 2):
                    pe.wait_ge(gelu_done, i - 1)
                else:
                    pe.wait_ge(scanned, 32 * NB)
                for f in range(FK):
                    last = nc.tensor.matmul(dv[c % 2][:, f * P:(f + 1) * P], f_w1[c % 2][:, f * P:(f + 1) * P],
                                            f_xT[c % 4][:, :], start=True, stop=True)
                last.then_inc(hidden_done, 1)

            def mlp_out(k, c):
                i = FU * k + c
                pe.wait_ge(gelu_done, i + 1)
                pe.wait_ge(w2_taken, i + 1)
                if not starts(k, c, 2):
                    pe.wait_ge(combined, i - 1)
                else:
                    pe.wait_ge(y_ready, NB)
                to = ysum[:, c % 2, 0:DM]
                nc.tensor.matmul(to, ones[0:1, :], f_w2[c % 4][0:1, EW - FF - DM:], start=True, stop=False)
                for f in range(FK):
                    last = nc.tensor.matmul(to, f_h[c % 2][:, f * P:(f + 1) * P],
                                            f_w2[c % 4][:, f * DM:(f + 1) * DM], start=False, stop=(f == FK - 1))
                last.then_inc(mlp_done, 1)

            def tiles(k):
                for c in range(FU):
                    hidden(k, c)
                    if not starts(k, c, 1):
                        mlp_out(*ahead(k, c))
                    if not ends(k, c, 2):
                        turn_row(*after(k, c, 2))
                    if starts(k, c, FU):
                        if c == 1:
                            out_proj(NB - 1, None)
                        if c == 4:
                            turn_xn2(NB - 1, None)
                        if c == 5:
                            router(NB - 1)
                        if c == 6:
                            ranks(NB - 1)

            sum_states(NB - 1, S - 2)
            turn_row(0, 0)
            turn_row(0, 1)
            sum_states(NB - 1, S - 1)
            for k in range(EARLY // FU):
                tiles(k)
            with pe.Fori(EARLY // FU, FTILES // FU - 1) as k:
                tiles(k)
            tiles(FTILES // FU - 1)
            mlp_out(FTILES // FU - 1, FU - 1)

        @block.scalar
        def _(act):
            def copy_xnT(n):
                act.wait_ge(xn_turned, n + 1)
                if not early(n):
                    act.wait_ge(in_done, 4 * n)
                nc.scalar.activation(xnT[:, :], bank[0][:, :], ACT.Copy).then_inc(xnT_ready, 1)

            def read_in_proj(n, m):
                act.wait_ge(in_done, 4 * n + m + 1)
                if m == 0 and not early(n):
                    act.wait_ge(conv_step, 6 * n)
                if m == 2 and not early(n):
                    act.wait_ge(poly_step, 5 * n)
                frm = bank[(m + 1) % 4][:, :]
                if m < H:
                    if m == 0 and not early(n):
                        act.wait_ge(poly_step, 5 * n)
                    nc.scalar.activation(xpad[:, m, TAPS - 1:], frm, ACT.Identity, bias=b_in[:, m:m + 1])
                    if early(n) and m == 0:
                        act.wait_ge(setup, 5)
                    nc.scalar.activation(conv[:, m, :], frm, ACT.Identity, bias=conv_in[:, m:m + 1],
                                         scale=conv_w[:, m, TAPS - 1:]).then_inc(in_read, 1)
                else:
                    nc.scalar.activation(z_half[:, m - H, :], frm, ACT.Identity, bias=half_bin[:, m:m + 1],
                                         scale=0.5).then_inc(in_read, 1)

            def tanh_of_z(n):
                act.wait_ge(in_read, 4 * n + 4)
                if not early(n):
                    act.wait_ge(yexp_ready, n)
                nc.scalar.activation(tanh_z[:, :, :], z_half[:, :, :], ACT.Tanh).then_inc(tanhz_ready, 1)

            def tanh_of_conv(n):
                act.wait_ge(conv_step, 6 * n + 6)
                nc.scalar.activation(tanh_u[:, :, :], conv[:, :, :], ACT.Tanh).then_inc(tanhu_ready, 1)

            def copy_xdbl(n):
                act.wait_ge(xdbl_done, n + 1)
                if not early(n):
                    act.wait_ge(xdbl_turned, n)
                    act.wait_ge(c_stored, 16 * n)
                nc.scalar.activation(x_dbl[:, :], bank[1][0:R + 2 * S, :], ACT.Copy).then_inc(xdbl_ready, 1)

            def copy_xcT(n, p, part):
                act.wait_ge(xc_turned, 2 * n + part + 1)
                if part == 0 and not early(n, 2):
                    act.wait_ge(dv_ready, 32 * (n - 1))
                to = xcT[p][:, 2 * part:2 * part + 2, :].rearrange("p j d -> p (j d)")
                nc.scalar.activation(to, bank[2 * part][:, :], ACT.Copy).then_inc(xcT_ready, 1)

            def softplus_parts(n, h):
                act.wait_ge(dt_done, 2 * n + h + 1)
                if h == 0:
                    act.wait_ge(gate_ready, n + 1)
                    act.wait_ge(xc_ready, n + 1)
                nc.scalar.activation(abs_p[:, h, :], bank[2 * h][:, :], ACT.Abs, bias=dt_b[:, h:h + 1])
                nc.scalar.activation(relu_p[:, h, :], bank[2 * h][:, :], ACT.Relu,
                                     bias=dt_b[:, h:h + 1]).then_inc(dt_read, 1)

            def softplus_exp(n):
                act.wait_ge(dt_read, 2 * n + 2)
                nc.scalar.activation(y_exp[:, :, :], abs_p[:, :, :], ACT.Exp, scale=-1.0).then_inc(yexp_ready, 1)

            def softplus_square(n, i):
                if i == 0:
                    act.wait_ge(yexp_ready, n + 1)
                if not (isinstance(n, int) and n == 0 and i < 2):
                    act.wait_ge(poly_step, 5 * n + i - 1 if i >= 2 else 5 * n)
                qa = const("quad_a")[:, i:i + 1]
                nc.scalar.activation(square[i % 2][:, :, :], y_exp[:, :, :], ACT.Square,
                                     bias=qa).then_inc(square_ready, 1)

            def copy_bc(n):
                act.wait_ge(bc_turned, n + 1)
                if not early(n):
                    act.wait_ge(q_done, 2 * n)
                nc.scalar.activation(bc_s[:, :], bank[1][0:S, :], ACT.Copy).then_inc(bcs_ready, 1)

            def copy_xn2T(t):
                act.wait_ge(xn2_turned, t + 1)
                nc.scalar.activation(xn2T[:, :], bank[3][:, :], ACT.Copy).then_inc(xn2T_ready, 1)

            def exp_logits(t):
                act.wait_ge(route, 7 * t + 7)
                nc.scalar.activation(expd[:, :, :], shifted[:, :, :], ACT.Exp).then_inc(expd_ready, 1)

            def decay(n, p, s, h):
                k = 32 * n + 2 * s + h
                if s == 0 and h == 0:
                    act.wait_ge(poly_step, 5 * n + 5)
                if not (isinstance(n, int) and k < 4):
                    act.wait_ge(scanned, k - 3)
                at = h * S + s
                nc.scalar.activation(a_bar[(2 * s + h) % 4][:, :], dt[p][:, h, :], ACT.Exp,
                                     scale=neg_a[:, at:at + 1]).then_inc(abar_ready, 1)

            def body(b, p, first=False, last=False):
                n = None if last else b + 1
                t = None if first else b - 1
                for s in range(S):
                    decay(b, p, s, 0)
                    decay(b, p, s, 1)
                    if n is not None and s == 2:
                        copy_xnT(n)
                    if n is not None and s == 3:
                        read_in_proj(n, 0)
                        read_in_proj(n, 1)
                    if n is not None and s == 4:
                        read_in_proj(n, 2)
                        read_in_proj(n, 3)
                        tanh_of_z(n)
                    if n is not None and s == 6:
                        tanh_of_conv(n)
                    if n is not None and s == 7:
                        copy_xdbl(n)
                    if n is not None and s == 8:
                        softplus_parts(n, 0)
                        softplus_parts(n, 1)
                    if t is not None and s == 9:
                        copy_xn2T(t)
                    if n is not None and s == 9:
                        copy_xcT(n, 1 - p, 0)
                        softplus_exp(n)
                    if n is not None and s == 10:
                        copy_xcT(n, 1 - p, 1)
                        softplus_square(n, 0)
                        softplus_square(n, 1)
                    if n is not None and s == 11:
                        copy_bc(n)
                        softplus_square(n, 2)
                    if t is not None and s == (11 if last else 12):
                        exp_logits(t)
                    if n is not None and s == 12:
                        softplus_square(n, 3)

            act.wait_ge(s_pack, 16)
            nc.scalar.activation(neg_a[:, :], const("a_log"), ACT.Exp)
            nc.scalar.activation(inv_a_s[:, :], a_log_s, ACT.Exp).then_inc(setup_a, 1)
            copy_xnT(0)
            for m in range(2):
                read_in_proj(0, m)
            act.wait_ge(setup, 4)
            for m in range(2, 4):
                read_in_proj(0, m)
            tanh_of_z(0)
            tanh_of_conv(0)
            copy_xdbl(0)
            softplus_parts(0, 0)
            softplus_parts(0, 1)
            copy_xcT(0, 0, 0)
            copy_xcT(0, 0, 1)
            softplus_exp(0)
            softplus_square(0, 0)
            softplus_square(0, 1)
            copy_bc(0)
            softplus_square(0, 2)
            softplus_square(0, 3)
            act.wait_ge(setup, 9)
            body(0, 0, first=True)
            with act.Fori(0, (NB - 2) // 2) as i:
                body(2 * i + 1, 1)
                body(2 * i + 2, 0)
            body(NB - 1, 1, last=True)

            def gelu(k, c):
                i = FU * k + c
                act.wait_ge(hidden_done, i + 1)
                act.wait_ge(w2_taken, i + 1)
                if not starts(k, c, 2):
                    act.wait_ge(mlp_done, i - 1)
                for f in range(FK):
                    at = FK * DM + f
                    last = nc.scalar.activation(f_h[c % 2][:, f * P:(f + 1) * P], dv[c % 2][:, f * P:(f + 1) * P],
                                                ACT.Gelu, bias=f_w2[c % 4][:, at:at + 1])
                last.then_inc(gelu_done, 1)

            def tiles(k):
                for c in range(FU):
                    if starts(k, c, FU):
                        if c == 5:
                            copy_xn2T(NB - 1)
                        if c == 7:
                            exp_logits(NB - 1)
                    if isinstance(k, int) and k == 1 and c == 1:
                        act.wait_ge(ends_ready, 1)
                        for e in range(E // 2, E):
                            at = act.value_load(filled_i[0:1, e:e + 1], min_val=e * REGION,
                                                max_val=e * REGION + TOK)
                            act.dma_start(rows_d[bass.ds(at, P), :], pad[:, :]).then_inc(padded, 16)
                    gelu(k, c)

            for k in range(EARLY // FU):
                tiles(k)
            with act.Fori(EARLY // FU, FTILES // FU - 1) as k:
                tiles(k)
            tiles(FTILES // FU - 1)

        @block.vector
        def _(dve):
            def statistics(n, p):
                dve.wait_ge(x_loaded, 16 * (n + 1))
                for j in range(TILES):
                    last = nc.vector.bn_stats(stat1[:, j, :], x_in[p][:, j, :])
                last.then_inc(stats1, 1)
                dve.wait_ge(stats1, n + 1)
                dve.sem_inc(wait_carrier)
                for j in range(TILES):
                    last = nc.vector.bn_aggr(mv1[:, j, :], stat1[:, j, :])
                last.then_inc(mv1_ready, 1)

            def normalise(n, p):
                dve.wait_ge(rstd1_ready, n + 1)
                if not early(n):
                    dve.wait_ge(xn_turned, n)
                for j in range(TILES):
                    last = nc.vector.tensor_scalar(xn[:, j, :], x_in[p][:, j, :], mv1[:, j, 0:1],
                                                   rstd1[:, j:j + 1], ALU.subtract, ALU.mult)
                last.then_inc(xn_ready, 1)

            def convolve(n, m):
                tap, h = m // H, m % H
                if m == 0:
                    dve.wait_ge(in_read, 4 * n + 2)
                elif tap > 0:
                    dve.wait_ge(conv_step, 6 * n + m - 1)
                nc.vector.scalar_tensor_tensor(conv[:, h, :], xpad[:, h, tap:tap + L],
                                               conv_w[:, h, tap:tap + 1], conv[:, h, :],
                                               ALU.mult, ALU.add).then_inc(conv_step, 1)

            def silu_z(n, p):
                dve.wait_ge(tanhz_ready, n + 1)
                if not early(n, 2):
                    dve.wait_ge(yg_ready, n - 1)
                nc.vector.scalar_tensor_tensor(gate_z[p][:, :, :], tanh_z[:, :, :], 1.0, z_half[:, :, :],
                                               ALU.add, ALU.mult).then_inc(gate_ready, 1)

            def silu_conv(n):
                dve.wait_ge(tanhu_ready, n + 1)
                if not early(n):
                    dve.wait_ge(xc_turned, 2 * n)
                    dve.wait_ge(skip_ready, 2 * n)
                nc.vector.scalar_tensor_tensor(xc[:, :, :], tanh_u[:, :, :], 1.0, conv[:, :, :],
                                               ALU.add, ALU.mult).then_inc(xc_ready, 1)

            def copy_bcT(n):
                dve.wait_ge(xdbl_turned, n + 1)
                if not early(n):
                    dve.wait_ge(delta_ready, 4 * n)
                frm = bank[1][:, 0:TILES * 96].rearrange("p (j c) -> p j c", j=TILES)[:, :, R:]
                nc.vector.tensor_copy(bc_T[:, :, :], frm).then_inc(bcT_ready, 1)
                dve.wait_ge(bcT_ready, n + 1)
                if not early(n):
                    dve.wait_ge(bc_turned, n)
                nc.vector.tensor_tensor(bc_mul[:, :, :], bc_T[:, :, 0:S], bc_T[:, :, S:],
                                        ALU.mult).then_inc(bcmul_ready, 1)

            def skip_term(n, p, h):
                dve.wait_ge(q_done, 2 * n + h + 1)
                if not early(n, 2):
                    dve.wait_ge(y_ready, n - 1)
                nc.vector.scalar_tensor_tensor(skip[p][:, h, :], bank[2 * h][:, :], neg_d[:, h:h + 1],
                                               xc[:, h, :], ALU.add, ALU.mult).then_inc(skip_ready, 1)

            def softplus_poly(n, p, i):
                if i < 4:
                    dve.wait_ge(square_ready, 4 * n + i + 1)
                if i == 0:
                    nc.vector.scalar_tensor_tensor(poly[:, :, :], square[0][:, :, :], QUAD_B[0], y_exp[:, :, :],
                                                   ALU.add, ALU.mult).then_inc(poly_step, 1)
                elif i < 4:
                    dve.wait_ge(poly_step, 5 * n + i)
                    nc.vector.scalar_tensor_tensor(poly[:, :, :], square[i % 2][:, :, :], QUAD_B[i], poly[:, :, :],
                                                   ALU.add, ALU.mult).then_inc(poly_step, 1)
                else:
                    dve.wait_ge(poly_step, 5 * n + i)
                    if not early(n, 2):
                        dve.wait_ge(abar_ready, 32 * (n - 1))
                    nc.vector.scalar_tensor_tensor(dt[p][:, :, :], poly[:, :, :], LEAD, relu_p[:, :, :],
                                                   ALU.mult, ALU.add).then_inc(poly_step, 1)

            def scan(n, s, h):
                k = 32 * n + 2 * s + h
                dve.wait_ge(dv_ready, k + 1)
                dve.wait_ge(abar_ready, k + 1)
                if h == 0:
                    m, before_s = (n, s - 2) if s >= 2 else (n - 1, S + s - 2)
                    if not (isinstance(m, int) and m < 0):
                        if before_s in POOL_STATES:
                            dve.wait_ge(prod_pool, NP_ * m + pool_before(before_s + 1))
                        else:
                            dve.wait_ge(prod_vec, NV * m + vec_before(before_s + 1))
                nc.vector.tensor_tensor_scan(k_st[s % 2][:, h, :], dv[h][:, :], a_bar[(2 * s + h) % 4][:, :], 0.0,
                                             ALU.add, ALU.mult).then_inc(scanned, 1)

            def times_c(n, s):
                dve.wait_ge(scanned, 32 * n + 2 * s + 2)
                if s % 4 == 0:
                    dve.wait_ge(c_loaded[s // 4], 16 * (n + 1))
                if not (isinstance(n, int) and 32 * n + 2 * s < 4):
                    dve.wait_ge(summed, 32 * n + 2 * s - 2)
                nc.vector.tensor_tensor(prod[s % 2][:, :, :], k_st[s % 2][:, :, :],
                                        c_all[:, s:s + 1, :].to_broadcast([P, H, L]),
                                        ALU.mult).then_inc(prod_vec, 1)

            def finish_y(t, p):
                dve.wait_ge(summed, 32 * t + 32)
                nc.vector.tensor_tensor(y[:, :, :], ysum[:, :, :], skip[p][:, :, :],
                                        ALU.subtract).then_inc(y_ready, 1)

            def residual(t):
                dve.wait_ge(out_done, t + 1)
                dve.wait_ge(res_ready, t + 1)
                dve.wait_ge(scattered, 64 * t + 16)
                nc.vector.tensor_tensor(row[:, :, DM:2 * DM], bank[0][:, :].rearrange("p (j d) -> p j d", j=TILES),
                                        x_res[:, :, :], ALU.add).then_inc(x1_ready, 1)

            def residual_moments(t):
                dve.wait_ge(x1_ready, t + 1)
                for j in range(TILES):
                    last = nc.vector.bn_stats(stat2[:, j, :], row[:, j, DM:2 * DM])
                last.then_inc(stats2, 1)
                dve.wait_ge(stats2, t + 1)
                dve.sem_inc(wait_carrier)
                for j in range(TILES):
                    last = nc.vector.bn_aggr(mv2[:, j, :], stat2[:, j, :])
                last.then_inc(mv2_ready, 1)

            def normalise2(t):
                dve.wait_ge(rstd2_ready, t + 1)
                for j in range(TILES):
                    last = nc.vector.tensor_scalar(row[:, j, 0:DM], row[:, j, DM:2 * DM], mv2[:, j, 0:1],
                                                   rstd2[:, j:j + 1], ALU.subtract, ALU.mult)
                last.then_inc(xn2_ready, 1)

            def choose(t):
                def spread(v):
                    return v.unsqueeze(1).to_broadcast([P, TILES, E])

                def along(v):
                    return v.unsqueeze(2).to_broadcast([P, TILES, E])

                dve.wait_ge(logit_done, t + 1)
                nc.vector.tensor_tensor(logit[:, :, :], bank[3][:, 0:TILES * E].rearrange("p (j e) -> p j e", j=TILES),
                                        spread(const("b_r")), ALU.add).then_inc(route, 1)
                dve.wait_ge(route, 7 * t + 1)
                nc.vector.tensor_reduce(top[:, :], logit[:, :, :], AX.X, ALU.max).then_inc(route, 1)
                dve.wait_ge(route, 7 * t + 2)
                nc.vector.tensor_tensor(is_top[:, :, :], logit[:, :, :], along(top[:, :]),
                                        ALU.is_equal).then_inc(route, 1)
                dve.wait_ge(route, 7 * t + 3)
                nc.vector.scalar_tensor_tensor(cand[:, :, :], is_top[:, :, :], -float(E), spread(const("expert_no8")),
                                               ALU.mult, ALU.add).then_inc(route, 1)
                dve.wait_ge(route, 7 * t + 4)
                nc.vector.tensor_reduce(chosen[:, :], cand[:, :, :], AX.X, ALU.min).then_inc(route, 1)
                dve.wait_ge(route, 7 * t + 5)
                nc.vector.tensor_tensor(one_hot[:, 0:TILES, :], spread(const("expert_no")), along(chosen[:, :]),
                                        ALU.is_equal).then_inc(route, 1)
                nc.vector.tensor_tensor(shifted[:, :, :], logit[:, :, :], along(top[:, :]),
                                        ALU.subtract).then_inc(route, 1)

            def place(t):
                dve.wait_ge(rank_done, t + 1)
                nc.vector.tensor_tensor(slot_e[:, :, :],
                                        bank[3][:, RANKS:RANKS + TILES * E].rearrange("p (j e) -> p j e", j=TILES),
                                        filled[:, :].unsqueeze(1).to_broadcast([P, TILES, E]), ALU.add).then_inc(placed, 1)
                dve.wait_ge(placed, 9 * t + 1)
                nc.vector.tensor_tensor(filled[:, :], bank[3][:, RANKS + TILES * E:RANKS + (TILES + 1) * E], filled[:, :], ALU.add).then_inc(placed, 1)
                nc.vector.tensor_tensor(slot_m[:, :, :], slot_e[:, :, :], one_hot[:, 0:TILES, :], ALU.mult).then_inc(placed, 1)
                dve.wait_ge(placed, 9 * t + 3)
                nc.vector.tensor_reduce(slot[:, :], slot_m[:, :, :], AX.X, ALU.add).then_inc(placed, 1)
                dve.wait_ge(placed, 9 * t + 4)
                nc.vector.tensor_copy(slot_i[:, :], slot[:, :]).then_inc(placed, 1)
                dve.wait_ge(expd_ready, t + 1)
                nc.vector.tensor_reduce(zsum[:, :], expd[:, :, :], AX.X, ALU.add).then_inc(placed, 1)
                dve.wait_ge(placed, 9 * t + 6)
                nc.vector.reciprocal(row[:, :, 2 * DM], zsum[:, :]).then_inc(placed, 1)
                nc.vector.tensor_copy(row[:, :, :].bitcast(I32)[:, :, 2 * DM + 1], token[:, :]).then_inc(placed, 1)
                dve.wait_ge(placed, 9 * t + 8)
                nc.vector.tensor_scalar(token[:, :], token[:, :], float(L), None, ALU.add).then_inc(placed, 1)

            def make_plan(stage):
                done = 10 * stage
                tiles = (0, EARLY) if stage == 0 else (EARLY, FTILES)
                m = tiles[1] - tiles[0]
                passed, passed_j = passed_all[:, 0:m, :], passed_jump[:, 0:m, :]
                tile_no = const("tile_no")[0:1, 0:m]

                def link(steps_done):
                    dve.wait_ge(planned, done + steps_done)

                dve.wait_ge(placed, 9 * (NB - 1 + stage))
                if stage == 0:
                    nc.vector.memset(taken[:, :], 0.0).then_inc(planned, 1)
                    nc.vector.scalar_tensor_tensor(count[:, :], filled[0:1, :], float(P - 1), const("region_at")[0:1, :],
                                                   ALU.subtract, ALU.subtract).then_inc(planned, 1)
                else:
                    nc.vector.tensor_tensor(count[:, :], filled[0:1, :], const("region_at")[0:1, :],
                                            ALU.subtract).then_inc(planned, 1)
                    link(1)
                    nc.vector.scalar_tensor_tensor(count[:, :], taken[:, 0:E], -float(P), count[:, :],
                                                   ALU.mult, ALU.add).then_inc(planned, 1)
                link(2)
                nc.vector.tensor_tensor(full[:, :, :], count[:, :].unsqueeze(2).to_broadcast([1, E, TOK // P]),
                                        const("tile_at")[0:1, :].unsqueeze(1).to_broadcast([1, E, TOK // P]),
                                        ALU.is_gt).then_inc(planned, 1)
                link(3)
                nc.vector.tensor_reduce(n_tiles[:, :], full[:, :, :], AX.X, ALU.add).then_inc(planned, 1)
                link(4)
                nc.vector.tensor_tensor(jump[:, :], taken[:, 1:E + 1], taken[:, 0:E], ALU.subtract)
                nc.vector.tensor_tensor_scan(end_tile[:, :], n_tiles[:, :], zero8[:, :], 0.0, ALU.add,
                                             ALU.add).then_inc(planned, 1)
                link(5)
                nc.vector.tensor_tensor(jump[:, :], jump[:, :], n_tiles[:, :], ALU.subtract)
                nc.vector.tensor_tensor(passed, end_tile[:, :].unsqueeze(1).to_broadcast([1, m, E]),
                                        tile_no.unsqueeze(2).to_broadcast([1, m, E]), ALU.is_le).then_inc(planned, 1)
                link(6)
                nc.vector.tensor_reduce(t_exp[:, 0:m], passed, AX.X, ALU.add)
                nc.vector.tensor_tensor(passed_j, passed, jump[:, :].unsqueeze(1).to_broadcast([1, m, E]),
                                        ALU.mult).then_inc(planned, 1)
                link(7)
                nc.vector.tensor_reduce(t_off[:, 0:m], passed_j, AX.X, ALU.add)
                nc.vector.tensor_scalar(t_exp_i[:, tiles[0]:tiles[1]], t_exp[:, 0:m], float(E - 1), None, ALU.min)
                nc.vector.tensor_scalar(t_row[:, 0:m], t_exp[:, 0:m], float(REGION), None, ALU.mult).then_inc(planned, 1)
                link(8)
                nc.vector.scalar_tensor_tensor(t_off[:, 0:m], tile_no, taken[:, 0:1], t_off[:, 0:m], ALU.add,
                                               ALU.add).then_inc(planned, 1)
                link(9)
                nc.vector.scalar_tensor_tensor(t_row_i[:, tiles[0]:tiles[1]], t_off[:, 0:m], float(P), t_row[:, 0:m],
                                               ALU.mult, ALU.add).then_inc(planned, 1)
                link(10)

            def expert_ends():
                dve.wait_ge(placed, 9 * NB)
                nc.vector.tensor_copy(filled_i[:, :], filled[0:1, :]).then_inc(ends_ready, 1)

            def gate_last():
                dve.wait_ge(y_ready, NB)
                nc.vector.tensor_tensor(y[:, :, :], y[:, :, :], gate_z[1][:, :, :], ALU.mult).then_inc(yg_ready, 1)

            def count_taken():
                nc.vector.tensor_scalar(taken[:, 0:E], end_tile[:, :], float(EARLY), None, ALU.min).then_inc(early_ends, 1)
                dve.wait_ge(early_ends, 1)
                nc.vector.tensor_copy(end_tile[:, :], taken[:, 0:E]).then_inc(early_ends, 1)
                dve.wait_ge(early_ends, 2)
                nc.vector.tensor_tensor(taken[:, 1:E], end_tile[:, 1:E], end_tile[:, 0:E - 1],
                                        ALU.subtract).then_inc(early_ends, 1)
                dve.wait_ge(early_ends, 3)

            def body(b, p, first=False, last=False):
                n = None if last else b + 1
                t = None if first else b - 1
                q = 1 - p
                for s in range(S):
                    if s == 0 and t is not None:
                        times_c(b - 1, S - 1)
                    scan(b, s, 0)
                    if s >= 1 and s - 1 in VEC_STATES:
                        times_c(b, s - 1)
                    if n is not None and s == 1:
                        normalise(n, q)
                    if n is not None and s in (4, 5):
                        convolve(n, 3 * s - 12)
                        convolve(n, 3 * s - 11)
                    if t is not None and s == 6:
                        residual(t)
                    if t is not None and s == 7:
                        residual_moments(t)
                    if n is not None and s == 9:
                        copy_bcT(n)
                    if n is not None and s == 11:
                        softplus_poly(n, q, 0)
                    if t is not None and not last and s == 12:
                        choose(t)
                    if n is not None and s == 13:
                        softplus_poly(n, q, 3)
                    if t is not None and not last and s == 14:
                        place(t)
                    if last and s == 11:
                        choose(t)
                    if last and s == 12:
                        place(t)
                    if last and s == 13:
                        make_plan(0)
                    if last and s == 14:
                        count_taken()
                    if n is not None and s == 15:
                        skip_term(n, q, 1)
                    scan(b, s, 1)
                    if n is not None and s == 0:
                        statistics(n, q)
                    if t is not None and s == 1:
                        finish_y(t, q)
                    if n is not None and s in (4, 5):
                        convolve(n, 3 * s - 10)
                    if n is not None and s == 6:
                        silu_conv(n)
                    if n is not None and s == 7:
                        silu_z(n, q)
                    if t is not None and s == 8:
                        normalise2(t)
                    if n is not None and s == 11:
                        softplus_poly(n, q, 1)
                    if n is not None and s == 12:
                        softplus_poly(n, q, 2)
                    if n is not None and s == 13:
                        softplus_poly(n, q, 4)
                    if n is not None and s == 14:
                        skip_term(n, q, 0)

            nc.vector.memset(xpad[:, :, 0:TAPS - 1], 0.0)
            nc.vector.memset(zero8[:, :], 0.0)
            nc.vector.memset(one_hot[:, TILES, :], 0.0)
            dve.wait_ge(s_pack, 16)
            nc.vector.tensor_copy(filled[:, :], const("region_at"))
            nc.vector.tensor_copy(token[:, :], const("token")).then_inc(setup, 1)
            statistics(0, 0)
            normalise(0, 0)
            nc.vector.tensor_scalar(half_bin[:, :], b_in, 0.5, None, ALU.mult).then_inc(setup, 1)
            nc.vector.tensor_scalar(const("conv_w"), const("conv_w"), 0.5, None, ALU.mult).then_inc(setup, 1)
            nc.vector.tensor_scalar(conv_b, conv_b, 0.5, None, ALU.mult).then_inc(setup, 1)
            dve.wait_ge(setup, 4)
            for h in range(H):
                last = nc.vector.scalar_tensor_tensor(conv_in[:, h:h + 1], b_in[:, h:h + 1], conv_w[:, h, TAPS - 1:],
                                                      conv_b[:, h:h + 1], ALU.mult, ALU.add)
            last.then_inc(setup, 1)
            for m in range(6):
                convolve(0, m)
            silu_z(0, 0)
            silu_conv(0)
            dve.wait_ge(setup_a, 1)
            nc.vector.tensor_scalar(tiny_a[:, :], neg_a[:, :], 1e-6, None, ALU.is_lt)
            nc.vector.tensor_scalar(tiny_s[:, :], inv_a_s[:, :], 1e-6, None, ALU.is_lt)
            nc.vector.tensor_scalar(neg_d[:, :], d_skip, -1.0, None, ALU.mult).then_inc(setup, 1)
            dve.wait_ge(setup, 6)
            nc.vector.scalar_tensor_tensor(inv_a[:, :], tiny_a[:, :], 1.0, neg_a[:, :], ALU.subtract, ALU.mult)
            nc.vector.scalar_tensor_tensor(inv_a_s[:, :], tiny_s[:, :], 1.0, inv_a_s[:, :],
                                           ALU.subtract, ALU.mult).then_inc(setup, 1)
            dve.wait_ge(setup, 7)
            nc.vector.tensor_tensor(inv_a[:, :], inv_a[:, :], tiny_a[:, :], ALU.add)
            nc.vector.tensor_scalar(neg_a[:, :], neg_a[:, :], -1.0, None, ALU.mult)
            nc.vector.tensor_tensor(inv_a_s[:, :], inv_a_s[:, :], tiny_s[:, :], ALU.add).then_inc(setup, 1)
            dve.wait_ge(setup, 8)
            nc.vector.reciprocal(inv_a[:, :], inv_a[:, :])
            nc.vector.reciprocal(inv_a_s[:, :], inv_a_s[:, :]).then_inc(setup, 1)
            copy_bcT(0)
            softplus_poly(0, 0, 0)
            softplus_poly(0, 0, 1)
            skip_term(0, 0, 0)
            skip_term(0, 0, 1)
            for i in range(2, 5):
                softplus_poly(0, 0, i)
            dve.wait_ge(setup, 9)
            for h in range(H):
                for s in range(S):
                    at = h * S + s
                    last = nc.vector.tensor_scalar(diag[:, h, s, :], ident, inv_a[:, at:at + 1], None, ALU.mult)
            last.then_inc(setup, 1)
            body(0, 0, first=True)
            with dve.Fori(0, (NB - 2) // 2) as i:
                body(2 * i + 1, 1)
                body(2 * i + 2, 0)
            body(NB - 1, 1, last=True)

            def take_weights(k, c):
                i = FU * k + c
                e = dve.value_load(t_exp_i[0:1, bass.ds(i, 1)], min_val=0, max_val=E - 1)
                if not starts(k, c, 2):
                    dve.wait_ge(hidden_done, i - 1)
                nc.vector.tensor_copy(f_w1[c % 2][:, :], w_all[:, bass.ds(e, 1), 0:FF].squeeze(1)).then_inc(w1_taken, 1)
                if not starts(k, c, 4):
                    dve.wait_ge(mlp_done, i - 3)
                nc.vector.tensor_copy(f_w2[c % 4][:, :], w_all[:, bass.ds(e, 1), FF:].squeeze(1)).then_inc(w2_taken, 1)

            def take_xT(k, c):
                i = FU * k + c
                dve.wait_ge(f_turned, i + 1)
                if not starts(k, c, 4):
                    dve.wait_ge(hidden_done, i - 3)
                nc.vector.tensor_copy(f_xT[c % 4][:, :], bank[1 + c % 2][:, 0:P]).then_inc(f_xT_ready, 1)

            def combine(k, c):
                i = FU * k + c
                dve.wait_ge(mlp_done, i + 1)
                nc.vector.scalar_tensor_tensor(f_out[c], ysum[:, c % 2, 0:DM], f_row[c][:, 2 * DM:2 * DM + 1],
                                               f_row[c][:, DM:2 * DM], ALU.mult, ALU.add).then_inc(combined, 1)

            def tiles(k):
                for c in range(FU):
                    if starts(k, c, FU) and c == 4:
                        normalise2(NB - 1)
                    if starts(k, c, FU) and c == 6:
                        choose(NB - 1)
                    if not starts(k, c, 1):
                        combine(*ahead(k, c))
                    if not ends(k, c, 2):
                        take_weights(*after(k, c, 2))
                        take_xT(*after(k, c, 2))
                    if starts(k, c, FU) and c == 1:
                        residual(NB - 1)
                        residual_moments(NB - 1)
                    if starts(k, c, FU) and c == 6:
                        place(NB - 1)
                        expert_ends()
                    if starts(k, c, FU + 1) and not starts(k, c, FU):
                        make_plan(1)

            times_c(NB - 1, S - 1)
            dve.wait_ge(w_loaded, 16 * E)
            take_weights(0, 0)
            take_xT(0, 0)
            take_weights(0, 1)
            take_xT(0, 1)
            finish_y(NB - 1, 1)
            gate_last()
            for k in range(EARLY // FU):
                tiles(k)
            with dve.Fori(EARLY // FU, FTILES // FU - 1) as k:
                tiles(k)
            tiles(FTILES // FU - 1)
            combine(FTILES // FU - 1, FU - 1)

        @block.gpsimd
        def _(pool):
            def rstd(n):
                pool.wait_ge(mv1_ready, n + 1)
                nc.gpsimd.tensor_tensor(var1[:, :], mv1[:, :, 1], const("eps"), ALU.add).then_inc(var1_ready, 1)
                pool.wait_ge(var1_ready, n + 1)
                if not early(n):
                    pool.wait_ge(xn_ready, n)
                nc.gpsimd.tensor_tensor(rstd1[:, :], var1[:, :], const("minus_half"), ALU.pow).then_inc(rstd1_ready, 1)

            def rstd_2(t):
                pool.wait_ge(mv2_ready, t + 1)
                nc.gpsimd.tensor_tensor(var2[:, :], mv2[:, :, 1], const("eps"), ALU.add).then_inc(var2_ready, 1)
                pool.wait_ge(var2_ready, t + 1)
                nc.gpsimd.tensor_tensor(rstd2[:, :], var2[:, :], const("minus_half"), ALU.pow).then_inc(rstd2_ready, 1)

            def build_delta(n, g):
                pool.wait_ge(bcT_ready, n + 1)
                if not early(n):
                    pool.wait_ge(dv_ready, 32 * (n - 1) + 8 * g + 8)
                b_col = bc_T[:, :, 4 * g:4 * g + 4].rearrange("p j s -> p s j")
                nc.gpsimd.tensor_tensor(delta[:, 4 * g:4 * g + 4, :, :],
                                        bidiag.unsqueeze(1).unsqueeze(1).to_broadcast([P, 4, TILES, BW]),
                                        b_col.unsqueeze(3).to_broadcast([P, 4, TILES, BW]),
                                        ALU.mult).then_inc(delta_ready, 1)

            def times_c(n, s):
                pool.wait_ge(scanned, 32 * n + 2 * s + 2)
                pool.wait_ge(c_loaded[s // 4], 16 * (n + 1))
                if not (isinstance(n, int) and 32 * n + 2 * s < 4):
                    pool.wait_ge(summed, 32 * n + 2 * s - 2)
                nc.gpsimd.tensor_tensor(prod[s % 2][:, :, :], k_st[s % 2][:, :, :],
                                        c_all[:, s:s + 1, :].to_broadcast([P, H, L]), ALU.mult).then_inc(prod_pool, 1)

            def times_gate(t, p):
                pool.wait_ge(y_ready, t + 1)
                pool.wait_ge(gate_ready, t + 1)
                nc.gpsimd.tensor_tensor(y[:, :, :], y[:, :, :], gate_z[p][:, :, :], ALU.mult).then_inc(yg_ready, 1)

            def residual_bias(t):
                pool.wait_ge(res_loaded, 16 * (t + 1))
                nc.gpsimd.tensor_tensor(x_res[:, :, :], x_res[:, :, :],
                                        const("out_b").unsqueeze(1).to_broadcast([P, TILES, DM]),
                                        ALU.add).then_inc(res_ready, 1)

            def scatter(t):
                pool.wait_ge(placed, 9 * t + 8)
                pool.wait_ge(xn2_ready, t + 1)
                pool.sem_inc(wait_carrier)
                for j in range(TILES):
                    nc.gpsimd.indirect_dma_start(rows_d, bass.IndirectOffsetOnAxis(ap=slot_i[:, j:j + 1], axis=0),
                                                 row[:, j, :], None, bounds_check=ROWS - 1,
                                                 oob_is_err=False).then_inc(scattered, 16)

            def body(b, p, first=False, last=False):
                n = None if last else b + 1
                t = None if first else b - 1
                for s in range(S):
                    if s >= 1 and s - 1 in POOL_STATES:
                        times_c(b, s - 1)
                    if n is not None and s == 1:
                        rstd(n)
                    if t is not None and s == 2:
                        times_gate(t, 1 - p)
                        residual_bias(t)
                    if t is not None and s == 4:
                        build_delta(b, 3)
                    if t is not None and s == 8:
                        rstd_2(t)
                    if n is not None and s in (10, 12, 13):
                        build_delta(n, (10, 12, 13).index(s))
                    if t is not None and s == (13 if last else 15):
                        scatter(t)

            nc.gpsimd.memset(pad[:, :], 0.0).then_inc(pad_zero, 1)
            pool.wait_ge(pad_zero, 1)
            nc.gpsimd.memset(pad[:, :].bitcast(I32)[:, 2 * DM + 1:], NO_TOKEN).then_inc(s_pad_ready, 1)
            pool.wait_ge(s_pad_ready, 1)
            pool.dma_start(rows_d[E * REGION:ROWS, :].rearrange("(c q) w -> q c w", q=P),
                           pad[:, :].unsqueeze(1).to_broadcast([P, (ROWS - E * REGION) // P, RW])).then_inc(scattered, 16)
            pool.wait_ge(s_pack, 16)
            rstd(0)
            for g in range(4):
                build_delta(0, g)
            body(0, 0, first=True)
            with pool.Fori(0, (NB - 2) // 2) as i:
                body(2 * i + 1, 1)
                body(2 * i + 2, 0)
            body(NB - 1, 1, last=True)
            residual_bias(NB - 1)

            def store_rows(k, c):
                pool.wait_ge(combined, FU * k + c + 1)
                pool.sem_inc(wait_carrier)
                nc.gpsimd.indirect_dma_start(
                    out_d, bass.IndirectOffsetOnAxis(ap=f_row[c][:, :].bitcast(I32)[:, 2 * DM + 1:], axis=0),
                    f_out[c], None, bounds_check=TOK - 1, oob_is_err=False).then_inc(f_stored[c], 16)

            def tiles(k):
                for c in range(FU):
                    if starts(k, c, FU) and c == 1:
                        rstd_2(NB - 1)
                    if starts(k, c, FU) and c == 6:
                        scatter(NB - 1)
                    store_rows(k, c)

            for k in range(EARLY // FU):
                tiles(k)
            with pool.Fori(EARLY // FU, FTILES // FU) as k:
                tiles(k)
            for c in range(FU):
                pool.wait_ge(f_stored[c], 16 * (FTILES // FU))


def packed(a):
    f = np.float32
    pack = np.zeros((P, PACK_W), f)

    def put(name, v):
        v = np.asarray(v, f)
        pack[:v.shape[0], AT[name][0]:AT[name][1]] = v

    def rows(v):
        return np.broadcast_to(np.asarray(v, f), (P, len(v)))

    def halves(v):
        return np.swapaxes(v.reshape((-1, P) + v.shape[1:]), 0, 1).reshape(P, -1)

    put("ident", np.eye(P))
    put("bidiag", np.eye(P, BW) - np.eye(P, BW, 1))
    put("before", np.triu(np.ones((P, P)), 1))
    put("ones", np.ones((P, P)))
    put("expert_no", rows(range(E)))
    put("expert_no8", rows(range(E, 2 * E)))
    put("region_at", rows([e * REGION for e in range(E)]))
    put("token", np.arange(TILES)[None, :] * P + np.arange(P)[:, None])
    put("quad_a", rows(QUAD_A))
    put("minus_half", np.full((P, TILES), -0.5))
    put("eps", np.full((P, TILES), EPS))
    put("tile_at", rows([P * j for j in range(TOK // P)]))
    put("tile_no", rows(range(FTILES)))
    put("w_in", a["L0_attn_in_proj_w"].T)
    put("b_in", halves(a["L0_attn_in_proj_b"]))
    put("conv_w", halves(a["L0_attn_conv_w"]))
    put("conv_b", halves(a["L0_attn_conv_b"]))
    put("a_log", halves(a["L0_attn_A_log"].T))
    put("d_skip", halves(a["L0_attn_D"]))
    put("x_proj", halves(a["L0_attn_x_proj_w"].T))
    put("dt_w", a["L0_attn_dt_proj_w"].T)
    put("dt_b", halves(a["L0_attn_dt_proj_b"]))
    put("a_log_s", a["L0_attn_A_log"])
    put("out_w", halves(a["L0_attn_out_proj_w"].T))
    put("out_b", rows(a["L0_attn_out_proj_b"]))
    put("w_r", a["L0_ffn_Wr"])
    put("b_r", rows(a["L0_ffn_br"]))
    return pack


def kernel(**inputs):
    import concourse.bacc as bacc
    from concourse.bass_utils import run_bass_kernel_spmd

    a = {k: np.asarray(v) for k, v in inputs.items()}
    experts = np.zeros((E, P, EW), np.float32)
    experts[:, :, 0:FF] = a["L0_ffn_W1"]
    experts[:, :, FF:FF + FK * DM] = a["L0_ffn_W2"].reshape(E, FK, P, DM).transpose(0, 2, 1, 3).reshape(E, P, FK * DM)
    experts[:, :, FF + FK * DM:FF + FK * DM + FK] = a["L0_ffn_b1"].reshape(E, FK, P).transpose(0, 2, 1)
    experts[:, 0, EW - DM:] = a["L0_ffn_b2"]
    arrays = {"x_d": np.ascontiguousarray(a["L0_attn_x"]), "pack_d": packed(a), "experts_d": experts}

    nc = bacc.Bacc("TRN2", target_bir_lowering=False, num_devices=1)
    f32 = mybir.dt.float32
    args = [nc.dram_tensor(n, v.shape, f32, kind="ExternalInput").ap() for n, v in arrays.items()]
    out = nc.dram_tensor("out", (TOK, DM), f32, kind="ExternalOutput").ap()
    c_scratch = nc.dram_tensor("c_scratch", (2, S, L), f32, kind="Internal").ap()
    rows_d = nc.dram_tensor("rows_d", (ROWS, RW), f32, kind="Internal").ap()
    program(nc, *args, out, c_scratch, rows_d)
    r = run_bass_kernel_spmd(nc, [arrays], core_ids=[0])
    return r.results[0]["out"].reshape(NB, L, DM)
```

```python
import numpy as np
import concourse.bass as bass
import concourse.mybir as mybir
from contextlib import ExitStack

P = 128
NB, L, DM = 8, 512, 128
TILES = L // P
H, S, R = 2, 16, 64
DI = H * P
TAPS = 4
E, FF = 8, 512
FK = FF // P
TOK = NB * L
REGION = TOK + P
FU = 8
FTILES = TOK // P + E
EARLY = 2 * FU
assert EARLY * P <= (NB - 1) * L - E * (P - 1)
ROWS = E * REGION + (FTILES - TOK // P) * P
RW = 2 * DM + 2
NO_TOKEN = TOK
RANKS = 64
BW = P + 1
EW = FF + FK * DM + FK + DM
EPS = 1e-5

QUAD_A = (1.0093575430011281, -0.08225440736378242, -1.424741164592344, -2.3216937658543895)
QUAD_B = (1.106067408717108, 3.2574833956522826, 2.702115883781287, 0.43240884150072795)
LEAD = 0.0052325939439559314

PACK = [("ident", P), ("minus_half", TILES), ("eps", TILES), ("b_in", 2 * H), ("conv_w", H * TAPS), ("conv_b", H),
        ("w_in", 2 * DI),
        ("bidiag", BW), ("before", P), ("ones", P), ("expert_no", E), ("expert_no8", E), ("region_at", E),
        ("token", TILES), ("quad_a", 4), ("tile_at", TOK // P), ("tile_no", FTILES), ("a_log", H * S), ("d_skip", H),
        ("x_proj", H * (R + 2 * S)), ("dt_w", DI), ("dt_b", H), ("a_log_s", DI), ("out_w", H * DM), ("out_b", DM),
        ("w_r", E), ("b_r", E)]
AT, PACK_W = {}, 0
for _name, _width in PACK:
    AT[_name] = (PACK_W, PACK_W + _width)
    PACK_W += _width
FIRST = AT["w_in"][1]

GROUPS, TERMS = S // 4, 3
POOL_STATES = tuple(4 * g + 2 for g in range(GROUPS))
VEC_STATES = tuple(s for s in range(S) if s not in POOL_STATES)
NV, NP_ = len(VEC_STATES), len(POOL_STATES)
K_SLOT = (0, 1, 2, 1)
SUMS = 2 * GROUPS * TERMS


def vec_before(s):
    return sum(1 for q in VEC_STATES if q < s)


def pool_before(s):
    return sum(1 for q in POOL_STATES if q < s)


def early(n, m=1):
    return isinstance(n, int) and n < m


SP_PADS = 5
PADS_AT = 6


def after(k, c, n=1):
    return (k, c + n) if c + n < FU else (k + 1, c + n - FU)


def ahead(k, c):
    return (k, c - 1) if c else (k - 1, FU - 1)


def starts(k, c, n):
    return isinstance(k, int) and FU * k + c < n


def ends(k, c, n=1):
    return isinstance(k, int) and FU * k + c >= FTILES - n


def program(nc, x_d, pack_d, experts_d, out_d, c_scratch, rows_d):
    F32, I32, BF16 = mybir.dt.float32, mybir.dt.int32, mybir.dt.bfloat16
    ALU, ACT, AX = mybir.AluOpType, mybir.ActivationFunctionType, mybir.AxisListType
    ctx = ExitStack()
    with ctx:
        def sb(name, shape, dt=F32):
            return ctx.enter_context(nc.sbuf_tensor(name, shape, dt))

        def sem(name):
            return ctx.enter_context(nc.semaphore(name))

        pack = sb("pack", [P, PACK_W])

        def const(name):
            return pack[:, AT[name][0]:AT[name][1]]

        ident, bidiag, before, ones = const("ident"), const("bidiag"), const("before"), const("ones")
        w_in, b_in = const("w_in"), const("b_in")
        conv_w = const("conv_w").rearrange("p (h k) -> p h k", h=H)
        conv_b, d_skip, dt_b = const("conv_b"), const("d_skip"), const("dt_b")
        x_proj = const("x_proj").rearrange("p (h r) -> p h r", h=H)
        out_w = const("out_w").rearrange("p (h r) -> p h r", h=H)
        dt_w = pack[0:R, AT["dt_w"][0]:AT["dt_w"][1]]
        a_log_s = pack[0:S, AT["a_log_s"][0]:AT["a_log_s"][1]]

        half_bin = sb("half_bin", [P, 2 * H])
        conv_in = sb("conv_in", [P, H])
        neg_d = sb("neg_d", [P, H])
        neg_a = sb("neg_a", [P, H * S])
        inv_a = sb("inv_a", [P, H * S])
        tiny_a = sb("tiny_a", [P, H * S])
        tiny_s = sb("tiny_s", [S, DI])
        inv_a_s = sb("inv_a_s", [S, DI])
        diag = sb("diag", [P, H, GROUPS, 2, P])

        x_in = [sb(f"x_in{i}", [P, TILES, DM]) for i in range(2)]
        stat1, mv1 = sb("stat1", [P, TILES, 6]), sb("mv1", [P, TILES, 2])
        var1, rstd1 = sb("var1", [P, TILES]), sb("rstd1", [P, TILES])
        xn, xnT = sb("xn", [P, TILES, DM]), sb("xnT", [P, L])
        xpad = sb("xpad", [P, H, TAPS - 1 + L])
        tanh_z = sb("tanh_z", [P, H, L])
        tanh_u = sb("tanh_u", [P, H, L])
        conv = sb("conv", [P, H, L])
        z_half = sb("z_half", [P, H, L])
        abs_p, y_exp, relu_p, poly = tanh_z, tanh_u, conv, z_half
        square = [sb(f"square{i}", [P, H, L]) for i in range(2)]
        gate_z = [sb(f"gate_z{i}", [P, H, L]) for i in range(2)]
        xc = sb("xc", [P, H, L])
        xcT = [sb(f"xcT{i}", [P, TILES, DI]) for i in range(2)]
        x_dbl = sb("x_dbl", [R + 2 * S, L])
        bc_T, bc_mul = sb("bc_T", [P, TILES, 2 * S]), sb("bc_mul", [P, TILES, S])
        bc_s = xn[0:S, :, :].rearrange("p j d -> p (j d)")
        skip = [sb(f"skip{i}", [P, H, L]) for i in range(2)]
        dt = [sb(f"dt{i}", [P, H, L]) for i in range(2)]

        big = sb("big", [P, S * TILES * BW + S * L])
        delta = big[:, 0:S * TILES * BW].rearrange("p (s j c) -> p s j c", s=S, j=TILES)
        c_all = big[:, S * TILES * BW:].rearrange("p (s t) -> p s t", s=S)
        w_all = big[:, 0:E * EW].rearrange("p (e c) -> p e c", e=E)
        a_bar = [sb(f"a_bar{i}", [P, L]) for i in range(4)]
        k_st = [sb(f"k_st{i}", [P, H, L]) for i in range(3)]
        prod = [sb(f"prod{i}", [P, H, L]) for i in range(4)]

        y = sb("y", [P, H, L])
        x_res = sb("x_res", [P, TILES, DM])
        row = sb("row", [P, TILES, RW])
        stat2, mv2 = sb("stat2", [P, TILES, 6]), sb("mv2", [P, TILES, 2])
        var2, rstd2 = sb("var2", [P, TILES]), sb("rstd2", [P, TILES])
        xn2T = xnT
        logit, shifted, expd = (sb(n, [P, TILES, E]) for n in ("logit", "shifted", "expd"))
        top, chosen, zsum = (sb(n, [P, TILES]) for n in ("top", "chosen", "zsum"))
        is_top, cand = (sb(n, [P, TILES, E]) for n in ("is_top", "cand"))
        one_hot = sb("one_hot", [P, TILES + 1, E], BF16)
        count_w = sb("count_w", [P, 2, P], BF16)
        slot_e, slot_m, slot = sb("slot_e", [P, TILES, E]), sb("slot_m", [P, TILES, E]), sb("slot", [P, TILES])
        slot_i = sb("slot_i", [P, TILES], I32)
        filled = sb("filled", [P, E])
        token = sb("token", [P, TILES])

        def flat(v):
            return v[:, :, :].rearrange("p h t -> p (h t)")

        plan_w = [0]

        def plan(width, dt=F32):
            at = plan_w[0]
            plan_w[0] += width
            v = flat(square[0])[0:1, at:at + width]
            return v if dt == F32 else v.bitcast(dt)

        STAGE = max(EARLY, FTILES - EARLY)
        count, n_tiles, end_tile, filled_i, jump = plan(E), plan(E), plan(E), plan(E, I32), plan(E)
        taken = plan(E + 1)
        full = plan(E * (TOK // P)).rearrange("p (e j) -> p e j", e=E)
        passed_all, passed_jump = (plan(STAGE * E).rearrange("p (i e) -> p i e", e=E) for _ in range(2))
        t_exp, t_off, t_row = plan(STAGE), plan(STAGE), plan(STAGE)
        t_exp_i, t_row_i = plan(FTILES, I32), plan(FTILES, I32)
        zero8 = sb("zero8", [1, E])
        pad = sb("pad", [P, RW])
        f_row = [flat(v)[:, i * RW:(i + 1) * RW] for v in (xcT[0], skip[0], gate_z[0]) for i in range(3)][:FU]
        f_xT = [xn[:, i, :] for i in range(4)]
        f_w1 = [conv[:, i, :] for i in range(2)]
        f_w2 = [flat(v)[:, 0:EW - FF] for v in (z_half, tanh_u, xc, square[1])]
        biased = [xpad[:, 0, i * DM:(i + 1) * DM] for i in range(2)]
        f_h = [tanh_z[:, i, :] for i in range(2)]
        f_out = [v[:, c, :] for v in x_in for c in range(TILES)]

        bank = [ctx.enter_context(nc.psum_tensor(f"bank{i}", [P, L], F32)) for i in range(2)]
        dv = [[ctx.enter_context(nc.psum_tensor(f"dv{h}_{i}", [P, L], F32)) for i in range(2)] for h in range(H)]
        f_turn, f_hid = [dv[h][0] for h in range(2)], [dv[h][1] for h in range(2)]
        ysum = ctx.enter_context(nc.psum_tensor("ysum", [P, H, L], F32))

        wait_carrier = sem("wait_carrier")
        first_loaded, rest_loaded, s_pad_ready = sem("first_loaded"), sem("rest_loaded"), sem("pad_ready")
        x_loaded, res_loaded = sem("x_loaded"), sem("res_loaded")
        c_stored = sem("c_stored")
        c_loaded = [sem(f"c_loaded{g}") for g in range(4)]
        setup_a, setup = sem("setup_a"), sem("setup")
        stats1, mv1_ready, var1_ready, rstd1_ready = (
            sem("stats1"), sem("mv1_ready"), sem("var1_ready"), sem("rstd1_ready"))
        xn_ready, xn_turned, xnT_ready = sem("xn_ready"), sem("xn_turned"), sem("xnT_ready")
        in_done, in_read = sem("in_done"), sem("in_read")
        conv_step, tanhz_ready, tanhu_ready = sem("conv_step"), sem("tanhz_ready"), sem("tanhu_ready")
        gate_ready, xc_ready = sem("gate_ready"), sem("xc_ready")
        xdbl_done, xdbl_ready = sem("xdbl_done"), sem("xdbl_ready")
        xc_turned, xcT_ready = sem("xc_turned"), sem("xcT_ready")
        xdbl_turned, bcT_ready, bcmul_ready = sem("xdbl_turned"), sem("bcT_ready"), sem("bcmul_ready")
        bc_turned, bcs_ready, q_done, skip_ready = (
            sem("bc_turned"), sem("bcs_ready"), sem("q_done"), sem("skip_ready"))
        dt_done, dt_read, yexp_ready, square_ready, poly_step = (
            sem("dt_done"), sem("dt_read"), sem("yexp_ready"), sem("square_ready"), sem("poly_step"))
        delta_ready, dv_ready, abar_ready, scanned = (
            sem("delta_ready"), sem("dv_ready"), sem("abar_ready"), sem("scanned"))
        prod_vec, prod_pool, pair_added, summed = (
            sem("prod_vec"), sem("prod_pool"), sem("pair_added"), sem("summed"))
        y_ready, yg_ready, out_done, res_ready = sem("y_ready"), sem("yg_ready"), sem("out_done"), sem("res_ready")
        x1_ready, stats2, mv2_ready, var2_ready, rstd2_ready = (
            sem("x1_ready"), sem("stats2"), sem("mv2_ready"), sem("var2_ready"), sem("rstd2_ready"))
        xn2_ready, xn2_turned, xn2T_ready, logit_done = (
            sem("xn2_ready"), sem("xn2_turned"), sem("xn2T_ready"), sem("logit_done"))
        route, expd_ready, rank_done, placed, scattered = (
            sem("route"), sem("expd_ready"), sem("rank_done"), sem("placed"), sem("scattered"))

        pad_zero, padded, planned, w_loaded = sem("pad_zero"), sem("padded"), sem("planned"), sem("w_loaded")
        b2_added = sem("b2_added")
        early_ends, ends_ready = sem("early_ends"), sem("ends_ready")
        f_loaded = [sem(f"f_loaded{c}") for c in range(FU)]
        f_stored = [sem(f"f_stored{c}") for c in range(FU)]
        f_turned, f_xT_ready, w1_taken, w2_taken = sem("f_turned"), sem("f_xT_ready"), sem("w1_taken"), sem("w2_taken")
        hidden_done, gelu_done, mlp_done, combined = (
            sem("hidden_done"), sem("gelu_done"), sem("mlp_done"), sem("combined"))

        block = ctx.enter_context(nc.Block())


        @block.sync
        def _(sp):
            def load_x(n, p):
                if not early(n):
                    sp.wait_ge(x_loaded, 16 * n)
                    sp.sem_inc(wait_carrier)
                if not early(n, 2):
                    sp.wait_ge(xn_ready, n - 1)
                sp.dma_start(x_in[p][:, :, :], x_d[n].rearrange("(j q) d -> q j d", q=P)).then_inc(x_loaded, 16)

            def load_residual(t):
                if not early(t):
                    sp.wait_ge(x1_ready, t)
                sp.dma_start(x_res[:, :, :], x_d[t].rearrange("(j q) d -> q j d", q=P)).then_inc(res_loaded, 16)

            def store_c(n, p):
                sp.wait_ge(xdbl_ready, n + 1)
                sp.dma_start(c_scratch[p], x_dbl[R + S:R + 2 * S, :]).then_inc(c_stored, 16)

            def load_c(n, p, g):
                sp.wait_ge(c_stored, 16 * (n + 1))
                if not early(n):
                    sp.sem_inc(wait_carrier)
                    sp.wait_ge(prod_vec, NV * (n - 1) + vec_before(4 * g + 4))
                    sp.sem_inc(wait_carrier)
                    sp.wait_ge(prod_pool, NP_ * (n - 1) + pool_before(4 * g + 4))
                src = bass.AP(c_scratch.tensor, (p * S + 4 * g) * L, [[0, P], [1, 4 * L]])
                sp.dma_start(c_all[:, 4 * g:4 * g + 4, :].rearrange("p s t -> p (s t)"), src).then_inc(c_loaded[g], 16)

            def body(b, p, first=False, last=False):
                if not last:
                    load_x(b + 1, 1 - p)
                load_c(b, p, 3)
                if not first:
                    load_residual(b - 1)
                if not last:
                    store_c(b + 1, 1 - p)
                    for g in range(3):
                        load_c(b + 1, 1 - p, g)

            load_x(0, 0)
            sp.dma_start(pack[:, 0:FIRST], pack_d[:, 0:FIRST]).then_inc(first_loaded, 16)
            sp.dma_start(pack[:, FIRST:], pack_d[:, FIRST:]).then_inc(rest_loaded, 16)
            store_c(0, 0)
            for g in range(3):
                load_c(0, 0, g)
            body(0, 0, first=True)
            with sp.Fori(0, (NB - 2) // 2) as i:
                body(2 * i + 1, 1)
                body(2 * i + 2, 0)
            body(NB - 1, 1, last=True)
            load_residual(NB - 1)

            def load_weights(e):
                states = min(S, -(-(e + 1) * EW // (TILES * BW)))
                sp.wait_ge(dv_ready, 32 * (NB - 1) + 2 * states)
                if (e + 1) * EW > S * TILES * BW:
                    c_states = -(-((e + 1) * EW - S * TILES * BW) // L)
                    sp.wait_ge(prod_vec, NV * (NB - 1) + vec_before(c_states))
                    sp.wait_ge(prod_pool, NP_ * (NB - 1) + pool_before(c_states))
                sp.dma_start(w_all[:, e, :], experts_d[e]).then_inc(w_loaded, 16)

            def load_rows(k, c):
                if not starts(k, c, FU):
                    sp.wait_ge(f_stored[c], 16 * k)
                    sp.sem_inc(wait_carrier)
                at = sp.value_load(t_row_i[0:1, bass.ds(FU * k + c, 1)], min_val=0, max_val=ROWS - P)
                sp.dma_start(f_row[c][:, :], rows_d[bass.ds(at, P), :]).then_inc(f_loaded[c], 16)

            for e in range(E - 2):
                load_weights(e)
            sp.wait_ge(scattered, 64 * (NB - 1) + 16)
            sp.wait_ge(planned, 10)
            sp.sem_inc(wait_carrier)
            for c in range(2):
                load_rows(0, c)
            for e in range(E - 2, E):
                load_weights(e)
            for c in range(2, FU):
                load_rows(0, c)
            for c in range(PADS_AT):
                load_rows(1, c)
            sp.wait_ge(ends_ready, 1)
            sp.sem_inc(wait_carrier)
            for e in range(SP_PADS):
                at = sp.value_load(filled_i[0:1, e:e + 1], min_val=e * REGION, max_val=e * REGION + TOK)
                sp.dma_start(rows_d[bass.ds(at, P), :], pad[:, :]).then_inc(padded, 16)
            for c in range(PADS_AT, FU):
                load_rows(1, c)
            sp.wait_ge(scattered, 64 * NB + 16)
            sp.wait_ge(padded, 16 * E)
            sp.wait_ge(planned, 20)
            sp.sem_inc(wait_carrier)
            with sp.Fori(EARLY // FU, FTILES // FU) as k:
                for c in range(FU):
                    load_rows(k, c)
            sp.wait_ge(w_loaded, 16 * E)

        @block.tensor
        def _(pe):
            def turn_xn(n):
                pe.wait_ge(xn_ready, n + 1)
                if not early(n):
                    pe.wait_ge(skip_ready, 2 * n)
                for j in range(TILES):
                    last = nc.tensor.transpose(bank[0][:, j * P:(j + 1) * P], xn[:, j, :], ident)
                last.then_inc(xn_turned, 1)

            def in_proj(n, m):
                if m < 2:
                    pe.wait_ge(xnT_ready, n + 1)
                else:
                    pe.wait_ge(in_read, 4 * n + m - 1)
                nc.tensor.matmul(bank[(m + 1) % 2][:, :], w_in[:, m * P:(m + 1) * P], xnT[:, :],
                                 start=True, stop=True).then_inc(in_done, 1)

            def out_proj(t, n):
                pe.wait_ge(yg_ready, t + 1)
                if n is not None:
                    pe.wait_ge(in_read, 4 * n + 3)
                else:
                    pe.wait_ge(placed, 9 * t)
                for j in range(TILES):
                    for h in range(H):
                        last = nc.tensor.matmul(bank[1][:, j * P:(j + 1) * P], y[:, h, j * P:(j + 1) * P],
                                                out_w[:, h, :], start=(h == 0), stop=(h == H - 1))
                last.then_inc(out_done, 1)

            def x_projection(n):
                pe.wait_ge(xc_ready, n + 1)
                pe.wait_ge(in_read, 4 * n + 4)
                for h in range(H):
                    last = nc.tensor.matmul(bank[0][0:R + 2 * S, :], x_proj[:, h, :], xc[:, h, :],
                                            start=(h == 0), stop=(h == H - 1))
                last.then_inc(xdbl_done, 1)

            def dt_proj(n, t, h):
                pe.wait_ge(xdbl_ready, n + 1)
                if h == 1 and t is not None:
                    pe.wait_ge(x1_ready, t + 1)
                nc.tensor.matmul(bank[h][:, :], dt_w[:, h * P:(h + 1) * P], x_dbl[0:R, :],
                                 start=True, stop=True).then_inc(dt_done, 1)

            def turn_xdbl(n):
                pe.wait_ge(dt_read, 2 * n + 1)
                for j in range(TILES):
                    last = nc.tensor.transpose(bank[0][:, j * 96:(j + 1) * 96], x_dbl[:, j * P:(j + 1) * P],
                                               ident[0:96, 0:96])
                last.then_inc(xdbl_turned, 1)

            def turn_xc(n, part):
                if part == 0:
                    pe.wait_ge(dt_read, 2 * n + 2)
                else:
                    pe.wait_ge(xcT_ready, 2 * n + 1)
                for j in range(2):
                    for h in range(H):
                        at = j * DI + h * P
                        j0 = (2 * part + j) * P
                        last = nc.tensor.transpose(bank[1][:, at:at + P], xc[:, h, j0:j0 + P], ident)
                last.then_inc(xc_turned, 1)

            def turn_xn2(t, n):
                pe.wait_ge(xn2_ready, t + 1)
                if n is not None:
                    pe.wait_ge(bcT_ready, n + 1)
                else:
                    pe.wait_ge(skip_ready, 2 * NB)
                    pe.wait_ge(xn2T_ready, t)
                for j in range(TILES):
                    last = nc.tensor.transpose(bank[0][:, j * P:(j + 1) * P], row[:, j, 0:DM], ident)
                last.then_inc(xn2_turned, 1)

            def turn_bc(n, t):
                pe.wait_ge(bcmul_ready, n + 1)
                if t is not None:
                    pe.wait_ge(xn2T_ready, t + 1)
                for j in range(TILES):
                    last = nc.tensor.transpose(bank[0][0:S, j * P:(j + 1) * P], bc_mul[:, j, :], ident)
                last.then_inc(bc_turned, 1)

            def q_matmul(n, h):
                if h == 0:
                    pe.wait_ge(bcs_ready, n + 1)
                else:
                    pe.wait_ge(skip_ready, 2 * n + 1)
                nc.tensor.matmul(bank[0][:, :], inv_a_s[:, h * P:(h + 1) * P], bc_s[:, :],
                                 start=True, stop=True).then_inc(q_done, 1)

            def router(t, n):
                pe.wait_ge(xn2T_ready, t + 1)
                if n is not None:
                    pe.wait_ge(xcT_ready, 2 * n + 2)
                for j in range(TILES):
                    last = nc.tensor.matmul(bank[1][:, j * E:(j + 1) * E], xn2T[:, j * P:(j + 1) * P],
                                            const("w_r"), start=True, stop=True)
                last.then_inc(logit_done, 1)

            def ranks(t):
                pe.wait_ge(route, 7 * t + 6)
                hot = one_hot[:, :, :].rearrange("p j e -> p (j e)")
                nc.tensor.matmul(bank[1][:, RANKS:RANKS + (TILES + 1) * E], count_w[:, 0, :], hot,
                                 start=True, stop=False, skip_group_check=True)
                for j in range(1, TILES + 1):
                    last = nc.tensor.matmul(bank[1][:, RANKS + j * E:RANKS + (TILES + 1) * E], count_w[:, 1, :],
                                            hot[:, 0:(TILES + 1 - j) * E], start=False, stop=(j == TILES),
                                            skip_group_check=True)
                last.then_inc(rank_done, 1)

            def difference(n, p, s, h):
                k = 32 * n + 2 * s + h
                if s % 4 == 0 and h == 0:
                    pe.wait_ge(delta_ready, 4 * n + s // 4 + 1)
                if s == 0 and h == 0:
                    pe.wait_ge(xcT_ready, 2 * n + 2)
                if not (early(n) and s < 2):
                    pe.wait_ge(scanned, k - 3)
                to = dv[h][s % 2]
                for j in range(TILES):
                    w = BW if j < TILES - 1 else P
                    last = nc.tensor.matmul(to[:, j * P:j * P + w], xcT[p][:, j, h * P:(h + 1) * P],
                                            delta[:, s, j, 0:w], start=(j == 0), stop=(j == TILES - 1),
                                            skip_group_check=True)
                last.then_inc(dv_ready, 1)

            def add_term(n, g, term):
                if term == 0:
                    pe.wait_ge(prod_pool, NP_ * n + g + 1)
                elif term == 1:
                    pe.wait_ge(pair_added, GROUPS * n + g + 1)
                else:
                    pe.wait_ge(prod_vec, NV * n + vec_before(4 * g + 4))
                if g == 0 and term == 0 and not early(n):
                    pe.wait_ge(y_ready, n)
                for h in range(H):
                    weights = ident if term == 1 else diag[:, h, g, term // 2, :]
                    nc.tensor.matmul(ysum[:, h, :], weights, prod[(2, 1, 3)[term]][:, h, :],
                                     start=(g == 0 and term == 0), stop=(g == GROUPS - 1 and term == 2),
                                     skip_group_check=True).then_inc(summed, 1)

            def body(b, p, first=False, last=False):
                n = None if last else b + 1
                t = None if first else b - 1
                for s in range(S):
                    ahead_of = (b, p, s + 1) if s < S - 1 else (n, 1 - p, 0)
                    if ahead_of[0] is not None:
                        difference(*ahead_of, 0)
                    if s >= 4 and s % 4 < TERMS:
                        add_term(b, s // 4 - 1, s % 4)
                    elif s < TERMS and not first:
                        add_term(b - 1, GROUPS - 1, s)
                    if ahead_of[0] is not None:
                        difference(*ahead_of, 1)
                    if first and s == 0:
                        q_matmul(0, 1)
                    if n is not None and s == 2:
                        turn_xn(n)
                    if n is not None and s == 3:
                        in_proj(n, 0)
                        in_proj(n, 1)
                    if n is not None and s == 4:
                        in_proj(n, 2)
                        in_proj(n, 3)
                    if t is not None and s == (5 if last else 6):
                        out_proj(t, n)
                    if n is not None and s == 7:
                        x_projection(n)
                    if n is not None and s == 8:
                        dt_proj(n, t, 0)
                        dt_proj(n, t, 1)
                    if n is not None and s == 9:
                        turn_xdbl(n)
                        turn_xc(n, 0)
                    if t is not None and s == (8 if last else 10):
                        turn_xn2(t, n)
                    if n is not None and s == 10:
                        turn_xc(n, 1)
                    if n is not None and s == 11:
                        turn_bc(n, t)
                    if t is not None and s == (9 if last else 11):
                        router(t, n)
                    if n is not None and s == 12:
                        q_matmul(n, 0)
                    if t is not None and s == (10 if last else 13):
                        ranks(t)
                    if n is not None and s == 14:
                        q_matmul(n, 1)

            pe.wait_ge(first_loaded, 16)
            turn_xn(0)
            for m in range(4):
                in_proj(0, m)
            pe.wait_ge(rest_loaded, 16)
            x_projection(0)
            dt_proj(0, None, 0)
            dt_proj(0, None, 1)
            turn_xdbl(0)
            turn_xc(0, 0)
            turn_xc(0, 1)
            turn_bc(0, None)
            difference(0, 0, 0, 0)
            difference(0, 0, 0, 1)
            pe.wait_ge(setup, 9)
            q_matmul(0, 0)
            body(0, 0, first=True)
            with pe.Fori(0, (NB - 2) // 2) as i:
                body(2 * i + 1, 1)
                body(2 * i + 2, 0)
            body(NB - 1, 1, last=True)

            def turn_row(k, c):
                i = FU * k + c
                pe.wait_ge(f_loaded[c], 16 * (k + 1))
                if starts(k, c, 2):
                    pe.wait_ge(scanned, 32 * NB - 2)
                else:
                    pe.wait_ge(f_xT_ready, i - 1)
                nc.tensor.transpose(f_turn[c % 2][:, 0:P], f_row[c][:, 0:DM], ident).then_inc(f_turned, 1)

            def hidden(k, c):
                i = FU * k + c
                pe.wait_ge(f_xT_ready, i + 1)
                pe.wait_ge(w1_taken, i + 1)
                if not starts(k, c, 2):
                    pe.wait_ge(gelu_done, i - 1)
                else:
                    pe.wait_ge(scanned, 32 * NB)
                for f in range(FK):
                    last = nc.tensor.matmul(f_hid[c % 2][:, f * P:(f + 1) * P], f_w1[c % 2][:, f * P:(f + 1) * P],
                                            f_xT[c % 4][:, :], start=True, stop=True)
                last.then_inc(hidden_done, 1)

            def mlp_out(k, c):
                i = FU * k + c
                pe.wait_ge(gelu_done, i + 1)
                pe.wait_ge(w2_taken, i + 1)
                if not starts(k, c, 2):
                    pe.wait_ge(b2_added, i - 1)
                else:
                    pe.wait_ge(y_ready, NB)
                to = ysum[:, c % 2, 0:DM]
                for f in range(FK):
                    last = nc.tensor.matmul(to, f_h[c % 2][:, f * P:(f + 1) * P],
                                            f_w2[c % 4][:, f * DM:(f + 1) * DM], start=(f == 0), stop=(f == FK - 1))
                last.then_inc(mlp_done, 1)

            def tiles(k):
                for c in range(FU):
                    hidden(k, c)
                    if not starts(k, c, 1):
                        mlp_out(*ahead(k, c))
                    if not ends(k, c, 2):
                        turn_row(*after(k, c, 2))
                    if starts(k, c, FU):
                        if c == 1:
                            out_proj(NB - 1, None)
                        if c == 4:
                            turn_xn2(NB - 1, None)
                        if c == 5:
                            router(NB - 1, None)
                        if c == 6:
                            ranks(NB - 1)

            for i in range(2):
                pe.wait_ge(prod_vec, NV * (NB - 1) + vec_before(S - 4 + i + 1))
                for h in range(H):
                    nc.tensor.matmul(ysum[:, h, :], ident, prod[i][:, h, :], start=False, stop=False,
                                     skip_group_check=True).then_inc(summed, 1)
            turn_row(0, 0)
            turn_row(0, 1)
            add_term(NB - 1, GROUPS - 1, 0)
            add_term(NB - 1, GROUPS - 1, 2)
            for k in range(EARLY // FU):
                tiles(k)
            with pe.Fori(EARLY // FU, FTILES // FU - 1) as k:
                tiles(k)
            tiles(FTILES // FU - 1)
            mlp_out(FTILES // FU - 1, FU - 1)

        @block.scalar
        def _(act):
            def copy_xnT(n):
                act.wait_ge(xn_turned, n + 1)
                if not early(n):
                    act.wait_ge(in_done, 4 * n)
                nc.scalar.activation(xnT[:, :], bank[0][:, :], ACT.Copy).then_inc(xnT_ready, 1)

            def read_in_proj(n, m):
                act.wait_ge(in_done, 4 * n + m + 1)
                if m == 0 and not early(n):
                    act.wait_ge(conv_step, 6 * n)
                if m == 2 and not early(n):
                    act.wait_ge(poly_step, 5 * n)
                frm = bank[(m + 1) % 2][:, :]
                if m < H:
                    if m == 0 and not early(n):
                        act.wait_ge(poly_step, 5 * n)
                    nc.scalar.activation(xpad[:, m, TAPS - 1:], frm, ACT.Identity, bias=b_in[:, m:m + 1])
                    if early(n) and m == 0:
                        act.wait_ge(setup, 5)
                    nc.scalar.activation(conv[:, m, :], frm, ACT.Identity, bias=conv_in[:, m:m + 1],
                                         scale=conv_w[:, m, TAPS - 1:]).then_inc(in_read, 1)
                else:
                    nc.scalar.activation(z_half[:, m - H, :], frm, ACT.Identity, bias=half_bin[:, m:m + 1],
                                         scale=0.5).then_inc(in_read, 1)

            def tanh_of_z(n):
                act.wait_ge(in_read, 4 * n + 4)
                if not early(n):
                    act.wait_ge(yexp_ready, n)
                nc.scalar.activation(tanh_z[:, :, :], z_half[:, :, :], ACT.Tanh).then_inc(tanhz_ready, 1)

            def tanh_of_conv(n):
                act.wait_ge(conv_step, 6 * n + 6)
                nc.scalar.activation(tanh_u[:, :, :], conv[:, :, :], ACT.Tanh).then_inc(tanhu_ready, 1)

            def copy_xdbl(n):
                act.wait_ge(xdbl_done, n + 1)
                if not early(n):
                    act.wait_ge(xdbl_turned, n)
                    act.wait_ge(c_stored, 16 * n)
                nc.scalar.activation(x_dbl[:, :], bank[0][0:R + 2 * S, :], ACT.Copy).then_inc(xdbl_ready, 1)

            def copy_xcT(n, p, part):
                act.wait_ge(xc_turned, 2 * n + part + 1)
                if part == 0 and not early(n, 2):
                    act.wait_ge(dv_ready, 32 * (n - 1))
                to = xcT[p][:, 2 * part:2 * part + 2, :].rearrange("p j d -> p (j d)")
                nc.scalar.activation(to, bank[1][:, :], ACT.Copy).then_inc(xcT_ready, 1)

            def softplus_parts(n, h):
                act.wait_ge(dt_done, 2 * n + h + 1)
                if h == 0:
                    act.wait_ge(gate_ready, n + 1)
                    act.wait_ge(xc_ready, n + 1)
                nc.scalar.activation(abs_p[:, h, :], bank[h][:, :], ACT.Abs, bias=dt_b[:, h:h + 1])
                nc.scalar.activation(relu_p[:, h, :], bank[h][:, :], ACT.Relu,
                                     bias=dt_b[:, h:h + 1]).then_inc(dt_read, 1)

            def softplus_exp(n):
                act.wait_ge(dt_read, 2 * n + 2)
                nc.scalar.activation(y_exp[:, :, :], abs_p[:, :, :], ACT.Exp, scale=-1.0).then_inc(yexp_ready, 1)

            def softplus_square(n, i):
                if i == 0:
                    act.wait_ge(yexp_ready, n + 1)
                if not (isinstance(n, int) and n == 0 and i < 2):
                    act.wait_ge(poly_step, 5 * n + i - 1 if i >= 2 else 5 * n)
                qa = const("quad_a")[:, i:i + 1]
                nc.scalar.activation(square[i % 2][:, :, :], y_exp[:, :, :], ACT.Square,
                                     bias=qa).then_inc(square_ready, 1)

            def copy_bc(n):
                act.wait_ge(bc_turned, n + 1)
                if not early(n):
                    act.wait_ge(q_done, 2 * n)
                nc.scalar.activation(bc_s[:, :], bank[0][0:S, :], ACT.Copy).then_inc(bcs_ready, 1)

            def copy_xn2T(t):
                act.wait_ge(xn2_turned, t + 1)
                nc.scalar.activation(xn2T[:, :], bank[0][:, :], ACT.Copy).then_inc(xn2T_ready, 1)

            def exp_logits(t):
                act.wait_ge(route, 7 * t + 7)
                nc.scalar.activation(expd[:, :, :], shifted[:, :, :], ACT.Exp).then_inc(expd_ready, 1)

            def decay(n, p, s, h):
                k = 32 * n + 2 * s + h
                if s == 0 and h == 0:
                    act.wait_ge(poly_step, 5 * n + 5)
                if not (isinstance(n, int) and k < 4):
                    act.wait_ge(scanned, k - 3)
                at = h * S + s
                nc.scalar.activation(a_bar[(2 * s + h) % 4][:, :], dt[p][:, h, :], ACT.Exp,
                                     scale=neg_a[:, at:at + 1]).then_inc(abar_ready, 1)

            def body(b, p, first=False, last=False):
                n = None if last else b + 1
                t = None if first else b - 1
                for s in range(S):
                    for h in range(H):
                        if s < S - 1:
                            decay(b, p, s + 1, h)
                        elif not last:
                            decay(n, 1 - p, 0, h)
                    if n is not None and s == 2:
                        copy_xnT(n)
                    if n is not None and s == 3:
                        read_in_proj(n, 0)
                        read_in_proj(n, 1)
                    if n is not None and s == 4:
                        read_in_proj(n, 2)
                        read_in_proj(n, 3)
                        tanh_of_z(n)
                    if n is not None and s == 6:
                        tanh_of_conv(n)
                    if n is not None and s == 7:
                        copy_xdbl(n)
                    if n is not None and s == 8:
                        softplus_parts(n, 0)
                        softplus_parts(n, 1)
                    if t is not None and s == (8 if last else 10):
                        copy_xn2T(t)
                    if n is not None and s == 9:
                        copy_xcT(n, 1 - p, 0)
                        softplus_exp(n)
                        softplus_square(n, 0)
                    if n is not None and s == 10:
                        copy_xcT(n, 1 - p, 1)
                        softplus_square(n, 1)
                    if n is not None and s == 11:
                        copy_bc(n)
                        softplus_square(n, 2)
                    if t is not None and s == (10 if last else 12):
                        exp_logits(t)
                    if n is not None and s == 12:
                        softplus_square(n, 3)

            act.wait_ge(first_loaded, 16)
            act.wait_ge(rest_loaded, 16)
            nc.scalar.activation(neg_a[:, :], const("a_log"), ACT.Exp)
            nc.scalar.activation(inv_a_s[:, :], a_log_s, ACT.Exp).then_inc(setup_a, 1)
            copy_xnT(0)
            for m in range(2):
                read_in_proj(0, m)
            act.wait_ge(setup, 4)
            for m in range(2, 4):
                read_in_proj(0, m)
            tanh_of_z(0)
            tanh_of_conv(0)
            copy_xdbl(0)
            softplus_parts(0, 0)
            softplus_parts(0, 1)
            softplus_exp(0)
            softplus_square(0, 0)
            softplus_square(0, 1)
            copy_xcT(0, 0, 0)
            copy_xcT(0, 0, 1)
            softplus_square(0, 2)
            softplus_square(0, 3)
            copy_bc(0)
            act.wait_ge(setup, 9)
            decay(0, 0, 0, 0)
            decay(0, 0, 0, 1)
            body(0, 0, first=True)
            with act.Fori(0, (NB - 2) // 2) as i:
                body(2 * i + 1, 1)
                body(2 * i + 2, 0)
            body(NB - 1, 1, last=True)

            def gelu(k, c):
                i = FU * k + c
                act.wait_ge(hidden_done, i + 1)
                act.wait_ge(w2_taken, i + 1)
                if not starts(k, c, 2):
                    act.wait_ge(mlp_done, i - 1)
                for f in range(FK):
                    at = FK * DM + f
                    last = nc.scalar.activation(f_h[c % 2][:, f * P:(f + 1) * P], f_hid[c % 2][:, f * P:(f + 1) * P],
                                                ACT.Gelu, bias=f_w2[c % 4][:, at:at + 1])
                last.then_inc(gelu_done, 1)

            def take_xT(k, c):
                i = FU * k + c
                act.wait_ge(f_turned, i + 1)
                if not starts(k, c, 4):
                    act.wait_ge(hidden_done, i - 3)
                nc.scalar.activation(f_xT[c % 4][:, :], f_turn[c % 2][:, 0:P], ACT.Copy).then_inc(f_xT_ready, 1)

            def tiles(k):
                for c in range(FU):
                    if starts(k, c, FU):
                        if c == 5:
                            copy_xn2T(NB - 1)
                        if c == 7:
                            exp_logits(NB - 1)
                    gelu(k, c)
                    if isinstance(k, int) and k == 1 and c < E - SP_PADS:
                        act.wait_ge(ends_ready, 1)
                        e = SP_PADS + c
                        at = act.value_load(filled_i[0:1, e:e + 1], min_val=e * REGION, max_val=e * REGION + TOK)
                        act.dma_start(rows_d[bass.ds(at, P), :], pad[:, :]).then_inc(padded, 16)
                    if not ends(k, c, 2):
                        take_xT(*after(k, c, 2))

            take_xT(0, 0)
            take_xT(0, 1)
            for k in range(EARLY // FU):
                tiles(k)
            with act.Fori(EARLY // FU, FTILES // FU - 1) as k:
                tiles(k)
            tiles(FTILES // FU - 1)

        @block.vector
        def _(dve):
            def statistics(n, p):
                dve.wait_ge(x_loaded, 16 * (n + 1))
                for j in range(TILES):
                    last = nc.vector.bn_stats(stat1[:, j, :], x_in[p][:, j, :])
                last.then_inc(stats1, 1)
                dve.wait_ge(stats1, n + 1)
                dve.sem_inc(wait_carrier)
                for j in range(TILES):
                    last = nc.vector.bn_aggr(mv1[:, j, :], stat1[:, j, :])
                last.then_inc(mv1_ready, 1)

            def normalise(n, p):
                dve.wait_ge(rstd1_ready, n + 1)
                if not early(n):
                    dve.wait_ge(xn_turned, n)
                for j in range(TILES):
                    last = nc.vector.tensor_scalar(xn[:, j, :], x_in[p][:, j, :], mv1[:, j, 0:1],
                                                   rstd1[:, j:j + 1], ALU.subtract, ALU.mult)
                last.then_inc(xn_ready, 1)

            def convolve(n, m):
                tap, h = m // H, m % H
                if m == 0:
                    dve.wait_ge(in_read, 4 * n + 2)
                elif tap > 0:
                    dve.wait_ge(conv_step, 6 * n + m - 1)
                nc.vector.scalar_tensor_tensor(conv[:, h, :], xpad[:, h, tap:tap + L],
                                               conv_w[:, h, tap:tap + 1], conv[:, h, :],
                                               ALU.mult, ALU.add).then_inc(conv_step, 1)

            def silu_z(n, p):
                dve.wait_ge(tanhz_ready, n + 1)
                if not early(n, 2):
                    dve.wait_ge(yg_ready, n - 1)
                nc.vector.scalar_tensor_tensor(gate_z[p][:, :, :], tanh_z[:, :, :], 1.0, z_half[:, :, :],
                                               ALU.add, ALU.mult).then_inc(gate_ready, 1)

            def silu_conv(n):
                dve.wait_ge(tanhu_ready, n + 1)
                if not early(n):
                    dve.wait_ge(xc_turned, 2 * n)
                    dve.wait_ge(skip_ready, 2 * n)
                nc.vector.scalar_tensor_tensor(xc[:, :, :], tanh_u[:, :, :], 1.0, conv[:, :, :],
                                               ALU.add, ALU.mult).then_inc(xc_ready, 1)

            def copy_bcT(n):
                dve.wait_ge(xdbl_turned, n + 1)
                if not early(n):
                    dve.wait_ge(delta_ready, 4 * n)
                frm = bank[0][:, 0:TILES * 96].rearrange("p (j c) -> p j c", j=TILES)[:, :, R:]
                nc.vector.tensor_copy(bc_T[:, :, :], frm).then_inc(bcT_ready, 1)
                dve.wait_ge(bcT_ready, n + 1)
                if not early(n):
                    dve.wait_ge(bc_turned, n)
                nc.vector.tensor_tensor(bc_mul[:, :, :], bc_T[:, :, 0:S], bc_T[:, :, S:],
                                        ALU.mult).then_inc(bcmul_ready, 1)

            def skip_term(n, p, h):
                dve.wait_ge(q_done, 2 * n + h + 1)
                if not early(n, 2):
                    dve.wait_ge(y_ready, n - 1)
                nc.vector.scalar_tensor_tensor(skip[p][:, h, :], bank[0][:, :], neg_d[:, h:h + 1],
                                               xc[:, h, :], ALU.add, ALU.mult).then_inc(skip_ready, 1)

            def softplus_poly(n, p, i):
                if i < 4:
                    dve.wait_ge(square_ready, 4 * n + i + 1)
                if i == 0:
                    nc.vector.scalar_tensor_tensor(poly[:, :, :], square[0][:, :, :], QUAD_B[0], y_exp[:, :, :],
                                                   ALU.add, ALU.mult).then_inc(poly_step, 1)
                elif i < 4:
                    dve.wait_ge(poly_step, 5 * n + i)
                    nc.vector.scalar_tensor_tensor(poly[:, :, :], square[i % 2][:, :, :], QUAD_B[i], poly[:, :, :],
                                                   ALU.add, ALU.mult).then_inc(poly_step, 1)
                else:
                    dve.wait_ge(poly_step, 5 * n + i)
                    if not early(n, 2):
                        dve.wait_ge(abar_ready, 32 * (n - 1))
                    nc.vector.scalar_tensor_tensor(dt[p][:, :, :], poly[:, :, :], LEAD, relu_p[:, :, :],
                                                   ALU.mult, ALU.add).then_inc(poly_step, 1)

            def scan(n, s, h):
                k = 32 * n + 2 * s + h
                dve.wait_ge(dv_ready, k + 1)
                dve.wait_ge(abar_ready, k + 1)
                if h == 0:
                    back = (4, 2, 4, 2)[s % 4]
                    m, before_s = (n, s - back) if s >= back else (n - 1, S + s - back)
                    if not (isinstance(m, int) and m < 0):
                        if before_s in POOL_STATES:
                            dve.wait_ge(prod_pool, NP_ * m + pool_before(before_s + 1))
                        else:
                            dve.wait_ge(prod_vec, NV * m + vec_before(before_s + 1))
                nc.vector.tensor_tensor_scan(k_st[K_SLOT[s % 4]][:, h, :], dv[h][s % 2][:, :],
                                             a_bar[(2 * s + h) % 4][:, :], 0.0, ALU.add, ALU.mult).then_inc(scanned, 1)

            def times_c(n, s):
                dve.wait_ge(scanned, 32 * n + 2 * s + 2)
                if s % 4 == 0:
                    dve.wait_ge(c_loaded[s // 4], 16 * (n + 1))
                g = s // 4
                if not (early(n) and g == 0):
                    if s % 4 == 0:
                        dve.wait_ge(pair_added, GROUPS * n + g)
                    else:
                        dve.wait_ge(summed, SUMS * n + 2 * TERMS * g - (2 if s % 4 == 1 else 0))
                if s % 4 == 3:
                    nc.vector.tensor_tensor(prod[3][:, :, :], k_st[K_SLOT[3]][:, :, :],
                                            c_all[:, s:s + 1, :].to_broadcast([P, H, L]),
                                            ALU.mult).then_inc(prod_vec, 1)
                    return
                for h in range(H):
                    at = h * S + s
                    last = nc.vector.scalar_tensor_tensor(prod[s % 4][:, h, :], k_st[K_SLOT[s % 4]][:, h, :],
                                                          inv_a[:, at:at + 1], c_all[:, s, :], ALU.mult, ALU.mult)
                last.then_inc(prod_vec, 1)

            def finish_y(t, p):
                dve.wait_ge(summed, SUMS * (t + 1) + (2 if isinstance(t, int) and t == NB - 1 else 0))
                nc.vector.tensor_tensor(y[:, :, :], ysum[:, :, :], skip[p][:, :, :],
                                        ALU.subtract).then_inc(y_ready, 1)

            def residual(t):
                dve.wait_ge(out_done, t + 1)
                dve.wait_ge(res_ready, t + 1)
                dve.wait_ge(scattered, 64 * t + 16)
                nc.vector.tensor_tensor(row[:, :, DM:2 * DM], bank[1][:, :].rearrange("p (j d) -> p j d", j=TILES),
                                        x_res[:, :, :], ALU.add).then_inc(x1_ready, 1)

            def residual_moments(t):
                dve.wait_ge(x1_ready, t + 1)
                for j in range(TILES):
                    last = nc.vector.bn_stats(stat2[:, j, :], row[:, j, DM:2 * DM])
                last.then_inc(stats2, 1)
                dve.wait_ge(stats2, t + 1)
                dve.sem_inc(wait_carrier)
                for j in range(TILES):
                    last = nc.vector.bn_aggr(mv2[:, j, :], stat2[:, j, :])
                last.then_inc(mv2_ready, 1)

            def normalise2(t):
                dve.wait_ge(rstd2_ready, t + 1)
                for j in range(TILES):
                    last = nc.vector.tensor_scalar(row[:, j, 0:DM], row[:, j, DM:2 * DM], mv2[:, j, 0:1],
                                                   rstd2[:, j:j + 1], ALU.subtract, ALU.mult)
                last.then_inc(xn2_ready, 1)

            def choose(t):
                def spread(v):
                    return v.unsqueeze(1).to_broadcast([P, TILES, E])

                def along(v):
                    return v.unsqueeze(2).to_broadcast([P, TILES, E])

                dve.wait_ge(logit_done, t + 1)
                nc.vector.tensor_tensor(logit[:, :, :], bank[1][:, 0:TILES * E].rearrange("p (j e) -> p j e", j=TILES),
                                        spread(const("b_r")), ALU.add).then_inc(route, 1)
                dve.wait_ge(route, 7 * t + 1)
                nc.vector.tensor_reduce(top[:, :], logit[:, :, :], AX.X, ALU.max).then_inc(route, 1)
                dve.wait_ge(route, 7 * t + 2)
                nc.vector.tensor_tensor(is_top[:, :, :], logit[:, :, :], along(top[:, :]),
                                        ALU.is_equal).then_inc(route, 1)
                dve.wait_ge(route, 7 * t + 3)
                nc.vector.scalar_tensor_tensor(cand[:, :, :], is_top[:, :, :], -float(E), spread(const("expert_no8")),
                                               ALU.mult, ALU.add).then_inc(route, 1)
                dve.wait_ge(route, 7 * t + 4)
                nc.vector.tensor_reduce(chosen[:, :], cand[:, :, :], AX.X, ALU.min).then_inc(route, 1)
                dve.wait_ge(route, 7 * t + 5)
                nc.vector.tensor_tensor(one_hot[:, 0:TILES, :], spread(const("expert_no")), along(chosen[:, :]),
                                        ALU.is_equal).then_inc(route, 1)
                nc.vector.tensor_tensor(shifted[:, :, :], logit[:, :, :], along(top[:, :]),
                                        ALU.subtract).then_inc(route, 1)

            def place(t):
                dve.wait_ge(rank_done, t + 1)
                nc.vector.tensor_tensor(slot_e[:, :, :],
                                        bank[1][:, RANKS:RANKS + TILES * E].rearrange("p (j e) -> p j e", j=TILES),
                                        filled[:, :].unsqueeze(1).to_broadcast([P, TILES, E]),
                                        ALU.add).then_inc(placed, 1)
                dve.wait_ge(placed, 9 * t + 1)
                nc.vector.tensor_tensor(filled[:, :], bank[1][:, RANKS + TILES * E:RANKS + (TILES + 1) * E],
                                        filled[:, :], ALU.add).then_inc(placed, 1)
                nc.vector.tensor_tensor(slot_m[:, :, :], slot_e[:, :, :], one_hot[:, 0:TILES, :],
                                        ALU.mult).then_inc(placed, 1)
                dve.wait_ge(placed, 9 * t + 3)
                nc.vector.tensor_reduce(slot[:, :], slot_m[:, :, :], AX.X, ALU.add).then_inc(placed, 1)
                dve.wait_ge(placed, 9 * t + 4)
                nc.vector.tensor_copy(slot_i[:, :], slot[:, :]).then_inc(placed, 1)
                dve.wait_ge(expd_ready, t + 1)
                nc.vector.tensor_reduce(zsum[:, :], expd[:, :, :], AX.X, ALU.add).then_inc(placed, 1)
                dve.wait_ge(placed, 9 * t + 6)
                nc.vector.reciprocal(row[:, :, 2 * DM], zsum[:, :]).then_inc(placed, 1)
                nc.vector.tensor_copy(row[:, :, :].bitcast(I32)[:, :, 2 * DM + 1], token[:, :]).then_inc(placed, 1)
                dve.wait_ge(placed, 9 * t + 8)
                nc.vector.tensor_scalar(token[:, :], token[:, :], float(L), None, ALU.add).then_inc(placed, 1)

            def planned_to(stage, steps):
                dve.wait_ge(planned, 10 * stage + steps)

            def plan_counts(stage):
                dve.wait_ge(placed, 9 * (NB - 1 + stage))
                if stage == 0:
                    nc.vector.memset(taken[:, :], 0.0).then_inc(planned, 1)
                    nc.vector.scalar_tensor_tensor(count[:, :], filled[0:1, :], float(P - 1),
                                                   const("region_at")[0:1, :], ALU.subtract,
                                                   ALU.subtract).then_inc(planned, 1)
                else:
                    nc.vector.tensor_tensor(count[:, :], filled[0:1, :], const("region_at")[0:1, :],
                                            ALU.subtract).then_inc(planned, 1)
                    planned_to(stage, 1)
                    nc.vector.scalar_tensor_tensor(count[:, :], taken[:, 0:E], -float(P), count[:, :],
                                                   ALU.mult, ALU.add).then_inc(planned, 1)
                planned_to(stage, 2)
                nc.vector.tensor_tensor(full[:, :, :], count[:, :].unsqueeze(2).to_broadcast([1, E, TOK // P]),
                                        const("tile_at")[0:1, :].unsqueeze(1).to_broadcast([1, E, TOK // P]),
                                        ALU.is_gt).then_inc(planned, 1)
                planned_to(stage, 3)
                nc.vector.tensor_reduce(n_tiles[:, :], full[:, :, :], AX.X, ALU.add).then_inc(planned, 1)

            def stage_tiles(stage):
                return (0, EARLY) if stage == 0 else (EARLY, FTILES)

            def plan_passed(stage):
                m = stage_tiles(stage)[1] - stage_tiles(stage)[0]
                planned_to(stage, 4)
                nc.vector.tensor_tensor(jump[:, :], taken[:, 1:E + 1], taken[:, 0:E], ALU.subtract)
                nc.vector.tensor_tensor_scan(end_tile[:, :], n_tiles[:, :], zero8[:, :], 0.0, ALU.add,
                                             ALU.add).then_inc(planned, 1)
                planned_to(stage, 5)
                nc.vector.tensor_tensor(jump[:, :], jump[:, :], n_tiles[:, :], ALU.subtract)
                nc.vector.tensor_tensor(passed_all[:, 0:m, :], end_tile[:, :].unsqueeze(1).to_broadcast([1, m, E]),
                                        const("tile_no")[0:1, 0:m].unsqueeze(2).to_broadcast([1, m, E]),
                                        ALU.is_le).then_inc(planned, 1)
                planned_to(stage, 6)
                nc.vector.tensor_reduce(t_exp[:, 0:m], passed_all[:, 0:m, :], AX.X, ALU.add)
                nc.vector.tensor_tensor(passed_jump[:, 0:m, :], passed_all[:, 0:m, :],
                                        jump[:, :].unsqueeze(1).to_broadcast([1, m, E]), ALU.mult).then_inc(planned, 1)

            def plan_rows(stage):
                first, end = stage_tiles(stage)
                m = end - first
                planned_to(stage, 7)
                nc.vector.tensor_reduce(t_off[:, 0:m], passed_jump[:, 0:m, :], AX.X, ALU.add)
                nc.vector.tensor_scalar(t_exp_i[:, first:end], t_exp[:, 0:m], float(E - 1), None, ALU.min)
                nc.vector.tensor_scalar(t_row[:, 0:m], t_exp[:, 0:m], float(REGION), None,
                                        ALU.mult).then_inc(planned, 1)
                planned_to(stage, 8)
                nc.vector.scalar_tensor_tensor(t_off[:, 0:m], const("tile_no")[0:1, 0:m], taken[:, 0:1], t_off[:, 0:m],
                                               ALU.add, ALU.add).then_inc(planned, 1)
                planned_to(stage, 9)
                nc.vector.scalar_tensor_tensor(t_row_i[:, first:end], t_off[:, 0:m], float(P), t_row[:, 0:m],
                                               ALU.mult, ALU.add).then_inc(planned, 1)
                planned_to(stage, 10)

            def expert_ends():
                dve.wait_ge(placed, 9 * NB)
                nc.vector.tensor_copy(filled_i[:, :], filled[0:1, :]).then_inc(ends_ready, 1)

            def gate_last():
                dve.wait_ge(y_ready, NB)
                nc.vector.tensor_tensor(y[:, :, :], y[:, :, :], gate_z[1][:, :, :], ALU.mult).then_inc(yg_ready, 1)

            def count_taken():
                nc.vector.tensor_scalar(taken[:, 0:E], end_tile[:, :], float(EARLY), None,
                                        ALU.min).then_inc(early_ends, 1)
                dve.wait_ge(early_ends, 1)
                nc.vector.tensor_copy(end_tile[:, :], taken[:, 0:E]).then_inc(early_ends, 1)
                dve.wait_ge(early_ends, 2)
                nc.vector.tensor_tensor(taken[:, 1:E], end_tile[:, 1:E], end_tile[:, 0:E - 1],
                                        ALU.subtract).then_inc(early_ends, 1)
                dve.wait_ge(early_ends, 3)

            def body(b, p, first=False, last=False):
                n = None if last else b + 1
                t = None if first else b - 1
                q = 1 - p
                for s in range(S):
                    if s == 0 and t is not None:
                        times_c(b - 1, S - 1)
                    scan(b, s, 0)
                    scan(b, s, 1)
                    if s >= 1 and s - 1 in VEC_STATES:
                        times_c(b, s - 1)
                    if first and s < 2:
                        skip_term(0, 0, s)
                    if n is not None and s == 1:
                        normalise(n, q)
                    if n is not None and s in (4, 5):
                        convolve(n, 3 * s - 12)
                        convolve(n, 3 * s - 11)
                    if t is not None and s == (6 if last else 7):
                        residual(t)
                    if t is not None and s == (7 if last else 8):
                        residual_moments(t)
                    if n is not None and s == 11:
                        softplus_poly(n, q, 0)
                    if t is not None and not last and s == 12:
                        choose(t)
                    if n is not None and s == 13:
                        skip_term(n, q, 0)
                    if t is not None and not last and s == 15:
                        place(t)
                    if last and s == 10:
                        choose(t)
                    if last and s == 11:
                        place(t)
                        plan_counts(0)
                    if last and s == 12:
                        plan_passed(0)
                    if last and s == 13:
                        plan_rows(0)
                    if last and s == 14:
                        count_taken()
                    if n is not None and s == 15:
                        skip_term(n, q, 1)
                    if n is not None and s == 0:
                        statistics(n, q)
                    if t is not None and s == 2:
                        finish_y(t, q)
                    if n is not None and s in (4, 5):
                        convolve(n, 3 * s - 10)
                    if n is not None and s == 6:
                        silu_conv(n)
                    if n is not None and s == 7:
                        silu_z(n, q)
                    if t is not None and s == (8 if last else 9):
                        normalise2(t)
                    if n is not None and s == 9:
                        copy_bcT(n)
                    if n is not None and s == 11:
                        softplus_poly(n, q, 1)
                    if n is not None and s == 12:
                        softplus_poly(n, q, 2)
                    if n is not None and s == 13:
                        softplus_poly(n, q, 3)
                    if n is not None and s == 14:
                        softplus_poly(n, q, 4)

            nc.vector.memset(xpad[:, :, 0:TAPS - 1], 0.0)
            nc.vector.memset(zero8[:, :], 0.0)
            nc.vector.memset(one_hot[:, TILES, :], 0.0)
            statistics(0, 0)
            dve.wait_ge(first_loaded, 16)
            normalise(0, 0)
            nc.vector.tensor_scalar(half_bin[:, :], b_in, 0.5, None, ALU.mult).then_inc(setup, 1)
            nc.vector.tensor_scalar(const("conv_w"), const("conv_w"), 0.5, None, ALU.mult).then_inc(setup, 1)
            nc.vector.tensor_scalar(conv_b, conv_b, 0.5, None, ALU.mult).then_inc(setup, 1)
            dve.wait_ge(setup, 3)
            for h in range(H):
                last = nc.vector.scalar_tensor_tensor(conv_in[:, h:h + 1], b_in[:, h:h + 1], conv_w[:, h, TAPS - 1:],
                                                      conv_b[:, h:h + 1], ALU.mult, ALU.add)
            last.then_inc(setup, 1)
            dve.wait_ge(rest_loaded, 16)
            nc.vector.tensor_copy(count_w[:, 0, :], before)
            nc.vector.tensor_copy(count_w[:, 1, :], ones)
            nc.vector.tensor_copy(filled[:, :], const("region_at"))
            nc.vector.tensor_copy(token[:, :], const("token")).then_inc(setup, 1)
            dve.wait_ge(setup_a, 1)
            nc.vector.tensor_scalar(tiny_a[:, :], neg_a[:, :], 1e-6, None, ALU.is_lt)
            nc.vector.tensor_scalar(tiny_s[:, :], inv_a_s[:, :], 1e-6, None, ALU.is_lt)
            nc.vector.tensor_scalar(neg_d[:, :], d_skip, -1.0, None, ALU.mult).then_inc(setup, 1)
            dve.wait_ge(setup, 6)
            nc.vector.scalar_tensor_tensor(inv_a[:, :], tiny_a[:, :], 1.0, neg_a[:, :], ALU.subtract, ALU.mult)
            nc.vector.scalar_tensor_tensor(inv_a_s[:, :], tiny_s[:, :], 1.0, inv_a_s[:, :],
                                           ALU.subtract, ALU.mult).then_inc(setup, 1)
            dve.wait_ge(setup, 7)
            nc.vector.tensor_tensor(inv_a[:, :], inv_a[:, :], tiny_a[:, :], ALU.add)
            nc.vector.tensor_scalar(neg_a[:, :], neg_a[:, :], -1.0, None, ALU.mult)
            nc.vector.tensor_tensor(inv_a_s[:, :], inv_a_s[:, :], tiny_s[:, :], ALU.add).then_inc(setup, 1)
            dve.wait_ge(setup, 8)
            nc.vector.reciprocal(inv_a[:, :], inv_a[:, :])
            nc.vector.reciprocal(inv_a_s[:, :], inv_a_s[:, :]).then_inc(setup, 1)
            dve.wait_ge(setup, 9)

            def diagonals(i):
                for h in range(H):
                    for g in range(GROUPS):
                        at = h * S + 4 * g + 2 + i
                        last = nc.vector.tensor_scalar(diag[:, h, g, i, :], ident, inv_a[:, at:at + 1], None, ALU.mult)
                last.then_inc(setup, 1)

            diagonals(0)
            for m in range(6):
                convolve(0, m)
            silu_z(0, 0)
            silu_conv(0)
            diagonals(1)
            copy_bcT(0)
            for i in range(5):
                softplus_poly(0, 0, i)
            body(0, 0, first=True)
            with dve.Fori(0, (NB - 2) // 2) as i:
                body(2 * i + 1, 1)
                body(2 * i + 2, 0)
            body(NB - 1, 1, last=True)

            def take_weights(k, c):
                i = FU * k + c
                e = dve.value_load(t_exp_i[0:1, bass.ds(i, 1)], min_val=0, max_val=E - 1)
                if not starts(k, c, 2):
                    dve.wait_ge(hidden_done, i - 1)
                nc.vector.tensor_copy(f_w1[c % 2][:, :], w_all[:, bass.ds(e, 1), 0:FF].squeeze(1)).then_inc(w1_taken, 1)
                if not starts(k, c, 4):
                    dve.wait_ge(mlp_done, i - 3)
                nc.vector.tensor_copy(f_w2[c % 4][:, :], w_all[:, bass.ds(e, 1), FF:].squeeze(1)).then_inc(w2_taken, 1)

            def add_b2(k, c):
                i = FU * k + c
                dve.wait_ge(mlp_done, i + 1)
                nc.vector.tensor_tensor(biased[c % 2][:, :], ysum[:, c % 2, 0:DM], f_w2[c % 4][:, EW - FF - DM:],
                                        ALU.add).then_inc(b2_added, 1)

            def combine(k, c):
                dve.wait_ge(b2_added, FU * k + c + 1)
                nc.vector.scalar_tensor_tensor(f_out[c], biased[c % 2][:, :], f_row[c][:, 2 * DM:2 * DM + 1],
                                               f_row[c][:, DM:2 * DM], ALU.mult, ALU.add).then_inc(combined, 1)

            def tiles(k):
                for c in range(FU):
                    if starts(k, c, FU) and c == 4:
                        normalise2(NB - 1)
                    if starts(k, c, FU) and c == 6:
                        choose(NB - 1)
                    if not starts(k, c, 1):
                        add_b2(*ahead(k, c))
                    if not ends(k, c, 2):
                        take_weights(*after(k, c, 2))
                    if not starts(k, c, 1):
                        combine(*ahead(k, c))
                    if starts(k, c, FU) and c == 1:
                        residual(NB - 1)
                        residual_moments(NB - 1)
                    if starts(k, c, FU) and c == 6:
                        place(NB - 1)
                        expert_ends()
                    if isinstance(k, int) and k == 1 and c < 3:
                        (plan_counts, plan_passed, plan_rows)[c](1)

            times_c(NB - 1, S - 1)
            dve.wait_ge(w_loaded, 16 * E)
            take_weights(0, 0)
            take_weights(0, 1)
            finish_y(NB - 1, 1)
            gate_last()
            for k in range(EARLY // FU):
                tiles(k)
            with dve.Fori(EARLY // FU, FTILES // FU - 1) as k:
                tiles(k)
            tiles(FTILES // FU - 1)
            add_b2(FTILES // FU - 1, FU - 1)
            combine(FTILES // FU - 1, FU - 1)

        @block.gpsimd
        def _(pool):
            def rstd(n):
                pool.wait_ge(mv1_ready, n + 1)
                nc.gpsimd.tensor_tensor(var1[:, :], mv1[:, :, 1], const("eps"), ALU.add).then_inc(var1_ready, 1)
                pool.wait_ge(var1_ready, n + 1)
                if not early(n):
                    pool.wait_ge(xn_ready, n)
                nc.gpsimd.tensor_tensor(rstd1[:, :], var1[:, :], const("minus_half"), ALU.pow).then_inc(rstd1_ready, 1)

            def rstd_2(t):
                pool.wait_ge(mv2_ready, t + 1)
                nc.gpsimd.tensor_tensor(var2[:, :], mv2[:, :, 1], const("eps"), ALU.add).then_inc(var2_ready, 1)
                pool.wait_ge(var2_ready, t + 1)
                nc.gpsimd.tensor_tensor(rstd2[:, :], var2[:, :], const("minus_half"), ALU.pow).then_inc(rstd2_ready, 1)

            def build_delta(n, g):
                pool.wait_ge(bcT_ready, n + 1)
                if not early(n):
                    pool.wait_ge(dv_ready, 32 * (n - 1) + 8 * g + 8)
                b_col = bc_T[:, :, 4 * g:4 * g + 4].rearrange("p j s -> p s j")
                nc.gpsimd.tensor_tensor(delta[:, 4 * g:4 * g + 4, :, :],
                                        bidiag.unsqueeze(1).unsqueeze(1).to_broadcast([P, 4, TILES, BW]),
                                        b_col.unsqueeze(3).to_broadcast([P, 4, TILES, BW]),
                                        ALU.mult).then_inc(delta_ready, 1)

            def times_c(n, s):
                pool.wait_ge(scanned, 32 * n + 2 * s + 2)
                pool.wait_ge(c_loaded[s // 4], 16 * (n + 1))
                if not (early(n) and s < 4):
                    pool.wait_ge(summed, SUMS * n + 2 * TERMS * (s // 4) - 4)
                nc.gpsimd.tensor_tensor(prod[2][:, :, :], k_st[2][:, :, :],
                                        c_all[:, s:s + 1, :].to_broadcast([P, H, L]), ALU.mult).then_inc(prod_pool, 1)

            def add_pair(n, g):
                pool.wait_ge(prod_vec, NV * n + vec_before(4 * g + 2))
                if not (early(n) and g == 0):
                    pool.wait_ge(summed, SUMS * n + 2 * TERMS * g - 2)
                nc.gpsimd.tensor_tensor(prod[1][:, :, :], prod[0][:, :, :], prod[1][:, :, :],
                                        ALU.add).then_inc(pair_added, 1)

            def times_gate(t, p):
                pool.wait_ge(y_ready, t + 1)
                pool.wait_ge(gate_ready, t + 1)
                nc.gpsimd.tensor_tensor(y[:, :, :], y[:, :, :], gate_z[p][:, :, :], ALU.mult).then_inc(yg_ready, 1)

            def residual_bias(t):
                pool.wait_ge(res_loaded, 16 * (t + 1))
                nc.gpsimd.tensor_tensor(x_res[:, :, :], x_res[:, :, :],
                                        const("out_b").unsqueeze(1).to_broadcast([P, TILES, DM]),
                                        ALU.add).then_inc(res_ready, 1)

            def scatter(t):
                pool.wait_ge(placed, 9 * t + 8)
                pool.wait_ge(xn2_ready, t + 1)
                pool.sem_inc(wait_carrier)
                for j in range(TILES):
                    nc.gpsimd.indirect_dma_start(rows_d, bass.IndirectOffsetOnAxis(ap=slot_i[:, j:j + 1], axis=0),
                                                 row[:, j, :], None, bounds_check=ROWS - 1,
                                                 oob_is_err=False).then_inc(scattered, 16)

            def body(b, p, first=False, last=False):
                n = None if last else b + 1
                t = None if first else b - 1
                for s in range(S):
                    if s % 4 == 3:
                        times_c(b, s - 1)
                    if s % 4 == 3 and not (last and s == S - 1):
                        add_pair(b, s // 4)
                    if n is not None and s == 1:
                        rstd(n)
                    if t is not None and s == 3:
                        times_gate(t, 1 - p)
                        residual_bias(t)
                    if t is not None and s == 4:
                        build_delta(b, 3)
                    if t is not None and s == (7 if last else 9):
                        rstd_2(t)
                    if n is not None and s in (10, 12, 13):
                        build_delta(n, (10, 12, 13).index(s))
                    if t is not None and s == (11 if last else 15):
                        scatter(t)

            nc.gpsimd.memset(pad[:, :], 0.0).then_inc(pad_zero, 1)
            pool.wait_ge(pad_zero, 1)
            nc.gpsimd.memset(pad[:, :].bitcast(I32)[:, 2 * DM + 1:], NO_TOKEN).then_inc(s_pad_ready, 1)
            pool.wait_ge(s_pad_ready, 1)
            pool.dma_start(rows_d[E * REGION:ROWS, :].rearrange("(c q) w -> q c w", q=P),
                           pad[:, :].unsqueeze(1).to_broadcast([P, (ROWS - E * REGION) // P, RW])
                           ).then_inc(scattered, 16)
            pool.wait_ge(first_loaded, 16)
            rstd(0)
            pool.wait_ge(rest_loaded, 16)
            for g in range(4):
                build_delta(0, g)
            body(0, 0, first=True)
            with pool.Fori(0, (NB - 2) // 2) as i:
                body(2 * i + 1, 1)
                body(2 * i + 2, 0)
            body(NB - 1, 1, last=True)
            residual_bias(NB - 1)

            def store_rows(k, c):
                pool.wait_ge(combined, FU * k + c + 1)
                pool.sem_inc(wait_carrier)
                nc.gpsimd.indirect_dma_start(
                    out_d, bass.IndirectOffsetOnAxis(ap=f_row[c][:, :].bitcast(I32)[:, 2 * DM + 1:], axis=0),
                    f_out[c], None, bounds_check=TOK - 1, oob_is_err=False).then_inc(f_stored[c], 16)

            def tiles(k):
                for c in range(FU):
                    if starts(k, c, FU) and c == 1:
                        rstd_2(NB - 1)
                    if starts(k, c, FU) and c == 6:
                        scatter(NB - 1)
                    store_rows(k, c)

            for k in range(EARLY // FU):
                tiles(k)
            with pool.Fori(EARLY // FU, FTILES // FU) as k:
                tiles(k)
            for c in range(FU):
                pool.wait_ge(f_stored[c], 16 * (FTILES // FU))


def packed(a):
    f = np.float32
    pack = np.zeros((P, PACK_W), f)

    def put(name, v):
        v = np.asarray(v, f)
        pack[:v.shape[0], AT[name][0]:AT[name][1]] = v

    def rows(v):
        return np.broadcast_to(np.asarray(v, f), (P, len(v)))

    def halves(v):
        return np.swapaxes(v.reshape((-1, P) + v.shape[1:]), 0, 1).reshape(P, -1)

    put("ident", np.eye(P))
    put("bidiag", np.eye(P, BW) - np.eye(P, BW, 1))
    put("before", np.triu(np.ones((P, P)), 1))
    put("ones", np.ones((P, P)))
    put("expert_no", rows(range(E)))
    put("expert_no8", rows(range(E, 2 * E)))
    put("region_at", rows([e * REGION for e in range(E)]))
    put("token", np.arange(TILES)[None, :] * P + np.arange(P)[:, None])
    put("quad_a", rows(QUAD_A))
    put("minus_half", np.full((P, TILES), -0.5))
    put("eps", np.full((P, TILES), EPS))
    put("tile_at", rows([P * j for j in range(TOK // P)]))
    put("tile_no", rows(range(FTILES)))
    put("w_in", a["L0_attn_in_proj_w"].T)
    put("b_in", halves(a["L0_attn_in_proj_b"]))
    put("conv_w", halves(a["L0_attn_conv_w"]))
    put("conv_b", halves(a["L0_attn_conv_b"]))
    put("a_log", halves(a["L0_attn_A_log"].T))
    put("d_skip", halves(a["L0_attn_D"]))
    put("x_proj", halves(a["L0_attn_x_proj_w"].T))
    put("dt_w", a["L0_attn_dt_proj_w"].T)
    put("dt_b", halves(a["L0_attn_dt_proj_b"]))
    put("a_log_s", a["L0_attn_A_log"])
    put("out_w", halves(a["L0_attn_out_proj_w"].T))
    put("out_b", rows(a["L0_attn_out_proj_b"]))
    put("w_r", a["L0_ffn_Wr"])
    put("b_r", rows(a["L0_ffn_br"]))
    return pack


def kernel(**inputs):
    import concourse.bacc as bacc
    from concourse.bass_utils import run_bass_kernel_spmd

    a = {k: np.asarray(v) for k, v in inputs.items()}
    experts = np.zeros((E, P, EW), np.float32)
    experts[:, :, 0:FF] = a["L0_ffn_W1"]
    experts[:, :, FF:FF + FK * DM] = a["L0_ffn_W2"].reshape(E, FK, P, DM).transpose(0, 2, 1, 3).reshape(E, P, FK * DM)
    experts[:, :, FF + FK * DM:FF + FK * DM + FK] = a["L0_ffn_b1"].reshape(E, FK, P).transpose(0, 2, 1)
    experts[:, :, EW - DM:] = a["L0_ffn_b2"][:, None, :]
    arrays = {"x_d": np.ascontiguousarray(a["L0_attn_x"]), "pack_d": packed(a), "experts_d": experts}

    nc = bacc.Bacc("TRN2", target_bir_lowering=False, num_devices=1)
    f32 = mybir.dt.float32
    args = [nc.dram_tensor(n, v.shape, f32, kind="ExternalInput").ap() for n, v in arrays.items()]
    out = nc.dram_tensor("out", (TOK, DM), f32, kind="ExternalOutput").ap()
    c_scratch = nc.dram_tensor("c_scratch", (2, S, L), f32, kind="Internal").ap()
    rows_d = nc.dram_tensor("rows_d", (ROWS, RW), f32, kind="Internal").ap()
    program(nc, *args, out, c_scratch, rows_d)
    r = run_bass_kernel_spmd(nc, [arrays], core_ids=[0])
    return r.results[0]["out"].reshape(NB, L, DM)
```
